# Optimizing a Trainium2 kernel written in Bass

```python
import numpy as np
import jax
import jax.numpy as jnp

def _softmax(x, axis=-1):
    return jax.nn.softmax(x, axis=axis)

def _gelu(x):
    return jax.nn.gelu(x, approximate=True)

def _silu(x):
    return jax.nn.silu(x)

def _sigmoid(x):
    return jax.nn.sigmoid(x)

def _layernorm(x, axis=-1, eps=1e-05):
    m = jnp.mean(x, axis=axis, keepdims=True)
    v = jnp.var(x, axis=axis, keepdims=True)
    return (x - m) / jnp.sqrt(v + eps)

def _scatter_add(tgt, idx, src, axis=0):
    return tgt.at[idx].add(src)

def _segment_sum(src, seg, n):
    return jax.ops.segment_sum(src, seg, n)
kernel_name = 'mk_flamingo_gated_d2_seqx_r4_20b055'

def setup_inputs(seed: int=0):
    np.random.seed(seed)
    _w = jnp.asarray

    def _rec_inputs():
        import jax
        import jax.numpy as jnp
        _rk = jax.random.key(seed)
        x = 7.22e-05 + 1 * jax.random.normal(jax.random.fold_in(_rk, 1), (8, 256, 512), jnp.float32)
        _lenS = 256 - jax.random.randint(jax.random.fold_in(_rk, 7), (8,), 0, max(1, 256 // 4) + 1, jnp.int32)
        _lenS2 = 256 - jax.random.randint(jax.random.fold_in(_rk, 8), (8,), 0, max(1, 256 // 4) + 1, jnp.int32)
        _ctx_2048P = jax.random.normal(jax.random.fold_in(_rk, 11), (8, 16, 512), jnp.float32)
        _ctx_2048c = jax.random.dirichlet(jax.random.fold_in(_rk, 511), 0.3 * jnp.ones((16,), jnp.float32), (8, 256))
        _ctx_2048t = jnp.einsum('bsk,bkd->bsd', _ctx_2048c, _ctx_2048P)
        _ctx_2048t = _ctx_2048t * jax.lax.rsqrt(jnp.mean(jnp.square(_ctx_2048t)) + 1e-12) * 0.953939
        ctx_2048 = 4.13588e-05 + 0.999923 * (_ctx_2048t + 0.3 * jax.random.normal(jax.random.fold_in(_rk, 611), (8, 256, 512), jnp.float32))
        _validS = jnp.arange(256)[None, :] < _lenS[:, None]
        _validS2 = jnp.arange(256)[None, :] < _lenS2[:, None]
        _causal = jnp.tril(jnp.ones((256, 256), dtype=bool))
        mask_SxS2_bc0 = jnp.logical_not(jnp.broadcast_to(_validS2[0:1, :], (256, 256)))
        mask_BxS2_bk0 = jnp.logical_not(jnp.broadcast_to(_validS2[:, :], (8, 256)))
        _g = jax.random.normal(jax.random.fold_in(_rk, 9001), (2, 2), jnp.float32)
        _g = jnp.sign(_g) * jnp.maximum(jnp.abs(_g), 1.0) + (_g == 0) * 1.0
        g_xattn = _g[0]
        g_ffn = _g[1]
        return (x, ctx_2048, mask_SxS2_bc0, mask_BxS2_bk0, g_xattn, g_ffn)
    x, ctx_2048, mask_SxS2_bc0, mask_BxS2_bk0, g_xattn, g_ffn = _rec_inputs()

    def _L0_xattn_setup():
        import jax, jax.numpy as jnp
        import numpy as np
        B, LQ, LKV = (4, 256, 256)
        HID, H, G = (512, 32, 8)
        HD = HID // H
        HPG = H // G
        key = jax.random.key(seed)
        ks = jax.random.split(key, 10)
        s = 0.02
        inp = {'X': jax.random.normal(ks[0], (B, LQ, HID), jnp.float32), 'encoder_output': jax.random.normal(ks[1], (B, LKV, HID), jnp.float32), 'causal_mask': jnp.triu(jnp.ones((LQ, LKV), bool), 1), 'padding_mask': jnp.zeros((B, LKV), bool).at[B // 2:, LKV - LKV // 4:].set(True), 'Wq': jax.random.normal(ks[2], (HID, HID), jnp.float32) * s, 'bq': jnp.zeros((HID,), jnp.float32), 'Wk': jax.random.normal(ks[3], (G * HD, HID), jnp.float32) * s, 'bk': jnp.zeros((G * HD,), jnp.float32), 'Wv': jax.random.normal(ks[4], (G * HD, HID), jnp.float32) * s, 'bv': jnp.zeros((G * HD,), jnp.float32), 'Wo': jax.random.normal(ks[5], (HID, HID), jnp.float32) * s, 'bo': jnp.zeros((HID,), jnp.float32)}
        return inp
    _L0_xattn_all = _L0_xattn_setup()
    _L0_xattn_in = {k: v for k, v in _L0_xattn_all.items() if k in ('Wq', 'bq', 'Wk', 'bk', 'Wv', 'bv', 'Wo', 'bo')}
    del _L0_xattn_all

    def _L0_ffn_setup():
        import jax, jax.numpy as jnp
        import numpy as np
        EPS = 1e-06
        Q_B = 128.0

        def layer_norm(x):
            mean = jnp.mean(x, axis=-1, keepdims=True)
            var = jnp.var(x, axis=-1, keepdims=True)
            return (x - mean) / jnp.sqrt(var + EPS)

        def absmax_quant(x):
            gamma = jnp.max(jnp.abs(x), axis=-1, keepdims=True)
            x_hat = jnp.clip(x * Q_B / gamma, -Q_B + EPS, Q_B - EPS)
            return x_hat * gamma / Q_B

        def ternarize_weights(w):
            gamma = jnp.mean(jnp.abs(w))
            return jnp.sign(jnp.round(w / (gamma + EPS))) * gamma

        def bitlinear(x, w):
            xn = layer_norm(x)
            x_hat = xn + jax.lax.stop_gradient(absmax_quant(xn) - xn)
            w_hat = w + jax.lax.stop_gradient(ternarize_weights(w) - w)
            return jnp.einsum('bsd,od->bso', x_hat, w_hat)
        key = jax.random.key(seed)
        k1, k2, k3 = jax.random.split(key, 3)
        B, S, D = (4, 512, 512)
        x = jax.random.normal(k1, (B, S, D), dtype=jnp.float32)
        w_fc = jax.random.normal(k2, (4 * D, D), dtype=jnp.float32) / np.sqrt(D)
        w_proj = jax.random.normal(k3, (D, 4 * D), dtype=jnp.float32) / np.sqrt(4 * D)
        return {'x': x, 'w_fc': w_fc, 'w_proj': w_proj}
    _L0_ffn_all = _L0_ffn_setup()
    _L0_ffn_in = {k: v for k, v in _L0_ffn_all.items() if k in ('w_fc', 'w_proj')}
    del _L0_ffn_all

    def _L1_xattn_setup():
        import jax, jax.numpy as jnp
        import numpy as np
        EPS = 1e-06
        NUM_HEADS = 16

        def _feature_map(x):
            return jnp.where(x > 0, x + 1.0, jnp.exp(x))
        key = jax.random.key(seed)
        ks = jax.random.split(key, 7)
        B, L, S, D = (4, 1024, 1024, 512)
        sc = 1.0 / np.sqrt(D)
        return {'query': jax.random.normal(ks[0], (B, L, D), jnp.float32), 'kv': jax.random.normal(ks[1], (B, S, D), jnp.float32), 'Wq': jax.random.normal(ks[2], (D, D), jnp.float32) * sc, 'Wg': jax.random.normal(ks[3], (D, D), jnp.float32) * sc, 'bg': jnp.ones((D,), jnp.float32), 'Wkv': jax.random.normal(ks[4], (2 * D, D), jnp.float32) * sc, 'Wo': jax.random.normal(ks[5], (D, D), jnp.float32) * sc}
    _L1_xattn_all = _L1_xattn_setup()
    _L1_xattn_in = {k: v for k, v in _L1_xattn_all.items() if k in ('Wq', 'Wg', 'bg', 'Wkv', 'Wo')}
    del _L1_xattn_all

    def _L1_ffn_setup():
        import jax, jax.numpy as jnp
        import numpy as np
        B, S, D = (2, 512, 512)
        E = 8
        TOPK = 2
        H_SHARED = 2048
        H_ROUTED = 256
        STD = 0.02
        key = jax.random.key(seed)
        ks = jax.random.split(key, 7)
        return {'x': jax.random.normal(ks[0], (B, S, D), jnp.float32), 'w12': jax.random.normal(ks[1], (E, 2 * H_ROUTED, D), jnp.float32) * STD, 'w3': jax.random.normal(ks[2], (E, D, H_ROUTED), jnp.float32) * STD, 'router_w': jax.random.normal(ks[3], (E, D), jnp.float32) * STD, 'expert_bias': jnp.zeros((E,), jnp.float32), 'sw1': jax.random.normal(ks[4], (H_SHARED, D), jnp.float32) * STD, 'sw2': jax.random.normal(ks[5], (H_SHARED, D), jnp.float32) * STD, 'sw3': jax.random.normal(ks[6], (D, H_SHARED), jnp.float32) * STD}
    _L1_ffn_all = _L1_ffn_setup()
    _L1_ffn_in = {k: v for k, v in _L1_ffn_all.items() if k in ('w12', 'w3', 'router_w', 'expert_bias', 'sw1', 'sw2', 'sw3')}
    del _L1_ffn_all
    return {'x': x, 'ctx_2048': ctx_2048, 'mask_SxS2_bc0': mask_SxS2_bc0, 'mask_BxS2_bk0': mask_BxS2_bk0, 'g_xattn': g_xattn, 'g_ffn': g_ffn, 'L0_xattn_Wq': _L0_xattn_in['Wq'], 'L0_xattn_bq': _L0_xattn_in['bq'], 'L0_xattn_Wk': _L0_xattn_in['Wk'], 'L0_xattn_bk': _L0_xattn_in['bk'], 'L0_xattn_Wv': _L0_xattn_in['Wv'], 'L0_xattn_bv': _L0_xattn_in['bv'], 'L0_xattn_Wo': _L0_xattn_in['Wo'], 'L0_xattn_bo': _L0_xattn_in['bo'], 'L0_ffn_w_fc': _L0_ffn_in['w_fc'], 'L0_ffn_w_proj': _L0_ffn_in['w_proj'], 'L1_xattn_Wq': _L1_xattn_in['Wq'], 'L1_xattn_Wg': _L1_xattn_in['Wg'], 'L1_xattn_bg': _L1_xattn_in['bg'], 'L1_xattn_Wkv': _L1_xattn_in['Wkv'], 'L1_xattn_Wo': _L1_xattn_in['Wo'], 'L1_ffn_w12': _L1_ffn_in['w12'], 'L1_ffn_w3': _L1_ffn_in['w3'], 'L1_ffn_router_w': _L1_ffn_in['router_w'], 'L1_ffn_expert_bias': _L1_ffn_in['expert_bias'], 'L1_ffn_sw1': _L1_ffn_in['sw1'], 'L1_ffn_sw2': _L1_ffn_in['sw2'], 'L1_ffn_sw3': _L1_ffn_in['sw3']}

def reference(x, ctx_2048, mask_SxS2_bc0, mask_BxS2_bk0, g_xattn, g_ffn, L0_xattn_Wq, L0_xattn_bq, L0_xattn_Wk, L0_xattn_bk, L0_xattn_Wv, L0_xattn_bv, L0_xattn_Wo, L0_xattn_bo, L0_ffn_w_fc, L0_ffn_w_proj, L1_xattn_Wq, L1_xattn_Wg, L1_xattn_bg, L1_xattn_Wkv, L1_xattn_Wo, L1_ffn_w12, L1_ffn_w3, L1_ffn_router_w, L1_ffn_expert_bias, L1_ffn_sw1, L1_ffn_sw2, L1_ffn_sw3):
    import jax
    import jax.numpy as jnp

    def _L0_xattn_ref(X, encoder_output, causal_mask, padding_mask, Wq, bq, Wk, bk, Wv, bv, Wo, bo):
        import jax, jax.numpy as jnp
        import numpy as np
        B, LQ, LKV = (4, 256, 256)
        HID, H, G = (512, 32, 8)
        HD = HID // H
        HPG = H // G
        b = X.shape[0]
        q = X @ Wq.T + bq
        k = encoder_output @ Wk.T + bk
        v = encoder_output @ Wv.T + bv
        q = q.reshape(b, LQ, G, HPG, HD).transpose(0, 2, 3, 1, 4)
        k = k.reshape(b, LKV, G, HD).transpose(0, 2, 1, 3)
        v = v.reshape(b, LKV, G, HD).transpose(0, 2, 1, 3)
        scores = jnp.einsum('bgrqd,bgkd->bgrqk', q, k) / jnp.sqrt(jnp.float32(HD))
        scores = jnp.where(causal_mask[None, None, None, :, :], -jnp.inf, scores)
        scores = jnp.where(padding_mask[:, None, None, None, :], -jnp.inf, scores)
        w = jax.nn.softmax(scores, axis=-1)
        out = jnp.einsum('bgrqk,bgkd->bgrqd', w, v)
        out = out.reshape(b, H, LQ, HD).transpose(0, 2, 1, 3).reshape(b, LQ, HID)
        return out @ Wo.T + bo

    def _L0_ffn_ref(x, w_fc, w_proj):
        import jax, jax.numpy as jnp
        import numpy as np
        EPS = 1e-06
        Q_B = 128.0

        def layer_norm(x):
            mean = jnp.mean(x, axis=-1, keepdims=True)
            var = jnp.var(x, axis=-1, keepdims=True)
            return (x - mean) / jnp.sqrt(var + EPS)

        def absmax_quant(x):
            gamma = jnp.max(jnp.abs(x), axis=-1, keepdims=True)
            x_hat = jnp.clip(x * Q_B / gamma, -Q_B + EPS, Q_B - EPS)
            return x_hat * gamma / Q_B

        def ternarize_weights(w):
            gamma = jnp.mean(jnp.abs(w))
            return jnp.sign(jnp.round(w / (gamma + EPS))) * gamma

        def bitlinear(x, w):
            xn = layer_norm(x)
            x_hat = xn + jax.lax.stop_gradient(absmax_quant(xn) - xn)
            w_hat = w + jax.lax.stop_gradient(ternarize_weights(w) - w)
            return jnp.einsum('bsd,od->bso', x_hat, w_hat)
        h = bitlinear(x, w_fc)
        h = jax.nn.gelu(h, approximate=False)
        return bitlinear(h, w_proj)

    def _L1_xattn_ref(query, kv, Wq, Wg, bg, Wkv, Wo):
        import jax, jax.numpy as jnp
        import numpy as np
        EPS = 1e-06
        NUM_HEADS = 16

        def _feature_map(x):
            return jnp.where(x > 0, x + 1.0, jnp.exp(x))
        B, L, D = query.shape
        S = kv.shape[1]
        H = NUM_HEADS
        hd = D // H
        q = query @ Wq.T
        gate = jax.nn.sigmoid(query @ Wg.T + bg)
        kvp = kv @ Wkv.T
        k, v = jnp.split(kvp, 2, axis=-1)
        q = _feature_map(q.reshape(B, L, H, hd).transpose(0, 2, 1, 3))
        k = _feature_map(k.reshape(B, S, H, hd).transpose(0, 2, 1, 3))
        v = v.reshape(B, S, H, hd).transpose(0, 2, 1, 3)
        kv_summary = jnp.einsum('bhsd,bhse->bhde', k, v)
        k_sum = k.sum(axis=-2)
        z = 1.0 / (jnp.einsum('bhld,bhd->bhl', q, k_sum)[..., None] + EPS)
        attn = jnp.einsum('bhld,bhde->bhle', q, kv_summary) * z
        attn = attn.transpose(0, 2, 1, 3).reshape(B, L, D)
        out = attn * gate @ Wo.T
        return out

    def _L1_ffn_ref(x, w12, w3, router_w, expert_bias, sw1, sw2, sw3):
        import jax, jax.numpy as jnp
        import numpy as np
        B, S, D = (2, 512, 512)
        E = 8
        TOPK = 2
        H_SHARED = 2048
        H_ROUTED = 256
        STD = 0.02
        b, s, d = x.shape
        g = x @ sw1.T
        u = x @ sw2.T
        shared_out = jax.nn.silu(g) * u @ sw3.T
        scores = jax.nn.sigmoid(x @ router_w.T)
        selection_scores = scores + expert_bias
        _, top_idx = jax.lax.top_k(selection_scores, TOPK)
        top_scores = jnp.take_along_axis(scores, top_idx, axis=-1)
        top_scores = top_scores / (top_scores.sum(-1, keepdims=True) + 1e-09)
        flat_x = x.reshape(-1, d)
        T = flat_x.shape[0]
        flat_idx = top_idx.reshape(T, TOPK)
        flat_sc = top_scores.reshape(T, TOPK)
        combine = jnp.zeros((T, E), x.dtype).at[jnp.arange(T)[:, None], flat_idx].add(flat_sc)
        h12 = jnp.einsum('td,ehd->teh', flat_x, w12)
        h1, h2 = jnp.split(h12, 2, axis=-1)
        h = jax.nn.silu(h1) * h2
        out_e = jnp.einsum('teh,edh->ted', h, w3)
        routed_out = jnp.einsum('ted,te->td', out_e, combine).reshape(b, s, d)
        return shared_out + routed_out
    x = x + jnp.tanh(g_xattn[0]) * _L0_xattn_ref(_layernorm(x, axis=-1), ctx_2048, mask_SxS2_bc0, mask_BxS2_bk0, L0_xattn_Wq, L0_xattn_bq, L0_xattn_Wk, L0_xattn_bk, L0_xattn_Wv, L0_xattn_bv, L0_xattn_Wo, L0_xattn_bo)
    x = x + jnp.tanh(g_ffn[0]) * _L0_ffn_ref(_layernorm(x, axis=-1), L0_ffn_w_fc, L0_ffn_w_proj)
    x = x + jnp.tanh(g_xattn[1]) * _L1_xattn_ref(_layernorm(x, axis=-1), ctx_2048, L1_xattn_Wq, L1_xattn_Wg, L1_xattn_bg, L1_xattn_Wkv, L1_xattn_Wo)
    x = x + jnp.tanh(g_ffn[1]) * _L1_ffn_ref(_layernorm(x, axis=-1), L1_ffn_w12, L1_ffn_w3, L1_ffn_router_w, L1_ffn_expert_bias, L1_ffn_sw1, L1_ffn_sw2, L1_ffn_sw3)
    return x

_drawn_inputs = setup_inputs


def setup_inputs(seed=0):
    import zlib

    import numpy as np

    out = dict(_drawn_inputs(seed))
    spreads = {'g_ffn': (-1.0, 0.6),
     'L0_xattn_bq': (0.0, 0.8),
     'L0_xattn_bk': (0.0, 0.8),
     'L0_xattn_bv': (0.0, 0.1),
     'L0_xattn_bo': (0.0, 0.1),
     'L1_xattn_bg': (1.0, 0.6),
     'L1_ffn_expert_bias': (0.0, 0.45)}
    factors = {'L0_xattn_Wq': 8.0,
     'L0_xattn_Wk': 8.0,
     'L1_xattn_Wq': 6.817,
     'L1_ffn_w12': 2.829,
     'L1_ffn_router_w': 3.659}
    for name, (base, spread) in spreads.items():
        noise = np.random.default_rng([zlib.crc32(name.encode()), seed]).standard_normal(out[name].shape)
        drawn = base * np.exp(spread * noise) if base else spread * noise
        out[name] = jnp.asarray(drawn.astype(out[name].dtype))
    for name, factor in factors.items():
        out[name] = (out[name] * factor).astype(out[name].dtype)
    return out
```

```python
from contextlib import ExitStack

import concourse.bass as bass
from concourse import mybir

F32 = mybir.dt.float32
F16 = mybir.dt.float16
U8 = mybir.dt.uint8
ALU = mybir.AluOpType
ACT = mybir.ActivationFunctionType
AX_X = mybir.AxisListType.X

P = 128
B, S, D = 8, 256, 512
TILES = B * S // P
KC = D // P
MASKED = -60000.0

H0, G0, HD0 = 32, 8, 16
STK = 64
H1, HD1 = 16, 32
F0 = 2048
FS, E, FR = 2048, 8, 256
CH = 512
BLK = 512


class Chain:

    def __init__(self, eng, sem, base=0):
        self.eng, self.sem, self.base, self.n = eng, sem, base, 0

    def __call__(self, ins):
        self.n += 1
        ins.then_inc(self.sem, 1)
        self.eng.wait_ge(self.sem, self.base + self.n)


def flamingo(nc, a, out, phases="ABCD"):
    with ExitStack() as ctx:
        used = {}

        def sb(name, shape, dt=F32, stack=None):
            used[name] = used.get(name, 0) + 1
            name = name if used[name] == 1 else f"{name}_{used[name]}"
            return (stack or ctx).enter_context(nc.sbuf_tensor(name, shape, dt))

        phase_sems = []

        def sem(name):
            if not phase_sems:
                return ctx.enter_context(nc.semaphore(name))
            stack, held = phase_sems[-1]
            s = stack.enter_context(nc.semaphore(name))
            held.append(s)
            return s

        def phase(write):
            phase_sems.append((ExitStack(), []))
            write(nc, a, env)
            stack, held = phase_sems.pop()
            with nc.Block() as block:
                @block.gpsimd
                def _(pool):
                    for s in held:
                        pool.sem_clear(s)
            stack.close()

        bank = [ctx.enter_context(nc.psum_tensor(f"bank{i}", [P, 512], F32)) for i in range(8)]

        def bank16(i):
            return bank[i][:, :].bitcast(F16)

        X = sb("X", [P, TILES, D])
        XTh = sb("XTh", [P, KC, TILES * P], F16)
        XTl = sb("XTl", [P, KC, TILES * P], F16)
        ident = sb("ident", [P, P])
        ident16 = sb("ident16", [P, P], F16)
        gates = sb("gates", [P, 4])
        tg = sb("tg", [P, 4])

        x_tiles = a["x"].rearrange("b (t p) d -> p (b t) d", p=P)
        out_tiles = out.rearrange("b (t p) d -> p (b t) d", p=P)
        ctx_tiles = a["ctx_2048"].rearrange("b (t p) d -> p (b t) d", p=P)

        def row(ap):
            return ap.rearrange("(a n) -> a n", a=1).partition_broadcast(P) if len(ap.shape) == 1 else ap

        s_load = [sem(f"s_load{i}") for i in range(4)]
        s_g = sem("s_gates")
        s_id = sem("s_ident")
        with nc.Block() as block:
            @block.sync
            def _(sp):
                for i in range(4):
                    sp.dma_start(X[:, 4 * i:4 * i + 4, :], x_tiles[:, 4 * i:4 * i + 4, :]).then_inc(s_load[i], 16)
                sp.dma_start(gates[:, 0:2], row(a["g_xattn"])).then_inc(s_g, 16)
                sp.dma_start(gates[:, 2:4], row(a["g_ffn"])).then_inc(s_g, 16)
                for i in range(4):
                    sp.wait_ge(s_load[i], 16)

            @block.gpsimd
            def _(pool):
                nc.gpsimd.memset(ident[:, :], 0.0).then_inc(s_id, 1)
                nc.gpsimd.memset(ident16[:, :], 0.0).then_inc(s_id, 1)
                pool.wait_ge(s_id, 2)
                for m in (ident, ident16):
                    nc.gpsimd.affine_select(out=m[:, :], in_=m[:, :], compare_op=ALU.not_equal, fill=1.0,
                                            base=0, pattern=[[-1, P]], channel_multiplier=1).then_inc(s_id, 1)

            @block.scalar
            def _(act):
                act.wait_ge(s_g, 32)
                nc.scalar.activation(tg[:, :], gates[:, :], ACT.Tanh)

        f_chain, f_pchain = sem("f_chain"), sem("f_pchain")
        f_var, f_rstd, f_xn, f_tr, f_hi, f_lo = (sem("f_" + n) for n in ("var", "rstd", "xn", "tr", "hi", "lo"))
        f_in = [sem("f_in0"), sem("f_in1")]
        f_base = {"n": 0, "chain": 0, "rstd": 0, "in": 0, "xn": 0}

        def front(kind, dsth, dstl):
            st = ExitStack()
            xn = sb("f_x", [P, 2, D], stack=st)
            stage = sb("f_stage", [P, 2, D], stack=st) if kind == "ctx" else None
            stats = sb("f_stats", [P, 2, 6], stack=st)
            mv = sb("f_mv", [P, 2, 2], stack=st)
            ve = sb("f_ve", [P, 2, 2], stack=st)
            rstd = sb("f_r", [P, 2, 2], stack=st)
            hold = sb("f_hold", [P, 1], stack=st)
            mhalf = sb("f_mh", [P, 1], stack=st)
            q = sb("f_q", [P, 2, 4], stack=st)
            x0 = f_base["xn"]
            n0, c0, r0, i0 = f_base["n"], f_base["chain"], f_base["rstd"], f_base["in"]
            norms = {"ln": 1, "bit": 2, "ctx": 0}[kind]
            per = {"ln": 4, "bit": 22, "ctx": 0}[kind]
            with nc.Block() as block:
                if kind == "ctx":
                    @block.sync
                    def _(sp):
                        for i in range(TILES):
                            sp.wait_ge(f_tr, n0 + i + 1)
                            sp.dma_start(stage[:, i % 2, :], ctx_tiles[:, i, :]).then_inc(f_in[i % 2], 16)

                @block.gpsimd
                def _(pool):
                    if norms:
                        nc.gpsimd.memset(mhalf[:, :], -0.5).then_inc(f_pchain, 1)
                        pool.wait_ge(f_pchain, f_base.setdefault("pool", 0) + 1)
                        f_base["pool"] += 1
                        with pool.Fori(0, TILES // 2) as i:
                            for v in range(norms):
                                for p in range(2):
                                    pool.wait_ge(f_var, r0 + 2 * norms * i + 2 * v + p + 1)
                                    nc.gpsimd.tensor_tensor(rstd[:, p, v:v + 1], ve[:, p, v:v + 1], mhalf[:, :],
                                                            ALU.pow).then_inc(f_rstd, 1)

                @block.tensor
                def _(pe):
                    if n0 == 0:
                        pe.sem_inc(f_tr, 2)
                    src = stage if kind == "ctx" else xn
                    with pe.Fori(0, TILES // 2) as i:
                        for p in range(2):
                            n = n0 + 2 * i + p
                            if kind == "ctx":
                                pe.wait_ge(f_in[p], i0 + 16 * i + 16)
                            else:
                                pe.wait_ge(f_xn, x0 + 2 * i + p + 1)
                            pe.wait_ge(f_lo, n + 1)
                            for k in range(KC):
                                last = nc.tensor.transpose(bank[p][:, k * P:(k + 1) * P],
                                                           src[:, p, k * P:(k + 1) * P], ident[:, :])
                            last.then_inc(f_tr, 1)

                @block.scalar
                def _(act):
                    with act.Fori(0, TILES // 2) as i:
                        for p in range(2):
                            n = n0 + 2 * i + p
                            act.wait_ge(f_tr, n + 3)
                            nc.scalar.activation(dsth[:, :, bass.ts(2 * i + p, P)],
                                                 bank[p][:, :].rearrange("p (k c) -> p k c", k=KC),
                                                 ACT.Copy).then_inc(f_hi, 1)

                @block.vector
                def _(dve):
                    if n0 == 0:
                        dve.sem_inc(f_lo, 2)
                    with dve.Fori(0, TILES // 2) as i:
                        link = Chain(dve, f_chain, c0 + per * i)
                        if norms:
                            for v in range(norms):
                                eps = (1e-5, 1e-6)[v]
                                for p in range(2):
                                    src = X[:, 2 * i + p, :] if v == 0 else xn[:, p, :]
                                    link(nc.vector.bn_stats(stats[:, p, :], src))
                                    nc.vector.memset(hold[:, :], 0.0)
                                    link(nc.vector.bn_aggr(mv[:, p, :], stats[:, p, :]))
                                    nc.vector.tensor_scalar(ve[:, p, v:v + 1], mv[:, p, 1:2], eps, None,
                                                            ALU.add).then_inc(f_var, 1)
                                for p in range(2):
                                    src = X[:, 2 * i + p, :] if v == 0 else xn[:, p, :]
                                    dve.wait_ge(f_rstd, r0 + 2 * norms * i + 2 * v + p + 1)
                                    if v == 0:
                                        dve.wait_ge(f_tr, n0 + 2 * i + p + 1)
                                    ins = nc.vector.tensor_scalar(xn[:, p, :], src, mv[:, p, 0:1],
                                                                  rstd[:, p, v:v + 1], ALU.subtract, ALU.mult)
                                    if kind == "ln":
                                        ins.then_inc(f_xn, 1)
                                    else:
                                        link(ins)
                            if kind == "bit":
                                for p in range(2):
                                    quantise(link, xn[:, p, :], q[:, p, :]).then_inc(f_xn, 1)
                        for p in range(2):
                            n = n0 + 2 * i + p
                            dve.wait_ge(f_hi, n + 1)
                            cols = bass.ts(2 * i + p, P)
                            nc.vector.tensor_tensor(dstl[:, :, cols],
                                                    bank[p][:, :].rearrange("p (k c) -> p k c", k=KC),
                                                    dsth[:, :, cols], ALU.subtract).then_inc(f_lo, 1)
                        assert link.n == per, link.n
            f_base["n"] += TILES
            f_base["xn"] += TILES if norms else 0
            f_base["chain"] += per * (TILES // 2)
            f_base["rstd"] += norms * TILES
            if kind == "ctx":
                f_base["in"] += 16 * (TILES // 2)
            st.close()

        def quantise(link, x, q):
            link(nc.vector.tensor_reduce(q[:, 0:1], x, AX_X, ALU.max, apply_absolute_value=True))
            link(nc.vector.reciprocal(q[:, 1:2], q[:, 0:1]))
            link(nc.vector.tensor_scalar(q[:, 2:3], q[:, 1:2], 128.0, None, ALU.mult))
            link(nc.vector.tensor_scalar(q[:, 3:4], q[:, 0:1], 1.0 / 128.0, None, ALU.mult))
            link(nc.vector.tensor_scalar(x, x, q[:, 2:3], 128.0 - 1e-6, ALU.mult, ALU.min))
            return nc.vector.tensor_scalar(x, x, 1e-6 - 128.0, q[:, 3:4], ALU.max, ALU.mult)

        w_st = [sem("w_st0"), sem("w_st1")]
        w_tr, w_hi, w_lo = sem("w_tr"), sem("w_hi"), sem("w_lo")
        w_base = {"u": 0, "g": 0}

        def prepare(units):
            st = ExitStack()
            stage = sb("w_stage", [P, 2, 4, D], stack=st)
            u0, g0 = w_base["u"], w_base["g"]
            with nc.Block() as block:
                @block.sync
                def _(sp):
                    for u, (w, hi, lo) in enumerate(units):
                        if u >= 2:
                            sp.wait_ge(w_tr, g0 + KC * (u - 1))
                        rts = w.shape[0] // P
                        sp.dma_start(stage[:, u % 2, 0:rts, :], w.rearrange("(r p) c -> p r c", p=P))\
                          .then_inc(w_st[u % 2], 16)

                @block.tensor
                def _(pe):
                    for u, (w, hi, lo) in enumerate(units):
                        pe.wait_ge(w_st[u % 2], 16 * (u0 // 2 + u // 2 + 1))
                        for k in range(KC):
                            g = KC * u + k
                            if g >= 2:
                                pe.wait_ge(w_lo, g0 + g - 1)
                            for r in range(w.shape[0] // P):
                                last = nc.tensor.transpose(bank[2 + g % 2][:, r * P:(r + 1) * P],
                                                           stage[:, u % 2, r, k * P:(k + 1) * P], ident[:, :])
                            last.then_inc(w_tr, 1)

                @block.scalar
                def _(act):
                    for u, (w, hi, lo) in enumerate(units):
                        for k in range(KC):
                            g = KC * u + k
                            act.wait_ge(w_tr, g0 + g + 1)
                            nc.scalar.activation(hi[:, k, :], bank[2 + g % 2][:, 0:w.shape[0]],
                                                 ACT.Copy).then_inc(w_hi, 1)

                @block.vector
                def _(dve):
                    for u, (w, hi, lo) in enumerate(units):
                        for k in range(KC):
                            g = KC * u + k
                            dve.wait_ge(w_hi, g0 + g + 1)
                            nc.vector.tensor_tensor(lo[:, k, :], bank[2 + g % 2][:, 0:w.shape[0]], hi[:, k, :],
                                                    ALU.subtract).then_inc(w_lo, 1)
            n = len(units)
            w_base["u"] += n + n % 2
            w_base["g"] += KC * n
            st.close()

        def three(out_ap, lhi, llo, rhi, rlo, first, last_one):
            nc.tensor.matmul(out_ap, lhi, rhi, start=first, stop=False)
            nc.tensor.matmul(out_ap, lhi, rlo, start=False, stop=False)
            return nc.tensor.matmul(out_ap, llo, rhi, start=False, stop=last_one)

        cst = ExitStack()
        if "A" in phases or "C" in phases:
            CTh = sb("CTh", [P, KC, TILES * P], F16, stack=cst)
            CTl = sb("CTl", [P, KC, TILES * P], F16, stack=cst)
            front("ctx", CTh, CTl)
        env = dict(locals())
        if "A" in phases:
            phase(phase_a)
        if "B" in phases:
            phase(phase_b)
        if "C" in phases:
            phase(phase_c)
        cst.close()
        if "D" in phases:
            phase(phase_d)

        s_out = sem("s_out")
        with nc.Block() as block:
            @block.sync
            def _(sp):
                sp.dma_start(out_tiles, X[:, :, :]).then_inc(s_out, 16)
                sp.wait_ge(s_out, 16)


def phase_a(nc, a, env):
    sem, bank, bank16, X, XTh, XTl, ident, ident16, tg = (env[k] for k in (
        "sem", "bank", "bank16", "X", "XTh", "XTl", "ident", "ident16", "tg"))
    st = ExitStack()

    def sb(name, shape, dt=F32):
        return env["sb"](name, shape, dt, stack=st)

    CTh, CTl = env["CTh"], env["CTl"]
    env["front"]("ln", XTh, XTl)
    KV = G0 * HD0
    NEG, ONE = 3 * HD0, 3 * HD0 + 1
    wqh = sb("a_wqh", [P, KC, D], F16)
    wql = sb("a_wql", [P, KC, D], F16)
    woh = sb("a_woh", [P, KC, D], F16)
    wol = sb("a_wol", [P, KC, D], F16)
    wkvh = sb("a_wkvh", [P, KC, 2 * KV], F16)
    wkvl = sb("a_wkvl", [P, KC, 2 * KV], F16)
    env["prepare"]([(a["L0_xattn_Wq"], wqh, wql), (a["L0_xattn_Wo"], woh, wol),
                    (a["L0_xattn_Wk"], wkvh[:, :, 0:KV], wkvl[:, :, 0:KV]),
                    (a["L0_xattn_Wv"], wkvh[:, :, KV:2 * KV], wkvl[:, :, KV:2 * KV])])

    bq = sb("a_bq", [P, D])
    bkv = sb("a_bkv", [P, 2 * KV])
    bo = sb("a_bo", [P, D])
    m8 = sb("a_m8", [P, 2, S], U8)
    pad8 = sb("a_pad8", [B, S], U8)
    padf = sb("a_padf", [B, S])
    madd = sb("a_madd", [P, 2, S], F16)
    maddT = sb("a_maddT", [P, 2, S], F16)
    pad = sb("a_pad", [P, 2, B])
    q32 = sb("a_q32", [P, 2, D])
    qs = sb("a_qs", [P, 2, H0, STK], F16)
    qT = sb("a_qT", [P, H0 // 2, S], F16)
    k32 = sb("a_k32", [P, 2, KV])
    ks = sb("a_ks", [P, 2, G0, 2, STK], F16)
    kT = sb("a_kT", [P, G0, S], F16)
    vv = sb("a_v", [P, 2, G0, 2 * HD0])
    mx = sb("a_mx", [P, 2, H0])
    NP = 4
    prob = sb("a_prob", [P, NP, D])
    av = sb("a_av", [P, 4, D])
    rec = sb("a_rec", [P, 4, 4, 4])
    on = sb("a_on", [P, 2, D])
    oTh = sb("a_oTh", [P, 2, KC, P], F16)
    oTl = sb("a_oTl", [P, 2, KC, P], F16)
    tmp = sb("a_tmp", [P, 2, D])

    k_in, k_ch, k_pad, k_tr, k_m = (sem("k_" + n) for n in ("in", "chain", "pad", "tr", "mask"))
    with nc.Block() as block:
        @block.sync
        def _(sp):
            sp.dma_start(bq[:, :], env["row"](a["L0_xattn_bq"])).then_inc(k_in, 16)
            sp.dma_start(bkv[:, 0:KV], env["row"](a["L0_xattn_bk"])).then_inc(k_in, 16)
            sp.dma_start(bkv[:, KV:2 * KV], env["row"](a["L0_xattn_bv"])).then_inc(k_in, 16)
            sp.dma_start(bo[:, :], env["row"](a["L0_xattn_bo"])).then_inc(k_in, 16)
            sp.dma_start(m8[:, :, :], a["mask_SxS2_bc0"].rearrange("(t p) k -> p t k", p=P)).then_inc(k_in, 16)
            sp.dma_start(pad8[:, :], a["mask_BxS2_bk0"]).then_inc(k_in, 16)

        @block.vector
        def _(dve):
            link = Chain(dve, k_ch)
            nc.vector.memset(qs[:, :, :, :], 0.0)
            nc.vector.memset(ks[:, :, :, :, :], 0.0)
            link(nc.vector.memset(vv[:, :, :, :], 0.0))
            nc.vector.memset(qs[:, :, :, ONE:ONE + 1], 1.0)
            nc.vector.memset(ks[:, :, :, :, NEG:NEG + 1], 1.0)
            nc.vector.memset(vv[:, :, :, HD0:HD0 + 1], 1.0)
            dve.wait_ge(k_in, 96)
            link(nc.vector.tensor_scalar(bq[:, :], bq[:, :], HD0 ** -0.5, None, ALU.mult))
            nc.vector.tensor_scalar(padf[:, :], pad8[:, :], MASKED, None, ALU.mult).then_inc(k_pad, 1)
            nc.vector.tensor_scalar(madd[:, :, :], m8[:, :, :], MASKED, None, ALU.mult).then_inc(k_m, 1)
            dve.wait_ge(k_tr, 1)
            link(nc.vector.tensor_copy(pad[:, :, :], bank[0][:, 0:2 * B].rearrange("p (t b) -> p t b", t=2)))
            dve.wait_ge(k_tr, 2)
            link(nc.vector.tensor_copy(maddT[:, :, :], bank16(1)[:, 0:2 * S].rearrange("p (t q) -> p t q", t=2)))

        @block.tensor
        def _(pe):
            pe.wait_ge(k_pad, 1)
            for t in range(2):
                last = nc.tensor.transpose(bank[0][:, t * B:(t + 1) * B], padf[:, t * P:(t + 1) * P], ident[0:B, 0:B])
            last.then_inc(k_tr, 1)
            pe.wait_ge(k_m, 1)
            for k in range(2):
                for t in range(2):
                    last = nc.tensor.transpose(bank16(1)[:, k * S + t * P:k * S + (t + 1) * P],
                                               madd[:, t, k * P:(k + 1) * P], ident16[:, :])
            last.then_inc(k_tr, 1)

    names = ("Q0", "Q1", "KV0", "KV1", "dq0", "dq1", "dk0", "dk1", "hq0", "hq1", "lq0", "lq1", "hk0", "hk1",
             "lk0", "lk1", "tq", "cq", "tk0", "tk1", "ck0", "ck1", "S", "M", "nm0", "nm1", "ST", "E", "AV", "acc",
             "evA", "OT", "ON", "To0", "To1", "hO0", "hO1", "lO0", "lO1", "O0", "O1", "x0", "x1", "ch")
    ev = {n: sem("a_" + n) for n in names}
    NS = 2 * G0 * 2
    SB = 4
    LAG = 2

    with nc.Block() as block:
        @block.tensor
        def _(pe):
            with pe.Fori(0, B) as b:
                def wait(n, count=1, per=1, credit=0):
                    pe.wait_ge(ev[n], b * per + count + credit)

                def project(dst, xh, xl, w_h, w_l, tt, n):
                    x = bass.ds((2 * b + tt) * P, P)
                    for k in range(KC):
                        last = env["three"](dst, xh[:, k, x], xl[:, k, x], w_h[:, k, :], w_l[:, k, :],
                                            k == 0, k == KC - 1)
                    last.then_inc(ev[n], 1)

                wait("ON", 4, 4)
                for tt in range(2):
                    project(bank[tt][:, :], XTh, XTl, wqh, wql, tt, f"Q{tt}")
                    project(bank[2 + tt][:, 0:2 * KV], CTh, CTl, wkvh, wkvl, tt, f"KV{tt}")

                def turn_q(tt, first, b0):
                    for h in range(2):
                        for j in range(8):
                            c = qs[:, tt, 16 * h + 2 * j:16 * h + 2 * j + 2, :].rearrange("p h c -> p (h c)")
                            last = nc.tensor.transpose(bank16(b0 + h)[:, j * P:(j + 1) * P], c, ident16[:, :])
                        last.then_inc(ev["tq"], 1)

                wait("x0")
                wait("x1")
                for tt in range(2):
                    wait(f"lq{tt}")
                    turn_q(tt, True, 4 + 2 * tt)
                    wait(f"lk{tt}")
                    wait(f"dq{tt}")
                    for g in range(G0):
                        last = nc.tensor.transpose(bank16(tt)[:, g * P:(g + 1) * P],
                                                   ks[:, tt, g].rearrange("p d c -> p (d c)"), ident16[:, :])
                    last.then_inc(ev[f"tk{tt}"], 1)
                wait("ck0")
                wait("ck1")
                for m in range(NS):
                    tt, g, half = m // 16, m // 2 % G0, m % 2
                    bk = bank[SB + m % 4]
                    if m < 4:
                        wait("cq", m + 1, 8)
                        if m == 0:
                            wait("cq", 4, 8)
                    else:
                        wait("M", m - 3, NS)
                    rows = slice(half * STK, (half + 1) * STK)
                    nc.tensor.matmul(bk[:, :].rearrange("p (r k) -> p r k", r=2), ident16[:, :],
                                     madd[:, tt, :].unsqueeze(1).broadcast_to([P, 2, S]), start=True, stop=False)
                    for r in range(2):
                        last = nc.tensor.matmul(bk[:, r * S:(r + 1) * S], qT[rows, 2 * g + r, tt * P:(tt + 1) * P],
                                                kT[rows, g, :], start=False, stop=(r == 1))
                    last.then_inc(ev["S"], 1)
                    if m == 24:
                        wait("nm0")
                        turn_q(0, False, 0)
                wait("nm1")
                wait("dk0")
                wait("dk1")
                turn_q(1, False, 2)
                wait("cq", 8, 8)

                def times_v(n):
                    g, half, kc = n // 4, n // 2 % 2, n % 2
                    quad, j = g // 4, g % 4
                    wait("E", n + 1, NS)
                    last = nc.tensor.matmul(bank[2 * quad + half][32 * j:32 * j + 32, :], vv[:, kc, g, :],
                                            prob[:, n % NP, :], start=(kc == 0), stop=(kc == 1))
                    last.then_inc(ev["AV"], 1)

                def turn_o(i):
                    wait("evA", i + 1, 4)
                    for r in range(2):
                        for qt in range(2):
                            c = (2 * r + qt) * P
                            last = nc.tensor.transpose(bank[i][:, c:c + P], av[:, i, c:c + P], ident[:, :])
                    last.then_inc(ev["OT"], 1)
                for n in range(NS + LAG):
                    if n < NS:
                        g, half, kc = n // 4, n // 2 % 2, n % 2
                        rows = slice(half * STK, (half + 1) * STK)
                        bk = bank[SB + n % 4]
                        if n < 4:
                            wait("M", NS - 3 + n, NS)
                        else:
                            wait("E", n - 3, NS)
                        nc.tensor.matmul(bk[:, :].rearrange("p (r k) -> p r k", r=2), ident16[:, :],
                                         maddT[:, kc, :].unsqueeze(1).broadcast_to([P, 2, S]), start=True, stop=False)
                        nc.tensor.matmul(bk[:, :], kT[rows, g, kc * P:(kc + 1) * P],
                                         qT[rows, 2 * g:2 * g + 2, :].rearrange("p r q -> p (r q)"),
                                         start=False, stop=True).then_inc(ev["ST"], 1)
                    if n >= LAG:
                        times_v(n - LAG)
                    if n == NS // 2 + 4 + LAG:
                        turn_o(0)
                        turn_o(1)
                turn_o(2)
                turn_o(3)
                wait("E", NS, NS)
                for tt in range(2):
                    if tt == 0:
                        wait("ON", 8, 4)
                    for k in range(KC):
                        last = nc.tensor.transpose(bank[4 + tt][:, k * P:(k + 1) * P], on[:, tt, k * P:(k + 1) * P],
                                                   ident[:, :])
                    last.then_inc(ev[f"To{tt}"], 1)
                for tt in range(2):
                    wait(f"lO{tt}")
                    for k in range(KC):
                        last = env["three"](bank[6 + tt][:, :], oTh[:, tt, k, :], oTl[:, tt, k, :],
                                            woh[:, k, :], wol[:, k, :], k == 0, k == KC - 1)
                    last.then_inc(ev[f"O{tt}"], 1)

        @block.scalar
        def _(act):
            with act.Fori(0, B) as b:
                def wait(n, count=1, per=1):
                    act.wait_ge(ev[n], b * per + count)
                for tt in range(2):
                    wait(f"dq{tt}")
                    q3 = q32[:, tt, :].rearrange("p (h c) -> p h c", h=H0)
                    nc.scalar.activation(qs[:, tt, :, 0:HD0], q3, ACT.Copy)
                    nc.scalar.activation(qs[:, tt, :, HD0:2 * HD0], q3, ACT.Copy).then_inc(ev[f"hq{tt}"], 1)
                    wait(f"dk{tt}")
                    k4 = k32[:, tt, :].rearrange("p (g c) -> p g c", g=G0).unsqueeze(2).broadcast_to([P, G0, 2, HD0])
                    nc.scalar.activation(ks[:, tt, :, :, 0:HD0], k4, ACT.Copy)
                    nc.scalar.activation(ks[:, tt, :, :, 2 * HD0:3 * HD0], k4, ACT.Copy).then_inc(ev[f"hk{tt}"], 1)

                def take_q(tt, i, b0):
                    for h in range(2):
                        wait("tq", i + h + 1, 8)
                        nc.scalar.activation(qT[:, 8 * h:8 * h + 8, tt * P:(tt + 1) * P],
                                             bank16(b0 + h).rearrange("p (j q) -> p j q", j=8), ACT.Copy)\
                          .then_inc(ev["cq"], 1)
                for tt in range(2):
                    take_q(tt, 2 * tt, 4 + 2 * tt)
                    wait(f"tk{tt}")
                    nc.scalar.activation(kT[:, :, tt * P:(tt + 1) * P],
                                         bank16(tt).rearrange("p (g k) -> p g k", g=G0), ACT.Copy)\
                      .then_inc(ev[f"ck{tt}"], 1)
                for tt in range(2):
                    take_q(tt, 4 + 2 * tt, 2 * tt)

                def evac(quad):
                    wait("AV", 16 * quad + 16, NS)
                    for half in range(2):
                        i = 2 * quad + half
                        nc.scalar.activation(av[:, i, :], bank[i][:, :], ACT.Copy).then_inc(ev["evA"], 1)
                for n in range(NS):
                    wait("ST", n + 1, NS)
                    if n >= NP:
                        wait("AV", n - NP + 1, NS)
                    nc.scalar.activation(prob[:, n % NP, :], bank[SB + n % 4][:, :], ACT.Exp).then_inc(ev["E"], 1)
                    if n == NS // 2 + 4:
                        evac(0)
                evac(1)
                for tt in range(2):
                    wait(f"To{tt}")
                    nc.scalar.activation(oTh[:, tt], bank[4 + tt][:, :].rearrange("p (k c) -> p k c", k=KC), ACT.Copy)\
                      .then_inc(ev[f"hO{tt}"], 1)

        @block.vector
        def _(dve):
            dve.sem_inc(ev["ON"], 4)
            dve.sem_inc(ev["x0"], 1)
            dve.sem_inc(ev["x1"], 1)
            PER = 8
            with dve.Fori(0, B) as b:
                link = Chain(dve, ev["ch"], b * PER)

                def wait(n, count=1, per=1):
                    dve.wait_ge(ev[n], b * per + count)
                for tt in range(2):
                    wait(f"Q{tt}")
                    nc.vector.memset(qs[:, tt, :, NEG:NEG + 1], 0.0)
                    nc.vector.scalar_tensor_tensor(out=q32[:, tt, :], in0=bank[tt][:, :], scalar=HD0 ** -0.5,
                                                   in1=bq[:, :], op0=ALU.mult, op1=ALU.add).then_inc(ev[f"dq{tt}"], 1)
                    wait(f"KV{tt}")
                    nc.vector.tensor_copy(ks[:, tt, :, :, ONE:ONE + 1].rearrange("p g d o -> p (g d) o"),
                                          pad[:, tt, bass.ds(b, 1)].unsqueeze(1).broadcast_to([P, 2 * G0, 1]))
                    nc.vector.tensor_tensor(vv[:, tt, :, 0:HD0],
                                            bank[2 + tt][:, KV:2 * KV].rearrange("p (g c) -> p g c", g=G0),
                                            bkv[:, KV:2 * KV].rearrange("p (g c) -> p g c", g=G0), ALU.add)
                    nc.vector.tensor_tensor(k32[:, tt, :], bank[2 + tt][:, 0:KV], bkv[:, 0:KV],
                                            ALU.add).then_inc(ev[f"dk{tt}"], 1)
                for tt in range(2):
                    wait(f"hq{tt}")
                    nc.vector.tensor_tensor(qs[:, tt, :, 2 * HD0:3 * HD0],
                                            q32[:, tt, :].rearrange("p (h c) -> p h c", h=H0),
                                            qs[:, tt, :, 0:HD0], ALU.subtract).then_inc(ev[f"lq{tt}"], 1)
                    wait(f"hk{tt}")
                    k4 = k32[:, tt, :].rearrange("p (g c) -> p g c", g=G0).unsqueeze(2).broadcast_to([P, G0, 2, HD0])
                    nc.vector.tensor_tensor(ks[:, tt, :, :, HD0:2 * HD0], k4, ks[:, tt, :, :, 0:HD0],
                                            ALU.subtract).then_inc(ev[f"lk{tt}"], 1)
                for m in range(NS):
                    tt, g, half = m // 16, m // 2 % G0, m % 2
                    wait("S", m + 1, NS)
                    nc.vector.tensor_reduce(mx[:, tt, 4 * g + half:4 * g + half + 3:2],
                                            bank[SB + m % 4][:, :].rearrange("p (r k) -> p r k", r=2), AX_X, ALU.max)\
                      .then_inc(ev["M"], 1)
                    if m % 16 == 15:
                        wait("M", m + 1, NS)
                        nc.vector.tensor_scalar(qs[:, tt, :, NEG], mx[:, tt, :], -1.0, None, ALU.mult)\
                          .then_inc(ev[f"nm{tt}"], 1)
                for i in range(4):
                    quad, half = i // 2, i % 2
                    wait("OT", i + 1, 4)
                    o4 = bank[i][:, :].rearrange("p (r t j c) -> p r t j c", r=2, t=2, j=4)
                    link(nc.vector.reciprocal(rec[:, i, :, :], bank[i][:, :].rearrange(
                        "p (s j c) -> p s j c", s=4, j=4)[:, :, :, HD0]))
                    for t in range(2):
                        for r in range(2):
                            o = on[:, t, :].rearrange("p (g r f c) -> p g r f c", g=G0, r=2, f=2)[
                                :, 4 * quad:4 * quad + 4, r, half, :]
                            last = nc.vector.tensor_tensor(
                                o, o4[:, r, t, :, 0:HD0],
                                rec[:, i, 2 * r + t, :].unsqueeze(2).broadcast_to([P, 4, HD0]), ALU.mult)
                    last.then_inc(ev["ON"], 1)
                for tt in range(2):
                    wait(f"hO{tt}")
                    nc.vector.tensor_tensor(oTl[:, tt], bank[4 + tt][:, :].rearrange("p (k c) -> p k c", k=KC),
                                            oTh[:, tt], ALU.subtract).then_inc(ev[f"lO{tt}"], 1)
                for tt in range(2):
                    wait(f"O{tt}")
                    link(nc.vector.tensor_tensor(tmp[:, tt, :], bank[6 + tt][:, :], bo[:, :], ALU.add))
                    link(nc.vector.scalar_tensor_tensor(out=X[:, 2 * b + tt, :], in0=tmp[:, tt, :], scalar=tg[:, 0:1],
                                                        in1=X[:, 2 * b + tt, :], op0=ALU.mult, op1=ALU.add))
                    nc.vector.memset(mx[:, 0, 0:1], 0.0).then_inc(ev[f"x{tt}"], 1)
                assert link.n == PER, link.n
    st.close()


def phase_b(nc, a, env):
    sem, bank, bank16, X, XTh, XTl, ident, ident16, tg = (env[k] for k in (
        "sem", "bank", "bank16", "X", "XTh", "XTl", "ident", "ident16", "tg"))
    st = ExitStack()

    def sb(name, shape, dt=F32):
        return env["sb"](name, shape, dt, stack=st)

    env["front"]("bit", XTh, XTl)
    NH = F0 // D
    HC = F0 // P
    wfc = sb("b_wfc", [P, NH, KC, D], F16)
    wpj = sb("b_wpj", [P, HC, D], F16)
    scale = sb("b_scale", [P, 8])

    wst = ExitStack()

    def wb(name, shape, dt=F32):
        return env["sb"](name, shape, dt, stack=wst)

    NUNIT = 2 * NH
    stage = wb("b_stage", [P, 2, 4, D])
    junk = wb("b_junk", [P, 4 * D])
    part = wb("b_part", [P, NUNIT])
    sums = wb("b_sums", [P, 2])
    ones = wb("b_ones", [P, P])
    below = wb("b_below", [P, 2, 4, D], F16)
    tern = wb("b_tern", [P, 2, 4, D], F16)
    t_in = [sem("t_in0"), sem("t_in1")]
    t_abs, t_ch, t_part, t_tot, t_use, t_ter, t_tr, t_cp = (sem("t_" + n) for n in (
        "abs", "ch", "part", "tot", "use", "ter", "tr", "cp"))

    def unit(u):
        if u < NH:
            return a["L0_ffn_w_fc"][u * D:(u + 1) * D, :].rearrange("(r p) c -> p r c", p=P)
        return a["L0_ffn_w_proj"][:, (u - NH) * D:(u - NH + 1) * D].rearrange("(r p) c -> p r c", p=P)

    with nc.Block() as block:
        @block.sync
        def _(sp):
            for n in range(2 * NUNIT):
                if n >= 2 and n - 2 < NUNIT:
                    sp.wait_ge(t_abs, n - 1)
                elif n >= 2:
                    sp.wait_ge(t_use, n - 1 - NUNIT)
                sp.dma_start(stage[:, n % 2, :, :], unit(n % NUNIT)).then_inc(t_in[n % 2], 16)

        @block.scalar
        def _(act):
            for u in range(NUNIT):
                if u:
                    act.wait_ge(t_abs, u)
                act.wait_ge(t_in[u % 2], 16 * (u // 2 + 1))
                nc.scalar.activation(junk[:, :], stage[:, u % 2, :, :].rearrange("p r c -> p (r c)"), ACT.Abs,
                                     accum_out=part[:, u:u + 1]).then_inc(t_abs, 1)
            for u in range(NUNIT):
                for h in range(2):
                    act.wait_ge(t_tr, 2 * u + h + 1)
                    if u < NH:
                        dst = wfc[:, u, 2 * h:2 * h + 2, :]
                    else:
                        dst = wpj[:, KC * (u - NH) + 2 * h:KC * (u - NH) + 2 * h + 2, :]
                    nc.scalar.activation(dst, bank16(h).rearrange("p (k c) -> p k c", k=2),
                                         ACT.Copy).then_inc(t_cp, 1)

        @block.vector
        def _(dve):
            link = Chain(dve, t_ch)
            link(nc.vector.memset(ones[:, :], 1.0))
            dve.wait_ge(t_abs, NUNIT)
            nc.vector.reduce_sum(sums[:, :], part[:, :].rearrange("p (m u) -> p m u", m=2), AX_X).then_inc(t_part, 1)
            dve.wait_ge(t_tot, 1)
            link(nc.vector.tensor_scalar(scale[:, 0:2], bank[2][:, 0:2], 1.0 / (F0 * D), None, ALU.mult))
            link(nc.vector.tensor_scalar(scale[:, 2:4], scale[:, 0:2], 1e-6, 0.5, ALU.add, ALU.mult))
            link(nc.vector.tensor_scalar(scale[:, 4:6], scale[:, 2:4], -1.0, None, ALU.mult))
            link(nc.vector.tensor_tensor(scale[:, 6:7], scale[:, 1:2], tg[:, 2:3], ALU.mult))
            for u in range(NUNIT):
                m = u // NH
                dve.wait_ge(t_in[u % 2], 16 * (NUNIT // 2 + u // 2 + 1))
                link(nc.vector.tensor_scalar(below[:, u % 2, :, :], stage[:, u % 2, :, :], scale[:, 4 + m:5 + m], None,
                                             ALU.is_lt))
                if u >= 2:
                    dve.wait_ge(t_tr, 2 * (u - 1))
                nc.vector.scalar_tensor_tensor(out=tern[:, u % 2, :, :], in0=stage[:, u % 2, :, :],
                                               scalar=scale[:, 2 + m:3 + m], in1=below[:, u % 2, :, :],
                                               op0=ALU.is_gt, op1=ALU.subtract).then_inc(t_use, 1)

        @block.tensor
        def _(pe):
            pe.wait_ge(t_part, 1)
            nc.tensor.matmul(bank[2][:, 0:2], ones[:, :], sums[:, :], start=True, stop=True).then_inc(t_tot, 1)
            for u in range(NUNIT):
                pe.wait_ge(t_use, u + 1)
                for h in range(2):
                    if u:
                        pe.wait_ge(t_cp, 2 * (u - 1) + h + 1)
                    for k in range(2):
                        for r in range(4):
                            last = nc.tensor.transpose(bank16(h)[:, (4 * k + r) * P:(4 * k + r + 1) * P],
                                                       tern[:, u % 2, r, (2 * h + k) * P:(2 * h + k + 1) * P],
                                                       ident16[:, :])
                    last.then_inc(t_tr, 1)
    wst.close()

    TPB = 4
    h32 = sb("b_h", [P, 2, F0])
    xn = sb("b_xn", [P, 2, F0])
    hTh = sb("b_hTh", [P, 2, HC, P], F16)
    hTl = sb("b_hTl", [P, 2, HC, P], F16)
    stats = sb("b_stats", [P, 2, NH, 6])
    mv = sb("b_mv", [P, 2, 2])
    ve = sb("b_ve", [P, 2, 1])
    rs = sb("b_rs", [P, 2, 2])
    q = sb("b_q", [P, 2, 4])
    mhalf = sb("b_mh", [P, 1])
    hold = sb("b_hold", [P, 1])
    b_up, b_ge, b_ch, b_var, b_rs, b_nm, b_xn, b_q, b_tr, b_hi, b_lo, b_dn, b_out, b_mh = (sem("b_" + n) for n in (
        "up", "gelu", "chain", "var", "rstd", "nmean", "norm", "quant", "tr", "hi", "lo", "down", "out", "mh"))
    UP, TR, ACC = 0, 2, 4

    with nc.Block() as block:
        @block.gpsimd
        def _(pool):
            nc.gpsimd.memset(mhalf[:, :], -0.5).then_inc(b_mh, 1)
            pool.wait_ge(b_mh, 1)
            with pool.Fori(0, TILES // 2) as i:
                for p in range(2):
                    pool.wait_ge(b_var, 2 * i + p + 1)
                    nc.gpsimd.tensor_tensor(rs[:, p, 0:1], ve[:, p, :], mhalf[:, :], ALU.pow).then_inc(b_rs, 1)

        @block.tensor
        def _(pe):
            pe.sem_inc(b_dn, 2)
            pe.sem_inc(b_tr, 2 * KC)
            with pe.Fori(0, TILES // TPB) as t:
                def up(i):
                    n = t * TPB + i
                    for h in range(NH):
                        pe.wait_ge(b_ge, NH * n + h + 1)
                        for k in range(KC):
                            x = bass.ds(n * P, P)
                            nc.tensor.matmul(bank[UP + h % 2][:, :], XTh[:, k, x], wfc[:, h, k, :],
                                             start=(k == 0), stop=False)
                            last = nc.tensor.matmul(bank[UP + h % 2][:, :], XTl[:, k, x], wfc[:, h, k, :],
                                                    start=False, stop=(k == KC - 1))
                        last.then_inc(b_up, 1)

                def turn(i):
                    n = t * TPB + i
                    pe.wait_ge(b_q, n + 1)
                    for g in range(KC):
                        pe.wait_ge(b_lo, KC * n + g + 1)
                        for r in range(4):
                            c = (4 * g + r) * P
                            last = nc.tensor.transpose(bank[TR + g % 2][:, r * P:(r + 1) * P],
                                                       xn[:, i % 2, c:c + P], ident[:, :])
                        last.then_inc(b_tr, 1)

                def down(i):
                    n = t * TPB + i
                    pe.wait_ge(b_lo, KC * n + KC + 2)
                    pe.wait_ge(b_out, t * TPB + i + 1)
                    for c in range(HC):
                        nc.tensor.matmul(bank[ACC + i][:, :], hTh[:, i % 2, c, :], wpj[:, c, :],
                                         start=(c == 0), stop=False)
                        last = nc.tensor.matmul(bank[ACC + i][:, :], hTl[:, i % 2, c, :], wpj[:, c, :],
                                                start=False, stop=(c == HC - 1))
                    last.then_inc(b_dn, 1)
                up(0)
                up(1)
                turn(0)
                up(2)
                down(0)
                turn(1)
                up(3)
                down(1)
                turn(2)
                down(2)
                turn(3)
                down(3)

        @block.scalar
        def _(act):
            act.sem_inc(b_ge, 2)
            with act.Fori(0, TILES // TPB) as t:
                def gelu(i, pieces):
                    n = t * TPB + i
                    for h in pieces:
                        act.wait_ge(b_up, NH * n + h + 1)
                        nc.scalar.activation(h32[:, i % 2, h * D:(h + 1) * D], bank[UP + h % 2][:, :], ACT.Gelu,
                                             scale=scale[:, 0:1]).then_inc(b_ge, 1)

                def norm(i):
                    n = t * TPB + i
                    act.wait_ge(b_nm, n + 1)
                    act.wait_ge(b_tr, KC * n + KC)
                    nc.scalar.activation(xn[:, i % 2, :], h32[:, i % 2, :], ACT.Identity, bias=rs[:, i % 2, 1:2],
                                         scale=rs[:, i % 2, 0:1]).then_inc(b_xn, 1)

                def high(i):
                    n = t * TPB + i
                    act.wait_ge(b_dn, n + 1)
                    for g in range(KC):
                        act.wait_ge(b_tr, KC * n + g + 1 + 2 * KC)
                        nc.scalar.activation(hTh[:, i % 2, 4 * g:4 * g + 4, :],
                                             bank[TR + g % 2][:, :].rearrange("p (r c) -> p r c", r=4),
                                             ACT.Copy).then_inc(b_hi, 1)
                gelu(0, range(NH))
                gelu(1, (0, 1))
                norm(0)
                gelu(1, (2, 3))
                high(0)
                gelu(2, (0, 1))
                norm(1)
                gelu(2, (2, 3))
                high(1)
                gelu(3, (0, 1))
                norm(2)
                gelu(3, (2, 3))
                high(2)
                norm(3)
                high(3)

        @block.vector
        def _(dve):
            dve.sem_inc(b_lo, 2)
            dve.sem_inc(b_out, TPB)
            PER = TPB * (NH + 1 + 5)
            with dve.Fori(0, TILES // TPB) as t:
                link = Chain(dve, b_ch, t * PER)

                def stat(i, pieces):
                    n = t * TPB + i
                    for h in pieces:
                        dve.wait_ge(b_ge, NH * n + h + 3)
                        link(nc.vector.bn_stats(stats[:, i % 2, h, :], h32[:, i % 2, h * D:(h + 1) * D]))

                def moments(i):
                    n = t * TPB + i
                    nc.vector.memset(hold[:, :], 0.0)
                    link(nc.vector.bn_aggr(mv[:, i % 2, :], stats[:, i % 2, :, :].rearrange("p h s -> p (h s)")))
                    nc.vector.tensor_scalar(ve[:, i % 2, :], mv[:, i % 2, 1:2], 1e-6, None, ALU.add).then_inc(b_var, 1)
                    dve.wait_ge(b_rs, n + 1)
                    nc.vector.scalar_tensor_tensor(out=rs[:, i % 2, 1:2], in0=mv[:, i % 2, 0:1], scalar=-1.0,
                                                   in1=rs[:, i % 2, 0:1], op0=ALU.mult, op1=ALU.mult).then_inc(b_nm, 1)

                def quant(i):
                    dve.wait_ge(b_xn, t * TPB + i + 1)
                    env["quantise"](link, xn[:, i % 2, :], q[:, i % 2, :]).then_inc(b_q, 1)

                def low(i):
                    n = t * TPB + i
                    for g in range(KC):
                        dve.wait_ge(b_hi, KC * n + g + 1)
                        nc.vector.tensor_tensor(hTl[:, i % 2, 4 * g:4 * g + 4, :],
                                                bank[TR + g % 2][:, :].rearrange("p (r c) -> p r c", r=4),
                                                hTh[:, i % 2, 4 * g:4 * g + 4, :], ALU.subtract).then_inc(b_lo, 1)

                def result(i):
                    n = t * TPB + i
                    dve.wait_ge(b_dn, n + 3)
                    nc.vector.scalar_tensor_tensor(out=X[:, n, :], in0=bank[ACC + i][:, :], scalar=scale[:, 6:7],
                                                   in1=X[:, n, :], op0=ALU.mult, op1=ALU.add).then_inc(b_out, 1)
                stat(0, range(NH))
                moments(0)
                stat(1, (0, 1))
                quant(0)
                stat(1, (2, 3))
                moments(1)
                low(0)
                stat(2, (0, 1))
                quant(1)
                stat(2, (2, 3))
                moments(2)
                low(1)
                result(0)
                stat(3, (0, 1))
                quant(2)
                stat(3, (2, 3))
                moments(3)
                low(2)
                result(1)
                quant(3)
                low(3)
                result(2)
                result(3)
                assert link.n == PER, link.n
    st.close()


def phase_c(nc, a, env):
    sem, bank, bank16, X, XTh, XTl, ident, ident16, tg = (env[k] for k in (
        "sem", "bank", "bank16", "X", "XTh", "XTl", "ident", "ident16", "tg"))
    st = ExitStack()

    def sb(name, shape, dt=F32):
        return env["sb"](name, shape, dt, stack=st)

    CTh, CTl = env["CTh"], env["CTl"]
    env["front"]("ln", XTh, XTl)
    NW = 5
    WQ, WG, WK, WV, WO = range(NW)
    wh = sb("c_wh", [P, NW, KC, D], F16)
    wl = sb("c_wl", [P, NW, KC, D], F16)
    wkv = a["L1_xattn_Wkv"]
    source = {WQ: a["L1_xattn_Wq"], WG: a["L1_xattn_Wg"], WK: wkv[0:D, :], WV: wkv[D:2 * D, :], WO: a["L1_xattn_Wo"]}
    env["prepare"]([(source[w], wh[:, w], wl[:, w]) for w in range(NW)])

    bg = sb("c_bg", [P, D])
    blocks = sb("c_blocks", [P, P])
    heads = sb("c_heads", [P, 4])
    GPH = P // HD1
    ek = sb("c_ek", [P, 2, D])
    kk = sb("c_k", [P, 2, D])
    vv = sb("c_v", [P, 2, D])
    eq = sb("c_eq", [P, 2, D])
    qq = sb("c_q", [P, 2, D])
    gt = sb("c_gt", [P, 2, D])
    kv = sb("c_kv", [P, KC, P])
    ks = sb("c_ks", [P, KC, GPH])
    ksr = sb("c_ksr", [P, KC])
    onec = sb("c_one", [P, 1])
    den = sb("c_den", [P, 2, H1])
    og = sb("c_og", [P, 2, D])
    oTh = sb("c_oTh", [P, 2, KC, P], F16)
    oTl = sb("c_oTl", [P, 2, KC, P], F16)
    T = B

    c_in = sem("c_in")
    c_cst = sem("c_const")
    names = ("K0", "K1", "V0", "V1", "Q0", "Q1", "G0", "G1",
             "eK0", "eK1", "eQ0", "eQ1", "tG0", "tG1", "cV0", "cV1", "lG0", "lG1",
             "pK0", "pK1", "pQ0", "pQ1",
             "SUM", "mSUM", "ATT0", "ATT1", "OG0", "OG1", "T0", "T1", "hT0", "hT1", "lT0", "lT1", "O0", "O1",
             "X0", "X1", "ch")
    ev = {n: sem("c_" + n) for n in names}

    with nc.Block() as block:
        @block.sync
        def _(sp):
            sp.dma_start(bg[:, :], env["row"](a["L1_xattn_bg"])).then_inc(c_in, 16)

        @block.gpsimd
        def _(pool):
            nc.gpsimd.memset(onec[:, :], 1.0).then_inc(c_cst, 1)

        @block.vector
        def _(dve):
            link = Chain(dve, ev["ch"])
            link(nc.vector.reduce_sum(heads[:, :], ident[:, :].rearrange("p (h c) -> p h c", h=GPH), AX_X))
            link(nc.vector.tensor_copy(blocks[:, :].rearrange("p (h c) -> p h c", h=GPH),
                                       heads[:, :].unsqueeze(2).broadcast_to([P, GPH, HD1])))

    with nc.Block() as block:
        @block.tensor
        def _(pe):
            pe.wait_ge(c_cst, 1)
            with pe.Fori(0, T) as b:
                def wait(n, credit=0):
                    pe.wait_ge(ev[n], b + 1 + credit)

                def before(n):
                    pe.wait_ge(ev[n], b + 1)

                def project(dst, xh, xl, w, tt, n):
                    x = bass.ds((2 * b + tt) * P, P)
                    for k in range(KC):
                        last = env["three"](dst, xh[:, k, x], xl[:, k, x], wh[:, w, k, :], wl[:, w, k, :],
                                            k == 0, k == KC - 1)
                    last.then_inc(ev[n], 1)
                before("mSUM")
                project(bank[0][:, :], CTh, CTl, WK, 0, "K0")
                before("X0")
                project(bank[1][:, :], CTh, CTl, WK, 1, "K1")
                before("X1")
                project(bank[2][:, :], CTh, CTl, WV, 0, "V0")
                before("OG1")
                project(bank[3][:, :], CTh, CTl, WV, 1, "V1")
                for half in range(2):
                    before(("lT0", "lT1")[half])
                    for oc in range(2):
                        o = (2 * half + oc) * P
                        for k in range(KC):
                            x = bass.ds(2 * b * P, 2 * P)
                            last = env["three"](bank[4 + half][:, oc * 2 * P:(oc + 1) * 2 * P],
                                                wh[:, WQ, k, o:o + P], wl[:, WQ, k, o:o + P],
                                                XTh[:, k, x], XTl[:, k, x], k == 0, k == KC - 1)
                    last.then_inc(ev[("Q0", "Q1")[half]], 1)
                for tt in range(2):
                    before(("OG0", "OG1")[tt])
                    project(bank[6 + tt][:, :], XTh, XTl, WG, tt, ("G0", "G1")[tt])
                wait("pK0")
                wait("pK1")
                wait("cV0")
                wait("cV1")
                for c in range(KC):
                    for tt in range(2):
                        nc.tensor.matmul(bank[0][:, c * P:(c + 1) * P], kk[:, tt, c * P:(c + 1) * P],
                                         vv[:, tt, c * P:(c + 1) * P], start=(tt == 0), stop=(tt == 1))
                for c in range(KC):
                    for tt in range(2):
                        last = nc.tensor.matmul(bank[1][:, c:c + 1], kk[:, tt, c * P:(c + 1) * P], onec[:, :],
                                                start=(tt == 0), stop=(tt == 1))
                last.then_inc(ev["SUM"], 1)
                pe.wait_ge(ev["mSUM"], b + 2)
                wait("pQ0")
                wait("pQ1")
                for tt in range(2):
                    pe.wait_ge(ev[("lG0", "lG1")[tt]], b + 2)
                    for c in range(KC):
                        qT = qq[:, c // 2, (c % 2) * 2 * P + tt * P:(c % 2) * 2 * P + (tt + 1) * P]
                        nc.tensor.matmul(bank[2 + tt][:, c * P:(c + 1) * P], qT, kv[:, c, :], start=True, stop=True)
                    for c in range(KC):
                        qT = qq[:, c // 2, (c % 2) * 2 * P + tt * P:(c % 2) * 2 * P + (tt + 1) * P]
                        last = nc.tensor.matmul(bank[6 + tt][:, c * GPH:(c + 1) * GPH], qT, ks[:, c, :],
                                                start=True, stop=True)
                    last.then_inc(ev[("ATT0", "ATT1")[tt]], 1)
                for tt in range(2):
                    pe.wait_ge(ev[("OG0", "OG1")[tt]], b + 2)
                    for k in range(KC):
                        last = nc.tensor.transpose(bank[4 + tt][:, k * P:(k + 1) * P],
                                                   og[:, tt, k * P:(k + 1) * P], ident[:, :])
                    last.then_inc(ev[("T0", "T1")[tt]], 1)
                for tt in range(2):
                    pe.wait_ge(ev[("lT0", "lT1")[tt]], b + 2)
                    for k in range(KC):
                        last = env["three"](bank[1 + tt][:, :], oTh[:, tt, k, :], oTl[:, tt, k, :],
                                            wh[:, WO, k, :], wl[:, WO, k, :], k == 0, k == KC - 1)
                    last.then_inc(ev[("O0", "O1")[tt]], 1)

        @block.scalar
        def _(act):
            with act.Fori(0, T) as b:
                def step(waits, ins_fn, n):
                    for w in waits:
                        act.wait_ge(ev[w], b + 1)
                    ins_fn().then_inc(ev[n], 1)
                for tt in range(2):
                    step((("K0", "K1")[tt],), lambda: nc.scalar.activation(ek[:, tt, :], bank[tt][:, :], ACT.Exp),
                         ("eK0", "eK1")[tt])
                for tt in range(2):
                    step((("V0", "V1")[tt],), lambda: nc.scalar.activation(vv[:, tt, :], bank[2 + tt][:, :], ACT.Copy),
                         ("cV0", "cV1")[tt])
                for tt in range(2):
                    step((("Q0", "Q1")[tt],), lambda: nc.scalar.activation(eq[:, tt, :], bank[4 + tt][:, :], ACT.Exp),
                         ("eQ0", "eQ1")[tt])
                for tt in range(2):
                    act.wait_ge(ev[("lG0", "lG1")[tt]], b + 2)
                    nc.scalar.activation(gt[:, tt, :], gt[:, tt, :], ACT.Tanh, scale=0.5)\
                      .then_inc(ev[("tG0", "tG1")[tt]], 1)
                for tt in range(2):
                    step((("T0", "T1")[tt],),
                         lambda: nc.scalar.activation(oTh[:, tt], bank[4 + tt][:, :].rearrange("p (k c) -> p k c", k=KC),
                                                      ACT.Copy), ("hT0", "hT1")[tt])

        @block.vector
        def _(dve):
            for n in ("mSUM", "X0", "X1", "OG0", "OG1", "lT0", "lT1", "lG0", "lG1"):
                dve.sem_inc(ev[n], 1)
            dve.wait_ge(c_in, 16)
            PER = 2 + 2 + 1 + 2 * 4
            with dve.Fori(0, T) as b:
                link = Chain(dve, ev["ch"], b * PER + 2)

                def phi(dst, e, src, n):
                    link(nc.vector.tensor_scalar(e, e, 1.0, None, ALU.min))
                    nc.vector.scalar_tensor_tensor(out=dst, in0=src, scalar=0.0, in1=e, op0=ALU.max,
                                                   op1=ALU.add).then_inc(ev[n], 1)
                for tt in range(2):
                    dve.wait_ge(ev[("eK0", "eK1")[tt]], b + 1)
                    phi(kk[:, tt, :], ek[:, tt, :], bank[tt][:, :], ("pK0", "pK1")[tt])
                for tt in range(2):
                    dve.wait_ge(ev[("eQ0", "eQ1")[tt]], b + 1)
                    phi(qq[:, tt, :], eq[:, tt, :], bank[4 + tt][:, :], ("pQ0", "pQ1")[tt])
                for tt in range(2):
                    dve.wait_ge(ev[("G0", "G1")[tt]], b + 1)
                    nc.vector.tensor_tensor(gt[:, tt, :], bank[6 + tt][:, :], bg[:, :], ALU.add)\
                      .then_inc(ev[("lG0", "lG1")[tt]], 1)
                dve.wait_ge(ev["SUM"], b + 1)
                nc.vector.tensor_tensor(kv[:, :, :], bank[0][:, :].rearrange("p (k c) -> p k c", k=KC),
                                        blocks[:, :].unsqueeze(1).broadcast_to([P, KC, P]), ALU.mult)
                link(nc.vector.tensor_copy(ksr[:, :], bank[1][:, 0:KC]))
                nc.vector.tensor_tensor(ks[:, :, :], ksr[:, :].unsqueeze(2).broadcast_to([P, KC, GPH]),
                                        heads[:, :].unsqueeze(1).broadcast_to([P, KC, GPH]), ALU.mult)\
                  .then_inc(ev["mSUM"], 1)
                for tt in range(2):
                    dve.wait_ge(ev[("ATT0", "ATT1")[tt]], b + 1)
                    link(nc.vector.tensor_scalar(den[:, tt, :], bank[6 + tt][:, 0:H1], 1e-6, None, ALU.add))
                    link(nc.vector.reciprocal(den[:, tt, :], den[:, tt, :]))
                    o3 = og[:, tt, :].rearrange("p (h c) -> p h c", h=H1)
                    link(nc.vector.tensor_tensor(o3, bank[2 + tt][:, :].rearrange("p (h c) -> p h c", h=H1),
                                                 den[:, tt, :].unsqueeze(2).broadcast_to([P, H1, HD1]), ALU.mult))
                    dve.wait_ge(ev[("tG0", "tG1")[tt]], b + 1)
                    link(nc.vector.tensor_scalar(gt[:, tt, :], gt[:, tt, :], 0.5, 0.5, ALU.mult, ALU.add))
                    nc.vector.tensor_tensor(og[:, tt, :], og[:, tt, :], gt[:, tt, :], ALU.mult)\
                      .then_inc(ev[("OG0", "OG1")[tt]], 1)
                for tt in range(2):
                    dve.wait_ge(ev[("hT0", "hT1")[tt]], b + 1)
                    nc.vector.tensor_tensor(oTl[:, tt], bank[4 + tt][:, :].rearrange("p (k c) -> p k c", k=KC),
                                            oTh[:, tt], ALU.subtract).then_inc(ev[("lT0", "lT1")[tt]], 1)
                for tt in range(2):
                    dve.wait_ge(ev[("O0", "O1")[tt]], b + 1)
                    xt = X[:, 2 * b + tt, :]
                    nc.vector.scalar_tensor_tensor(out=xt, in0=bank[1 + tt][:, :], scalar=tg[:, 1:2], in1=xt,
                                                   op0=ALU.mult, op1=ALU.add).then_inc(ev[("X0", "X1")[tt]], 1)
                assert link.n == PER, link.n
    st.close()


def phase_d(nc, a, env):
    sem, bank, bank16, X, XTh, XTl, ident, ident16, tg = (env[k] for k in (
        "sem", "bank", "bank16", "X", "XTh", "XTl", "ident", "ident16", "tg"))
    st = ExitStack()

    def sb(name, shape, dt=F32):
        return env["sb"](name, shape, dt, stack=st)

    env["front"]("ln", XTh, XTl)
    NU = 3
    wh = sb("d_wh", [P, 2, NU, KC, CH], F16)
    wl = sb("d_wl", [P, 2, NU, KC, CH], F16)
    stage = sb("d_stage", [P, NU, 4, P])
    combT = sb("d_combT", [P, TILES * P], F16)
    pick = sb("d_pick", [P, E, P], F16)

    rst = ExitStack()

    def rb(name, shape, dt=F32):
        return env["sb"](name, shape, dt, stack=rst)

    rw = rb("r_w", [E, D])
    rwT = rb("r_wT", [P, KC, 2 * E], F16)
    ebias = rb("r_bias", [P, E])
    sc = rb("r_sc", [P, TILES, E])
    sel = rb("r_sel", [P, TILES, E])
    rank = rb("r_rank", [P, TILES, E])
    cmp_ = rb("r_cmp", [P, TILES, E])
    tot = rb("r_tot", [P, TILES])
    inv = rb("r_inv", [P, TILES])
    both = rb("r_both", [P, TILES, 2 * E], F16)
    ones = rb("r_ones", [2 * E, E])
    r_in, r_wt, r_whi, r_wlo, r_lg, r_add, r_sig, r_ch, r_split, r_tr, r_done = (sem("r_" + n) for n in (
        "in", "wt", "whi", "wlo", "lg", "add", "sig", "ch", "split", "tr", "done"))
    with nc.Block() as block:
        @block.sync
        def _(sp):
            sp.dma_start(rw[:, :], a["L1_ffn_router_w"]).then_inc(r_in, 16)
            sp.dma_start(ebias[:, :], env["row"](a["L1_ffn_expert_bias"])).then_inc(r_in, 16)

        @block.tensor
        def _(pe):
            pe.wait_ge(r_in, 32)
            for k in range(KC):
                last = nc.tensor.transpose(bank[0][:, k * E:(k + 1) * E], rw[:, k * P:(k + 1) * P], ident[0:E, 0:E])
            last.then_inc(r_wt, 1)
            pe.wait_ge(r_wlo, 1)
            with pe.Fori(0, TILES) as i:
                for k in range(KC):
                    cols = bass.ts(i, P)
                    nc.tensor.matmul(bank[1][:, bass.ts(i, 2 * E)], XTh[:, k, cols], rwT[:, k, :],
                                     start=(k == 0), stop=False)
                    nc.tensor.matmul(bank[1][:, bass.ds(i * 2 * E, E)], XTl[:, k, cols], rwT[:, k, 0:E],
                                     start=False, stop=(k == KC - 1)).then_inc(r_lg, 1)
            pe.wait_ge(r_split, 1)
            for i in range(TILES):
                last = nc.tensor.transpose(bank16(2 + i // 8)[0:2 * E, (i % 8) * P:(i % 8 + 1) * P],
                                           both[:, i, :], ident16[:, :])
            last.then_inc(r_tr, 1)

        @block.scalar
        def _(act):
            act.wait_ge(r_wt, 1)
            nc.scalar.activation(rwT[:, :, 0:E], bank[0][:, 0:KC * E].rearrange("p (k e) -> p k e", k=KC),
                                 ACT.Copy).then_inc(r_whi, 1)
            act.wait_ge(r_add, 1)
            nc.scalar.activation(sc[:, :, :], rank[:, :, :], ACT.Sigmoid).then_inc(r_sig, 1)
            act.wait_ge(r_tr, 1)
            for h in range(2):
                nc.scalar.activation(combT[0:2 * E, h * 1024:(h + 1) * 1024], bank16(2 + h)[0:2 * E, :],
                                     ACT.Copy).then_inc(r_done, 1)

        @block.vector
        def _(dve):
            link = Chain(dve, r_ch)
            link(nc.vector.memset(combT[:, :], 0.0))
            link(nc.vector.memset(pick[:, :, :], 0.0))
            link(nc.vector.tensor_tensor(ones[:, :], ident16[0:2 * E, 0:E], ident16[0:2 * E, E:2 * E], ALU.add))
            link(nc.vector.tensor_copy(pick[0:2 * E, :, :], ones[:, :].unsqueeze(2).broadcast_to([2 * E, E, P])))
            dve.wait_ge(r_whi, 1)
            nc.vector.tensor_tensor(rwT[:, :, E:2 * E], bank[0][:, 0:KC * E].rearrange("p (k e) -> p k e", k=KC),
                                    rwT[:, :, 0:E], ALU.subtract).then_inc(r_wlo, 1)
            dve.wait_ge(r_lg, TILES * KC)
            lg = bank[1][:, 0:TILES * 2 * E].rearrange("p (t e) -> p t e", t=TILES)
            link(nc.vector.tensor_copy(cmp_[:, :, :], lg[:, :, E:2 * E]))
            nc.vector.tensor_tensor(rank[:, :, :], lg[:, :, 0:E], cmp_[:, :, :], ALU.add).then_inc(r_add, 1)
            dve.wait_ge(r_sig, 1)
            link(nc.vector.tensor_tensor(sel[:, :, :], sc[:, :, :],
                                         ebias[:, :].unsqueeze(1).broadcast_to([P, TILES, E]), ALU.add))
            link(nc.vector.memset(rank[:, :, :], 0.0))
            for d in range(1, E):
                link(nc.vector.tensor_tensor(cmp_[:, :, 0:E - d], sel[:, :, 0:E - d], sel[:, :, d:E], ALU.is_ge))
                link(nc.vector.tensor_tensor(rank[:, :, d:E], rank[:, :, d:E], cmp_[:, :, 0:E - d], ALU.add))
                link(nc.vector.tensor_tensor(cmp_[:, :, 0:E - d], sel[:, :, d:E], sel[:, :, 0:E - d], ALU.is_gt))
                link(nc.vector.tensor_tensor(rank[:, :, 0:E - d], rank[:, :, 0:E - d], cmp_[:, :, 0:E - d], ALU.add))
            link(nc.vector.scalar_tensor_tensor(out=sel[:, :, :], in0=rank[:, :, :], scalar=1.5, in1=sc[:, :, :],
                                                op0=ALU.is_lt, op1=ALU.mult))
            link(nc.vector.reduce_sum(tot[:, :], sel[:, :, :], AX_X))
            link(nc.vector.tensor_scalar(tot[:, :], tot[:, :], 1e-9, None, ALU.add))
            link(nc.vector.reciprocal(inv[:, :], tot[:, :]))
            link(nc.vector.tensor_tensor(sel[:, :, :], sel[:, :, :],
                                         inv[:, :].unsqueeze(2).broadcast_to([P, TILES, E]), ALU.mult))
            link(nc.vector.tensor_copy(both[:, :, 0:E], sel[:, :, :]))
            nc.vector.tensor_tensor(both[:, :, E:2 * E], sel[:, :, :], both[:, :, 0:E],
                                    ALU.subtract).then_inc(r_split, 1)
    rst.close()

    silu = sb("d_silu", [P, BLK])
    hid = sb("d_hid", [P, 2, BLK])
    hh = sb("d_hh", [P, 2, BLK], F16)
    hl = sb("d_hl", [P, 2, BLK], F16)
    d_g, d_u, d_s, d_hm, d_h, d_hi, d_lo, d_dn, d_accf, d_bc = (sem("d_" + n) for n in (
        "gate", "up", "silu", "mul", "weighted", "hi", "lo", "down", "acc_free", "bc"))
    p_st = [sem(f"p_stage{k}") for k in range(NU)]
    p_tr, p_hi, p_lo = sem("p_tr"), sem("p_hi"), sem("p_lo")
    PRE = NU * KC
    GATE, UP, BC, TR = 4, 5, 6, 7
    NS = FS // CH
    NR = E * FR // CH
    BPC = TILES * P // BLK
    TPB = BLK // P

    def source(c, k, t):
        if k < 2:
            if isinstance(c, tuple):
                return [a["L1_ffn_w12"][2 * c[1] + j, k * FR:(k + 1) * FR, t * P:(t + 1) * P]
                        .rearrange("(r p) c -> p r c", p=P) for j in range(2)]
            w = a[("L1_ffn_sw1", "L1_ffn_sw2")[k]]
            return [w[bass.ts(c, CH), t * P:(t + 1) * P].rearrange("(r p) c -> p r c", p=P)]
        if isinstance(c, tuple):
            return [a["L1_ffn_w3"][2 * c[1] + t // 2, :, (t % 2) * P:(t % 2 + 1) * P]
                    .rearrange("(r p) c -> p r c", p=P)]
        return [a["L1_ffn_sw3"][:, bass.ds(c * CH + t * P, P)].rearrange("(r p) c -> p r c", p=P)]

    def plan(eng, chunk):
        with eng.Fori(0, NS // 2 - 1) as cp:
            chunk(2 * cp, 0, None, 2 * cp + 1)
            chunk(2 * cp + 1, 1, None, 2 * cp + 2)
        chunk(NS - 2, 0, None, NS - 1)
        chunk(NS - 1, 1, None, ("routed", 0))
        for r in range(NR):
            chunk(NS + r, r % 2, r, ("routed", r + 1) if r + 1 < NR else None)

    with nc.Block() as block:
        @block.sync
        def _(sp):
            def load(c, q):
                for t in range(BPC):
                    for k in range(NU):
                        sp.wait_ge(p_tr, q + NU * t + k + 1)
                        parts = source(c, k, t)
                        w = 4 // len(parts)
                        for j, part in enumerate(parts):
                            sp.dma_start(stage[:, k, w * j:w * j + w, :], part)\
                              .then_inc(p_st[k], 16)
            for c in range(NS):
                load(c, PRE * c)
            for r in range(NR):
                load(("routed", r), PRE * (NS + r))

        @block.tensor
        def _(pe):
            pe.sem_inc(p_tr, NU)
            pe.sem_inc(d_dn, 2)

            def transposes(k, q, dma):
                pe.wait_ge(p_st[k], dma)
                pe.wait_ge(p_lo, q + 1)
                for r in range(4):
                    last = nc.tensor.transpose(bank[TR][:, r * P:(r + 1) * P], stage[:, k, r, :], ident[:, :])
                last.then_inc(p_tr, 1)

            def down(j, s, n, par):
                pe.wait_ge(d_lo, s + 1)
                if j == 0:
                    pe.wait_ge(d_accf, n + 1)
                for tt in range(TPB):
                    cols = slice(tt * P, (tt + 1) * P)
                    last = three_(bank[tt][:, :], hh[:, j % 2, cols], hl[:, j % 2, cols],
                                  wh[:, par, 2, j, :], wl[:, par, 2, j, :], j == 0, j == KC - 1)
                last.then_inc(d_dn, 1)

            three_ = env["three"]

            def chunk(c, par, routed, nxt):
                with pe.Fori(0, BPC) as t:
                    n = c * BPC + t
                    tok = bass.ts(t, BLK)
                    for j in range(KC):
                        s = n * KC + j
                        pe.wait_ge(d_s, s + 1)
                        cols = slice(j * P, (j + 1) * P)
                        for k in range(KC):
                            last = three_(bank[GATE][:, :], wh[:, par, 0, k, cols], wl[:, par, 0, k, cols],
                                          XTh[:, k, tok], XTl[:, k, tok], k == 0, k == KC - 1)
                        last.then_inc(d_g, 1)
                        pe.wait_ge(d_hm, s + 1)
                        for k in range(KC):
                            last = three_(bank[UP][:, :], wh[:, par, 1, k, cols], wl[:, par, 1, k, cols],
                                          XTh[:, k, tok], XTl[:, k, tok], k == 0, k == KC - 1)
                        last.then_inc(d_u, 1)
                        if routed is not None and j % 2 == 0:
                            pe.wait_ge(d_h, s - NS * BPC * KC + 1)
                            nc.tensor.matmul(bank[BC][:, :], pick[:, 2 * routed + j // 2, :], combT[:, tok],
                                             start=True, stop=True).then_inc(d_bc, 1)
                        if nxt is not None and j < NU:
                            transposes(j, PRE + n * NU + j, dma_value(nxt, j, t))
                        if j:
                            down(j - 1, s - 1, n, par)
                    down(KC - 1, n * KC + KC - 1, n, par)

            def dma_value(c, k, t):
                if isinstance(c, tuple):
                    per = 2 if k < 2 else 1
                    return 16 * BPC * NS + 16 * per * (BPC * c[1] + t + 1)
                return 16 * (BPC * c + t + 1)

            with pe.Fori(0, BPC) as t:
                for k in range(NU):
                    transposes(k, NU * t + k, dma_value(0, k, t))
            plan(pe, chunk)

        @block.scalar
        def _(act):
            act.sem_inc(d_s, 1)

            def high(par, k, t, q):
                act.wait_ge(p_tr, q + 1 + NU)
                nc.scalar.activation(wh[:, par, k, t, :], bank[TR][:, :], ACT.Copy).then_inc(p_hi, 1)

            def chunk(c, par, routed, nxt):
                with act.Fori(0, BPC) as t:
                    n = c * BPC + t
                    for j in range(KC):
                        s = n * KC + j
                        act.wait_ge(d_g, s + 1)
                        act.wait_ge(d_hm, s + 1)
                        nc.scalar.activation(silu[:, :], bank[GATE][:, :], ACT.Silu).then_inc(d_s, 1)
                        if nxt is not None and j < NU:
                            high(1 - par, j, t, PRE + n * NU + j)
                        if routed is None:
                            act.wait_ge(d_hm, s + 2)
                        else:
                            act.wait_ge(d_h, s - NS * BPC * KC + 2)
                        act.wait_ge(d_dn, s + 1)
                        nc.scalar.activation(hh[:, j % 2, :], hid[:, j % 2, :], ACT.Copy).then_inc(d_hi, 1)

            with act.Fori(0, BPC) as t:
                for k in range(NU):
                    high(0, k, t, NU * t + k)
            plan(act, chunk)

        @block.vector
        def _(dve):
            dve.sem_inc(d_hm, 1)
            dve.sem_inc(d_accf, 1)
            dve.sem_inc(p_lo, 1)
            dve.sem_inc(d_h, 1)

            def low(par, k, t, q):
                dve.wait_ge(p_hi, q + 1)
                nc.vector.tensor_tensor(wl[:, par, k, t, :], bank[TR][:, :], wh[:, par, k, t, :],
                                        ALU.subtract).then_inc(p_lo, 1)

            def chunk(c, par, routed, nxt):
                with dve.Fori(0, BPC) as t:
                    n = c * BPC + t
                    for j in range(KC):
                        s = n * KC + j
                        dve.wait_ge(d_u, s + 1)
                        dve.wait_ge(d_s, s + 2)
                        nc.vector.tensor_tensor(hid[:, j % 2, :], silu[:, :], bank[UP][:, :],
                                                ALU.mult).then_inc(d_hm, 1)
                        if routed is not None:
                            dve.wait_ge(d_hm, s + 2)
                            if j % 2 == 0:
                                dve.wait_ge(d_bc, (n - NS * BPC) * 2 + j // 2 + 1)
                            nc.vector.tensor_tensor(hid[:, j % 2, :], hid[:, j % 2, :], bank[BC][:, :],
                                                    ALU.mult).then_inc(d_h, 1)
                        if nxt is not None and j < NU:
                            low(1 - par, j, t, PRE + n * NU + j)
                        dve.wait_ge(d_hi, s + 1)
                        nc.vector.tensor_tensor(hl[:, j % 2, :], hid[:, j % 2, :], hh[:, j % 2, :],
                                                ALU.subtract).then_inc(d_lo, 1)
                    dve.wait_ge(d_dn, (n + 1) * KC + 2)
                    for tt in range(TPB):
                        xt = X[:, t * TPB + tt, :]
                        last = nc.vector.scalar_tensor_tensor(out=xt, in0=bank[tt][:, :], scalar=tg[:, 3:4], in1=xt,
                                                              op0=ALU.mult, op1=ALU.add)
                    last.then_inc(d_accf, 1)

            with dve.Fori(0, BPC) as t:
                for k in range(NU):
                    low(0, k, t, NU * t + k)
            plan(dve, chunk)
    st.close()


_INS = ['x', 'ctx_2048', 'mask_SxS2_bc0', 'mask_BxS2_bk0', 'g_xattn', 'g_ffn', 'L0_xattn_Wq', 'L0_xattn_bq',
        'L0_xattn_Wk', 'L0_xattn_bk', 'L0_xattn_Wv', 'L0_xattn_bv', 'L0_xattn_Wo', 'L0_xattn_bo', 'L0_ffn_w_fc',
        'L0_ffn_w_proj', 'L1_xattn_Wq', 'L1_xattn_Wg', 'L1_xattn_bg', 'L1_xattn_Wkv', 'L1_xattn_Wo', 'L1_ffn_w12',
        'L1_ffn_w3', 'L1_ffn_router_w', 'L1_ffn_expert_bias', 'L1_ffn_sw1', 'L1_ffn_sw2', 'L1_ffn_sw3']
PHASES = "ABCD"


def kernel(**inputs):
    import numpy as _np
    import concourse.bacc as _bacc
    from concourse import mybir as _mybir
    from concourse.bass_utils import run_bass_kernel_spmd as _run

    nc = _bacc.Bacc("TRN2", target_bir_lowering=False, num_devices=1)
    arrays, args = {}, {}
    for name in _INS:
        v = _np.ascontiguousarray(inputs[name])
        arrays[f"in_{name}"] = v
        args[name] = nc.dram_tensor(f"in_{name}", v.shape, _mybir.dt.from_np(v.dtype), kind="ExternalInput").ap()
    out = nc.dram_tensor("out_x", (B, S, D), F32, kind="ExternalOutput").ap()
    flamingo(nc, args, out, PHASES)
    r = _run(nc, [arrays], core_ids=[0])
    return r.results[0]["out_x"]
```

```python
from contextlib import ExitStack

import concourse.bass as bass
from concourse import mybir

F32 = mybir.dt.float32
F16 = mybir.dt.float16
U8 = mybir.dt.uint8
ALU = mybir.AluOpType
ACT = mybir.ActivationFunctionType
AX_X = mybir.AxisListType.X

P = 128
B, S, D = 8, 256, 512
TILES = B * S // P
KC = D // P
MASKED = -60000.0

H0, G0, HD0 = 32, 8, 16
STK = 64
H1, HD1 = 16, 32
F0 = 2048
FS, E, FR = 2048, 8, 256
CH = 512
BLK = 512


class Chain:

    def __init__(self, eng, sem, base=0):
        self.eng, self.sem = eng, sem
        self.start(base)

    def start(self, base):
        self.base, self.n = base, 0

    def __call__(self, ins):
        self.n += 1
        ins.then_inc(self.sem, 1)
        self.eng.wait_ge(self.sem, self.base + self.n)


def flamingo(nc, a, out, phases="ABCD"):
    with ExitStack() as ctx:
        used = {}

        def sb(name, shape, dt=F32, stack=None):
            used[name] = used.get(name, 0) + 1
            name = name if used[name] == 1 else f"{name}_{used[name]}"
            return (stack or ctx).enter_context(nc.sbuf_tensor(name, shape, dt))

        phase_sems = []

        def sem(name):
            if not phase_sems:
                return ctx.enter_context(nc.semaphore(name))
            stack, held = phase_sems[-1]
            s = stack.enter_context(nc.semaphore(name))
            held.append(s)
            return s

        def phase(write):
            phase_sems.append((ExitStack(), []))
            write(nc, a, env)
            stack, held = phase_sems.pop()
            with nc.Block() as block:
                @block.gpsimd
                def _(pool):
                    for s in held:
                        pool.sem_clear(s)
            stack.close()

        bank = [ctx.enter_context(nc.psum_tensor(f"bank{i}", [P, 512], F32)) for i in range(8)]

        def bank16(i):
            return bank[i][:, :].bitcast(F16)

        X = sb("X", [P, TILES, D])
        XTh = sb("XTh", [P, KC, TILES * P], F16)
        XTl = sb("XTl", [P, KC, TILES * P], F16)
        ident = sb("ident", [P, P])
        ident16 = sb("ident16", [P, P], F16)
        gates = sb("gates", [P, 4])
        tg = sb("tg", [P, 4])

        x_tiles = a["x"].rearrange("b (t p) d -> p (b t) d", p=P)
        out_tiles = out.rearrange("b (t p) d -> p (b t) d", p=P)
        ctx_tiles = a["ctx_2048"].rearrange("b (t p) d -> p (b t) d", p=P)

        def row(ap):
            return ap.rearrange("(a n) -> a n", a=1).partition_broadcast(P) if len(ap.shape) == 1 else ap

        s_load = [sem(f"s_load{i}") for i in range(4)]
        s_g = sem("s_gates")
        s_id = sem("s_ident")
        with nc.Block() as block:
            @block.sync
            def _(sp):
                for i in range(4):
                    sp.dma_start(X[:, 4 * i:4 * i + 4, :], x_tiles[:, 4 * i:4 * i + 4, :]).then_inc(s_load[i], 16)
                sp.dma_start(gates[:, 0:2], row(a["g_xattn"])).then_inc(s_g, 16)
                sp.dma_start(gates[:, 2:4], row(a["g_ffn"])).then_inc(s_g, 16)
                for i in range(4):
                    sp.wait_ge(s_load[i], 16)

            @block.gpsimd
            def _(pool):
                nc.gpsimd.memset(ident[:, :], 0.0).then_inc(s_id, 1)
                nc.gpsimd.memset(ident16[:, :], 0.0).then_inc(s_id, 1)
                pool.wait_ge(s_id, 2)
                for m in (ident, ident16):
                    nc.gpsimd.affine_select(out=m[:, :], in_=m[:, :], compare_op=ALU.not_equal, fill=1.0,
                                            base=0, pattern=[[-1, P]], channel_multiplier=1).then_inc(s_id, 1)

            @block.scalar
            def _(act):
                act.wait_ge(s_g, 32)
                nc.scalar.activation(tg[:, :], gates[:, :], ACT.Tanh)

        f_chain, f_pchain = sem("f_chain"), sem("f_pchain")
        f_var, f_rstd, f_nm, f_nrm, f_q, f_tr, f_hi, f_lo = (sem("f_" + n) for n in (
            "var", "rstd", "nmean", "normed", "quant", "tr", "hi", "lo"))
        FT = 4
        f_in = [sem(f"f_in{p}") for p in range(FT)]
        w_in, w_tr, w_hi, w_lo = (sem("w_" + n) for n in ("in", "tr", "hi", "lo"))
        f_base = {"w": 0, "tile": 0, "norm": 0, "nrm": 0, "chain": 0, "front": 1}

        def front(kind, dsth, dstl, load=None, beside=None, weights=()):
            st = ExitStack()
            NW = len(weights)
            rows = [w.shape[0] // P for w, hi, lo in weights]
            wst = sb("f_w", [P, sum(rows), P], stack=st) if NW else None
            WB = 4
            xn = sb("f_x", [P, FT, D], stack=st)
            stats = sb("f_stats", [P, FT, 6], stack=st)
            mv = sb("f_mv", [P, FT, 2], stack=st)
            ve = sb("f_ve", [P, 2, FT], stack=st)
            rstd = sb("f_r", [P, 2, FT], stack=st)
            nmean = sb("f_nm", [P, 2, FT], stack=st)
            hold = sb("f_hold", [P, 1], stack=st)
            mhalf = sb("f_mh", [P, FT], stack=st)
            q = sb("f_q", [P, 4 * FT], stack=st)
            at = dict(f_base)
            norms = {"ln": 1, "bit": 2, "ctx": 0}[kind]
            per = {"ln": 2, "bit": 4 + 4 + FT, "ctx": 0}[kind]

            def transposed(g):
                return bank[WB + g % 4][:, 0:rows[g] * P].rearrange("p (o c) -> p o c", o=1)

            with nc.Block() as block:
                @block.sync
                def _(sp):
                    if kind == "ctx":
                        for i in range(TILES):
                            sp.wait_ge(f_tr, at["tile"] + i + 1)
                            sp.dma_start(xn[:, i % FT, :], ctx_tiles[:, i, :]).then_inc(f_in[i % FT], 16)
                    if load:
                        load(sp)
                    for k in range(KC if NW else 0):
                        if k:
                            sp.wait_ge(w_tr, at["w"] + NW * k)
                        for g, (w, hi, lo) in enumerate(weights):
                            r0 = sum(rows[:g])
                            sp.dma_start(wst[:, r0:r0 + rows[g], :],
                                         w[:, k * P:(k + 1) * P].rearrange("(r p) c -> p r c", p=P)).then_inc(w_in, 16)

                @block.gpsimd
                def _(pool):
                    if norms:
                        nc.gpsimd.memset(mhalf[:, :], -0.5).then_inc(f_pchain, 1)
                        pool.wait_ge(f_pchain, at["front"])
                        with pool.Fori(0, TILES // FT) as i:
                            for v in range(norms):
                                pool.wait_ge(f_var, at["norm"] + norms * i + v + 1)
                                nc.gpsimd.tensor_tensor(rstd[:, v, :], ve[:, v, :], mhalf[:, :],
                                                        ALU.pow).then_inc(f_rstd, 1)

                @block.tensor
                def _(pe):
                    if at["tile"] == 0:
                        pe.sem_inc(f_tr, FT)
                    with pe.Fori(0, TILES // FT) as i:
                        if NW:
                            pe.wait_ge(w_in, 16 * (at["w"] + NW * i + NW))
                        for g in range(NW):
                            pe.wait_ge(w_lo, at["w"] + NW * i + max(0, g - 3) + 1)
                            for r in range(rows[g]):
                                last = nc.tensor.transpose(bank[WB + g % 4][:, r * P:(r + 1) * P],
                                                           wst[:, sum(rows[:g]) + r, :], ident[:, :])
                            last.then_inc(w_tr, 1)
                        for p in range(FT):
                            n = at["tile"] + FT * i + p
                            if kind == "ctx":
                                pe.wait_ge(f_in[p], 16 * i + 16)
                            elif kind == "ln":
                                pe.wait_ge(f_nrm, at["nrm"] + FT * i + p + 1)
                            else:
                                pe.wait_ge(f_q, FT * i + p + 1)
                            pe.wait_ge(f_lo, n + 1)
                            for k in range(KC):
                                last = nc.tensor.transpose(bank[p][:, k * P:(k + 1) * P],
                                                           xn[:, p, k * P:(k + 1) * P], ident[:, :])
                            last.then_inc(f_tr, 1)

                @block.scalar
                def _(act):
                    with act.Fori(0, TILES // FT) as i:
                        for v in range(norms):
                            act.wait_ge(f_nm, at["norm"] + norms * i + v + 1)
                            for p in range(FT):
                                if v == 0:
                                    act.wait_ge(f_tr, at["tile"] + FT * i + p + 1)
                                nc.scalar.activation(xn[:, p, :], X[:, FT * i + p, :] if v == 0 else xn[:, p, :],
                                                     ACT.Identity, bias=nmean[:, v, p:p + 1],
                                                     scale=rstd[:, v, p:p + 1]).then_inc(f_nrm, 1)
                        if beside:
                            beside(act, i)
                        for g, (w, hi, lo) in enumerate(weights):
                            act.wait_ge(w_tr, at["w"] + NW * i + g + 1)
                            nc.scalar.activation(hi[:, bass.ds(i, 1), :], transposed(g), ACT.Copy).then_inc(w_hi, 1)
                        for p in range(FT):
                            act.wait_ge(f_tr, at["tile"] + FT * i + p + 1 + FT)
                            nc.scalar.activation(dsth[:, :, bass.ts(FT * i + p, P)],
                                                 bank[p][:, :].rearrange("p (k c) -> p k c", k=KC),
                                                 ACT.Copy).then_inc(f_hi, 1)

                @block.vector
                def _(dve):
                    if at["tile"] == 0:
                        dve.sem_inc(f_lo, FT)
                        dve.sem_inc(w_lo, 1)
                    with dve.Fori(0, TILES // FT) as i:
                        link = Chain(dve, f_chain, at["chain"] + per * i)
                        for v in range(norms):
                            for p in range(FT):
                                if v == 1:
                                    dve.wait_ge(f_nrm, at["nrm"] + norms * FT * i + p + 1)
                                last = nc.vector.bn_stats(stats[:, p, :], X[:, FT * i + p, :] if v == 0 else xn[:, p, :])
                            link(last)
                            nc.vector.memset(hold[:, :], 0.0)
                            for p in range(FT):
                                last = nc.vector.bn_aggr(mv[:, p, :], stats[:, p, :])
                            link(last)
                            nc.vector.tensor_scalar(ve[:, v, :], mv[:, :, 1], (1e-5, 1e-6)[v], None,
                                                    ALU.add).then_inc(f_var, 1)
                            dve.wait_ge(f_rstd, at["norm"] + norms * i + v + 1)
                            nc.vector.scalar_tensor_tensor(out=nmean[:, v, :], in0=mv[:, :, 0], scalar=-1.0,
                                                           in1=rstd[:, v, :], op0=ALU.mult,
                                                           op1=ALU.mult).then_inc(f_nm, 1)
                        for g, (w, hi, lo) in enumerate(weights):
                            dve.wait_ge(w_hi, at["w"] + NW * i + g + 1)
                            nc.vector.tensor_tensor(lo[:, bass.ds(i, 1), :], transposed(g), hi[:, bass.ds(i, 1), :],
                                                    ALU.subtract).then_inc(w_lo, 1)
                        if kind == "bit":
                            for p, ins in enumerate(quantise(
                                    link, [xn[:, p, :] for p in range(FT)], q,
                                    lambda p: dve.wait_ge(f_nrm, at["nrm"] + norms * FT * i + FT + p + 1))):
                                ins.then_inc(f_q, 1)
                        for p in range(FT):
                            dve.wait_ge(f_hi, at["tile"] + FT * i + p + 1)
                            cols = bass.ts(FT * i + p, P)
                            nc.vector.tensor_tensor(dstl[:, :, cols],
                                                    bank[p][:, :].rearrange("p (k c) -> p k c", k=KC),
                                                    dsth[:, :, cols], ALU.subtract).then_inc(f_lo, 1)
                        assert link.n == per, link.n
            f_base["w"] += NW * KC
            f_base["tile"] += TILES
            if norms:
                f_base["front"] += 1
            f_base["norm"] += norms * TILES // FT
            f_base["nrm"] += norms * TILES
            f_base["chain"] += per * (TILES // FT)
            st.close()

        def quantise(link, xs, q, ready=lambda p: None):
            n = len(xs)
            g, r, up, down = (q[:, k * n:(k + 1) * n] for k in range(4))
            for p, x in enumerate(xs):
                ready(p)
                last = nc.vector.tensor_reduce(g[:, p:p + 1], x, AX_X, ALU.max, apply_absolute_value=True)
            link(last)
            link(nc.vector.reciprocal(r, g))
            link(nc.vector.tensor_scalar(up, r, 128.0, None, ALU.mult))
            link(nc.vector.tensor_scalar(down, g, 1.0 / 128.0, None, ALU.mult))
            for p, x in enumerate(xs):
                link(nc.vector.tensor_scalar(x, x, up[:, p:p + 1], 128.0 - 1e-6, ALU.mult, ALU.min))
                yield nc.vector.tensor_scalar(x, x, 1e-6 - 128.0, down[:, p:p + 1], ALU.max, ALU.mult)

        def three(out_ap, lhi, llo, rhi, rlo, first, last_one):
            nc.tensor.matmul(out_ap, lhi, rhi, start=first, stop=False)
            nc.tensor.matmul(out_ap, lhi, rlo, start=False, stop=False)
            return nc.tensor.matmul(out_ap, llo, rhi, start=False, stop=last_one)

        cst = ExitStack()
        if "A" in phases or "C" in phases:
            CTh = sb("CTh", [P, KC, TILES * P], F16, stack=cst)
            CTl = sb("CTl", [P, KC, TILES * P], F16, stack=cst)
            front("ctx", CTh, CTl)
        env = dict(locals())
        if "A" in phases:
            phase(phase_a)
        if "B" in phases:
            phase(phase_b)
        if "C" in phases:
            phase(phase_c)
        cst.close()
        if "D" in phases:
            phase(phase_d)

        s_out = sem("s_out")
        with nc.Block() as block:
            @block.sync
            def _(sp):
                sp.dma_start(out_tiles, X[:, :, :]).then_inc(s_out, 16)
                sp.wait_ge(s_out, 16)


def phase_a(nc, a, env):
    sem, bank, bank16, X, XTh, XTl, ident, ident16, tg = (env[k] for k in (
        "sem", "bank", "bank16", "X", "XTh", "XTl", "ident", "ident16", "tg"))
    st = ExitStack()

    def sb(name, shape, dt=F32):
        return env["sb"](name, shape, dt, stack=st)

    CTh, CTl = env["CTh"], env["CTl"]
    KV = G0 * HD0
    NEG, ONE = 3 * HD0, 3 * HD0 + 1
    wqh = sb("a_wqh", [P, KC, D], F16)
    wql = sb("a_wql", [P, KC, D], F16)
    woh = sb("a_woh", [P, KC, D], F16)
    wol = sb("a_wol", [P, KC, D], F16)
    wkvh = sb("a_wkvh", [P, KC, 2 * KV], F16)
    wkvl = sb("a_wkvl", [P, KC, 2 * KV], F16)
    env["front"]("ln", XTh, XTl, weights=[
        (a["L0_xattn_Wq"], wqh, wql), (a["L0_xattn_Wo"], woh, wol),
        (a["L0_xattn_Wk"], wkvh[:, :, 0:KV], wkvl[:, :, 0:KV]),
        (a["L0_xattn_Wv"], wkvh[:, :, KV:2 * KV], wkvl[:, :, KV:2 * KV])])

    bq = sb("a_bq", [P, D])
    bkv = sb("a_bkv", [P, 2 * KV])
    bo = sb("a_bo", [P, D])
    m8 = sb("a_m8", [P, 2, S], U8)
    pad8 = sb("a_pad8", [B, S], U8)
    padf = sb("a_padf", [B, S])
    madd = sb("a_madd", [P, 2, S], F16)
    maddT = sb("a_maddT", [P, 2, S], F16)
    pad = sb("a_pad", [P, 2, B])
    q32 = sb("a_q32", [P, 2, D])
    qs = sb("a_qs", [P, 2, H0, STK], F16)
    qT = sb("a_qT", [P, 2, H0 // 2, S], F16)
    k32 = sb("a_k32", [P, 2, KV])
    ks = sb("a_ks", [P, 2, G0, 4, STK], F16)
    kd = ks[:, :, :, 0:4:3, :]
    kT = sb("a_kT", [P, 2, 2 * G0, S], F16)
    v32 = sb("a_v32", [P, 2, KV])
    VW = 2 * HD0 + 1
    vv = sb("a_v", [P, 2, 2, G0, VW], F16)
    mx = sb("a_mx", [P, 2, H0])
    NP = 4
    prob = sb("a_prob", [P, 2, D])
    ph = sb("a_ph", [P, NP, D], F16)
    pl = sb("a_pl", [P, NP, D], F16)
    rec = sb("a_rec", [P, 2, 8])
    oa = sb("a_oa", [P, 2, 8, HD0])
    ob = sb("a_ob", [P, 2, 8, HD0])
    on = sb("a_on", [P, 2, D])
    oTh = sb("a_oTh", [P, 2, KC, P], F16)
    oTl = sb("a_oTl", [P, 2, KC, P], F16)

    k_in, k_ch, k_pad, k_tr, k_m = (sem("k_" + n) for n in ("in", "chain", "pad", "tr", "mask"))
    with nc.Block() as block:
        @block.sync
        def _(sp):
            sp.dma_start(bq[:, :], env["row"](a["L0_xattn_bq"])).then_inc(k_in, 16)
            sp.dma_start(bkv[:, 0:KV], env["row"](a["L0_xattn_bk"])).then_inc(k_in, 16)
            sp.dma_start(bkv[:, KV:2 * KV], env["row"](a["L0_xattn_bv"])).then_inc(k_in, 16)
            sp.dma_start(bo[:, :], env["row"](a["L0_xattn_bo"])).then_inc(k_in, 16)
            sp.dma_start(m8[:, :, :], a["mask_SxS2_bc0"].rearrange("(t p) k -> p t k", p=P)).then_inc(k_in, 16)
            sp.dma_start(pad8[:, :], a["mask_BxS2_bk0"]).then_inc(k_in, 16)

        @block.vector
        def _(dve):
            link = Chain(dve, k_ch)
            nc.vector.memset(qs[:, :, :, :], 0.0)
            nc.vector.memset(ks[:, :, :, :, :], 0.0)
            link(nc.vector.memset(mx[:, :, :], 0.0))
            nc.vector.memset(qs[:, :, :, ONE:ONE + 1], 1.0)
            nc.vector.memset(kd[:, :, :, :, NEG:NEG + 1], 1.0)
            nc.vector.memset(vv[:, :, :, :, HD0:HD0 + 1], 1.0)
            dve.wait_ge(k_in, 96)
            link(nc.vector.tensor_scalar(bq[:, :], bq[:, :], HD0 ** -0.5, None, ALU.mult))
            nc.vector.tensor_scalar(padf[:, :], pad8[:, :], MASKED, None, ALU.mult).then_inc(k_pad, 1)
            nc.vector.tensor_scalar(madd[:, :, :], m8[:, :, :], MASKED, None, ALU.mult).then_inc(k_m, 1)
            dve.wait_ge(k_tr, 1)
            link(nc.vector.tensor_copy(pad[:, :, :], bank[0][:, 0:2 * B].rearrange("p (t b) -> p t b", t=2)))
            dve.wait_ge(k_tr, 2)
            link(nc.vector.tensor_copy(maddT[:, :, :], bank16(1)[:, 0:2 * S].rearrange("p (t q) -> p t q", t=2)))

        @block.tensor
        def _(pe):
            pe.wait_ge(k_pad, 1)
            for t in range(2):
                last = nc.tensor.transpose(bank[0][:, t * B:(t + 1) * B], padf[:, t * P:(t + 1) * P], ident[0:B, 0:B])
            last.then_inc(k_tr, 1)
            pe.wait_ge(k_m, 1)
            for k in range(2):
                for t in range(2):
                    last = nc.tensor.transpose(bank16(1)[:, k * S + t * P:k * S + (t + 1) * P],
                                               madd[:, t, k * P:(k + 1) * P], ident16[:, :])
            last.then_inc(k_tr, 1)

    names = ("Q0", "Q1", "KV0", "KV1", "dq0", "dq1", "dk0", "dk1", "hq0", "hq1", "lq0", "lq1", "hk0", "hk1",
             "lk0", "lk1", "hv0", "hv1", "lv0", "lv1", "tq", "t2", "tk", "cq", "ck", "c2", "S", "M", "nm0", "nm1",
             "ST", "E", "L", "AV", "ON", "To0", "To1", "hO0", "hO1", "lO0", "lO1", "O0", "O1", "x0", "x1", "ch")
    ev = {n: sem("a_" + n) for n in names}
    NS = 2 * G0 * 2
    LAG = 3
    BST, BAV, BS, BM = 0, 2, 4, 6
    PQ, PK = (0, 4), (2, 6)
    TQ, TK = (8, 10), (9, 11)
    FIRST = 12
    NORM = LAG + 4

    def due(n):
        if not FIRST <= n < NS:
            return range(0)
        return range((n - FIRST) * NS // (NS - FIRST), (n + 1 - FIRST) * NS // (NS - FIRST))
    HALF = next(n for n in range(NS) if due(n).stop >= NS // 2 + 3)

    def rounds(eng, first, body):
        first()
        with eng.Fori(0, B // 2 - 1) as i:
            body(2 * i, 0, True)
            body(2 * i + 1, 1, True)
        body(B - 2, 0, True)
        body(B - 1, 1, False)

    with nc.Block() as block:
        @block.tensor
        def _(pe):
            pe.sem_inc(ev["AV"], 4)

            def wait(n, b, count=1, per=1):
                pe.wait_ge(ev[n], b * per + count)

            def project(dst, xh, xl, w_h, w_l, b, tt, n):
                x = bass.ds((2 * b + tt) * P, P)
                for k in range(KC):
                    last = env["three"](dst, xh[:, k, x], xl[:, k, x], w_h[:, k, :], w_l[:, k, :],
                                        k == 0, k == KC - 1)
                last.then_inc(ev[n], 1)

            def q_of(b, tt):
                wait("dq0" if tt else "x0", b, 1)
                project(bank[BM][:, :], XTh, XTl, wqh, wql, b, tt, f"Q{tt}")

            def kv_of(b, tt):
                wait("dk0" if tt else "x1", b, 1)
                project(bank[BM + 1][:, 0:2 * KV], CTh, CTl, wkvh, wkvl, b, tt, f"KV{tt}")

            def turn_q(b, tt, n):
                for h in range(2):
                    if n == "tq":
                        if tt:
                            wait("ck", b, h + 1, 4)
                        else:
                            wait(("dq1", "dk1")[h], b)
                    elif tt:
                        wait("c2", b, h + 1, 4)
                    else:
                        wait("ck", b, h + 3, 4)
                    for j in range(8):
                        c = qs[:, tt, 16 * h + 2 * j:16 * h + 2 * j + 2, :].rearrange("p h c -> p (h c)")
                        last = nc.tensor.transpose(bank16(BM + h)[:, j * P:(j + 1) * P], c, ident16[:, :])
                    last.then_inc(ev[n], 1)

            def turn_k(b, tt):
                wait(f"lk{tt}", b)
                for h in range(2):
                    wait("cq", b, 2 * tt + h + 1, 4)
                    for j in range(8):
                        c = ks[:, tt, 4 * h + j // 2, 2 * (j % 2):2 * (j % 2) + 2, :].rearrange("p d c -> p (d c)")
                        last = nc.tensor.transpose(bank16(BM + h)[:, j * P:(j + 1) * P], c, ident16[:, :])
                    last.then_inc(ev["tk"], 1)

            def scores(b, par, m):
                tt, g, half = m // 16, m // 2 % G0, m % 2
                bk = bank[BS + m % 2]
                wait("M", b, m + 1, NS)
                if m == 0:
                    wait("ck", b, 4, 4)
                    wait("cq", b, 4, 4)
                nc.tensor.matmul(bk[:, :].rearrange("p (r k) -> p r k", r=2), ident16[:, :],
                                 madd[:, tt, :].unsqueeze(1).broadcast_to([P, 2, S]), start=True, stop=False)
                for r in range(2):
                    last = nc.tensor.matmul(bk[:, r * S:(r + 1) * S], qT[:, par, 2 * g + r, tt * P:(tt + 1) * P],
                                            kT[:, par, 2 * g + half, :], start=False, stop=(r == 1))
                last.then_inc(ev["S"], 1)

            def second(b, tt):
                wait(f"nm{tt}", b)
                turn_q(b, tt, "t2")

            def turned_scores(b, par, n):
                g, half, kc = n // 4, n // 2 % 2, n % 2
                bk = bank[BST + n % 2]
                wait("E", b, n + 1, NS)
                nc.tensor.matmul(bk[:, :].rearrange("p (r k) -> p r k", r=2), ident16[:, :],
                                 maddT[:, kc, :].unsqueeze(1).broadcast_to([P, 2, S]), start=True, stop=False)
                nc.tensor.matmul(bk[:, :], kT[:, par, 2 * g + half, kc * P:(kc + 1) * P],
                                 qT[:, par, 2 * g:2 * g + 2, :].rearrange("p r q -> p (r q)"),
                                 start=False, stop=True).then_inc(ev["ST"], 1)

            def times_v(b, par, n):
                g, half, kc = n // 4, n // 2 % 2, n % 2
                if n % 4 == 0:
                    wait("ON", b, g + 1, G0)
                wait("L", b, n + 3, NS)
                for r in range(2):
                    for qt in range(2):
                        c = ((qt * 2 + r) * 2 + half) * VW
                        q = slice((2 * r + qt) * P, (2 * r + qt + 1) * P)
                        first = n % 4 == 0 and r == 0 and qt == 0
                        nc.tensor.matmul(bank[BAV + g % 2][:, c:c + VW], ph[:, n % NP, q], vv[:, par, kc, g, :],
                                         start=first, stop=False, skip_group_check=True)
                        last = nc.tensor.matmul(bank[BAV + g % 2][:, c:c + HD0 + 1], pl[:, n % NP, q],
                                                vv[:, par, kc, g, 0:HD0 + 1], start=False, stop=(kc == 1),
                                                skip_group_check=True)
                last.then_inc(ev["AV"], 1)

            def output(b):
                wait("ch", b, 2 * G0, 2 * G0)
                for tt in range(2):
                    for k in range(KC):
                        last = nc.tensor.transpose(bank[BM + tt][:, k * P:(k + 1) * P], on[:, tt, k * P:(k + 1) * P],
                                                   ident[:, :])
                    last.then_inc(ev[f"To{tt}"], 1)
                for tt in range(2):
                    wait(f"lO{tt}", b)
                    for k in range(KC):
                        last = env["three"](bank[BM + tt][:, :], oTh[:, tt, k, :], oTl[:, tt, k, :],
                                            woh[:, k, :], wol[:, k, :], k == 0, k == KC - 1)
                    last.then_inc(ev[f"O{tt}"], 1)

            def first():
                for tt in range(2):
                    q_of(0, tt)
                    kv_of(0, tt)
                for tt in range(2):
                    wait(f"lq{tt}", 0)
                    turn_q(0, tt, "tq")
                    turn_k(0, tt)
                for m in range(NS):
                    scores(0, 0, m)
                second(0, 0)
                second(0, 1)

            def body(b, par, more):
                nx = b + 1
                wait("c2", b, 4, 4)
                wait("lv0", b)
                wait("lv1", b)
                for n in range(NS + LAG):
                    if n < NS:
                        turned_scores(b, par, n)
                    if n >= LAG:
                        times_v(b, par, n - LAG)
                    if not more:
                        continue
                    for tt in range(2):
                        if n == PQ[tt]:
                            q_of(nx, tt)
                        if n == PK[tt]:
                            kv_of(nx, tt)
                        if n == TQ[tt]:
                            wait(f"lq{tt}", nx)
                            turn_q(nx, tt, "tq")
                        if n == TK[tt]:
                            turn_k(nx, tt)
                    for m in due(n - 1):
                        scores(nx, 1 - par, m)
                    if n == HALF:
                        second(nx, 0)
                if more:
                    second(nx, 1)
                    wait("c2", nx, 4, 4)
                output(b)
            rounds(pe, first, body)

        @block.scalar
        def _(act):
            act.sem_inc(ev["E"], 2)

            def wait(n, b, count=1, per=1):
                act.wait_ge(ev[n], b * per + count)

            def high_q(b, tt):
                wait(f"dq{tt}", b)
                q3 = q32[:, tt, :].rearrange("p (h c) -> p h c", h=H0)
                nc.scalar.activation(qs[:, tt, :, 0:HD0], q3, ACT.Copy)
                nc.scalar.activation(qs[:, tt, :, HD0:2 * HD0], q3, ACT.Copy).then_inc(ev[f"hq{tt}"], 1)

            def high_kv(b, par, tt):
                wait(f"dk{tt}", b)
                k4 = k32[:, tt, :].rearrange("p (g c) -> p g c", g=G0).unsqueeze(2).broadcast_to([P, G0, 2, HD0])
                nc.scalar.activation(vv[:, par, tt, :, 0:HD0], v32[:, tt, :].rearrange("p (g c) -> p g c", g=G0),
                                     ACT.Copy).then_inc(ev[f"hv{tt}"], 1)
                nc.scalar.activation(kd[:, tt, :, :, 0:HD0], k4, ACT.Copy)
                nc.scalar.activation(kd[:, tt, :, :, 2 * HD0:3 * HD0], k4, ACT.Copy).then_inc(ev[f"hk{tt}"], 1)

            def take_second(b, par, tt):
                for h in range(2):
                    wait("t2", b, 2 * tt + h + 1, 4)
                    nc.scalar.activation(qT[:, par, 8 * h:8 * h + 8, tt * P:(tt + 1) * P],
                                         bank16(BM + h).rearrange("p (j q) -> p j q", j=8), ACT.Copy)\
                      .then_inc(ev["c2"], 1)

            def first():
                for tt in range(2):
                    high_q(0, tt)
                    high_kv(0, 0, tt)
                take_second(0, 0, 0)
                take_second(0, 0, 1)

            def body(b, par, more):
                for n in range(NS):
                    wait("ST", b, n + 1, NS)
                    wait("AV", b, n + 1, NS)
                    wait("L", b, n + 1, NS)
                    nc.scalar.activation(ph[:, n % NP, :], bank[BST + n % 2][:, :], ACT.Exp)
                    nc.scalar.activation(prob[:, n % 2, :], bank[BST + n % 2][:, :], ACT.Exp).then_inc(ev["E"], 1)
                    if not more:
                        continue
                    for tt in range(2):
                        if n == PQ[tt] + 2:
                            high_q(b + 1, tt)
                        if n == PK[tt] + 2:
                            high_kv(b + 1, 1 - par, tt)
                    if n == min(HALF + 1, NS - 1):
                        take_second(b + 1, 1 - par, 0)
                if more:
                    take_second(b + 1, 1 - par, 1)
                for tt in range(2):
                    wait(f"To{tt}", b)
                    nc.scalar.activation(oTh[:, tt], bank[BM + tt][:, :].rearrange("p (k c) -> p k c", k=KC), ACT.Copy)\
                      .then_inc(ev[f"hO{tt}"], 1)
            rounds(act, first, body)

        @block.gpsimd
        def _(pool):
            pool.sem_inc(ev["L"], 2)

            def body(b, par, more):
                for n in range(NS):
                    pool.wait_ge(ev["E"], b * NS + n + 3)
                    nc.gpsimd.tensor_tensor(pl[:, n % NP, :], prob[:, n % 2, :], ph[:, n % NP, :],
                                            ALU.subtract).then_inc(ev["L"], 1)
            rounds(pool, lambda: None, body)

        @block.vector
        def _(dve):
            for n, credit in (("ON", 2), ("x0", 2), ("x1", 2), ("M", 2)):
                dve.sem_inc(ev[n], credit)

            def wait(n, b, count=1, per=1):
                dve.wait_ge(ev[n], b * per + count)

            PER = 2 * G0

            def bias_q(b, tt):
                wait(f"Q{tt}", b)
                nc.vector.memset(qs[:, tt, :, NEG:NEG + 1], 0.0)
                nc.vector.scalar_tensor_tensor(out=q32[:, tt, :], in0=bank[BM][:, :], scalar=HD0 ** -0.5,
                                               in1=bq[:, :], op0=ALU.mult, op1=ALU.add).then_inc(ev[f"dq{tt}"], 1)

            def bias_kv(b, tt):
                wait(f"KV{tt}", b)
                nc.vector.tensor_copy(kd[:, tt, :, :, ONE],
                                      pad[:, tt, bass.ds(b, 1)].unsqueeze(1).broadcast_to([P, G0, 2]))
                nc.vector.tensor_tensor(v32[:, tt, :], bank[BM + 1][:, KV:2 * KV], bkv[:, KV:2 * KV], ALU.add)
                nc.vector.tensor_tensor(k32[:, tt, :], bank[BM + 1][:, 0:KV], bkv[:, 0:KV],
                                        ALU.add).then_inc(ev[f"dk{tt}"], 1)

            def low_q(b, tt):
                wait(f"hq{tt}", b)
                nc.vector.tensor_tensor(qs[:, tt, :, 2 * HD0:3 * HD0],
                                        q32[:, tt, :].rearrange("p (h c) -> p h c", h=H0),
                                        qs[:, tt, :, 0:HD0], ALU.subtract).then_inc(ev[f"lq{tt}"], 1)

            def low_kv(b, par, tt):
                wait(f"hk{tt}", b)
                k4 = k32[:, tt, :].rearrange("p (g c) -> p g c", g=G0).unsqueeze(2).broadcast_to([P, G0, 2, HD0])
                nc.vector.tensor_tensor(kd[:, tt, :, :, HD0:2 * HD0], k4, kd[:, tt, :, :, 0:HD0],
                                        ALU.subtract).then_inc(ev[f"lk{tt}"], 1)
                wait(f"hv{tt}", b)
                nc.vector.tensor_tensor(vv[:, par, tt, :, HD0 + 1:VW], v32[:, tt, :].rearrange("p (g c) -> p g c", g=G0),
                                        vv[:, par, tt, :, 0:HD0], ALU.subtract).then_inc(ev[f"lv{tt}"], 1)

            def take(b, par, tt, what):
                dst, n, c = (qT, "tq", "cq") if what == "q" else (kT, "tk", "ck")
                for h in range(2):
                    wait(n, b, 2 * tt + h + 1, 4)
                    nc.vector.tensor_copy(dst[:, par, 8 * h:8 * h + 8, tt * P:(tt + 1) * P],
                                          bank16(BM + h).rearrange("p (j q) -> p j q", j=8)).then_inc(ev[c], 1)

            def maxima(b, m):
                tt, g, half = m // 16, m // 2 % G0, m % 2
                wait("S", b, m + 1, NS)
                nc.vector.tensor_reduce(mx[:, tt, 4 * g + half:4 * g + half + 3:2],
                                        bank[BS + m % 2][:, :].rearrange("p (r k) -> p r k", r=2), AX_X, ALU.max)\
                  .then_inc(ev["M"], 1)
                if m % 16 == 15:
                    wait("M", b, m + 3, NS)
                    nc.vector.tensor_scalar(qs[:, tt, :, NEG], mx[:, tt, :], -1.0, None, ALU.mult)\
                      .then_inc(ev[f"nm{tt}"], 1)

            def normalise(link, b, g):
                wait("AV", b, 4 * g + 4 + NP, NS)
                o = bank[BAV + g % 2][:, 0:8 * VW].rearrange("p (s c) -> p s c", s=8)
                nc.vector.reciprocal(rec[:, g % 2, :], o[:, :, HD0])
                link(nc.vector.tensor_copy(oa[:, g % 2], o[:, :, HD0 + 1:VW]))
                nc.vector.tensor_tensor(ob[:, g % 2], o[:, :, 0:HD0], oa[:, g % 2], ALU.add).then_inc(ev["ON"], 1)
                wait("ON", b, g + 3, G0)
                link(nc.vector.tensor_tensor(on[:, :, g * 4 * HD0:(g + 1) * 4 * HD0].rearrange(
                    "p t (h c) -> p t h c", h=4), ob[:, g % 2].rearrange("p (t h) c -> p t h c", t=2),
                    rec[:, g % 2, :].rearrange("p (t h) -> p t h", t=2).unsqueeze(3)
                    .broadcast_to([P, 2, 4, HD0]), ALU.mult))

            def first():
                for tt in range(2):
                    bias_q(0, tt)
                    bias_kv(0, tt)
                    low_q(0, tt)
                    low_kv(0, 0, tt)
                for tt in range(2):
                    take(0, 0, tt, "q")
                    take(0, 0, tt, "k")
                for m in range(NS):
                    maxima(0, m)

            def body(b, par, more):
                link = Chain(dve, ev["ch"], b * PER)
                nx = b + 1
                for n in range(NS):
                    if n >= NORM and (n - NORM) % 4 == 0:
                        normalise(link, b, (n - NORM) // 4)
                    if not more:
                        continue
                    for tt in range(2):
                        if n == PQ[tt]:
                            bias_q(nx, tt)
                        if n == PK[tt]:
                            low_q(nx, tt)
                            bias_kv(nx, tt)
                        if n == PK[tt] + 2:
                            low_kv(nx, 1 - par, tt)
                    for tt in range(2):
                        if n == TQ[tt]:
                            take(nx, 1 - par, tt, "q")
                        if n == TK[tt]:
                            take(nx, 1 - par, tt, "k")
                    for m in due(n):
                        maxima(nx, m)
                normalise(link, b, G0 - 1)
                for tt in range(2):
                    wait(f"hO{tt}", b)
                    nc.vector.tensor_tensor(oTl[:, tt], bank[BM + tt][:, :].rearrange("p (k c) -> p k c", k=KC),
                                            oTh[:, tt], ALU.subtract).then_inc(ev[f"lO{tt}"], 1)
                for tt in range(2):
                    wait(f"O{tt}", b)
                    nc.vector.tensor_tensor(on[:, tt, :], bank[BM + tt][:, :], bo[:, :], ALU.add)\
                      .then_inc(ev[f"x{tt}"], 1)
                    wait(f"x{tt}", b, 3)
                    nc.vector.scalar_tensor_tensor(out=X[:, 2 * b + tt, :], in0=on[:, tt, :], scalar=tg[:, 0:1],
                                                   in1=X[:, 2 * b + tt, :], op0=ALU.mult, op1=ALU.add)
                assert link.n == PER, link.n
            rounds(dve, first, body)
    st.close()


def phase_b(nc, a, env):
    sem, bank, bank16, X, XTh, XTl, ident, ident16, tg = (env[k] for k in (
        "sem", "bank", "bank16", "X", "XTh", "XTl", "ident", "ident16", "tg"))
    st = ExitStack()

    def sb(name, shape, dt=F32):
        return env["sb"](name, shape, dt, stack=st)

    NH = F0 // D
    HC = F0 // P
    wfc = sb("b_wfc", [P, NH, KC, D], F16)
    wpj = sb("b_wpj", [P, HC, D], F16)
    scale = sb("b_scale", [P, 8])

    wst = ExitStack()

    def wb(name, shape, dt=F32):
        return env["sb"](name, shape, dt, stack=wst)

    NUNIT = 2 * NH
    stage = wb("b_stage", [P, NUNIT, 4, D])
    part = wb("b_part", [P, NUNIT])
    sums = wb("b_sums", [P, 2])
    ones = wb("b_ones", [P, P])
    t_in, t_abs, t_ch, t_part, t_tot, t_low, t_use, t_tr, t_cp = (sem("t_" + n) for n in (
        "in", "abs", "ch", "part", "tot", "below", "use", "tr", "cp"))
    jst = ExitStack()
    junk = env["sb"]("b_junk", [P, 4 * D], F16, stack=jst)
    PER = NUNIT // (TILES // env["FT"])

    def unit(u):
        if u < NH:
            return a["L0_ffn_w_fc"][u * D:(u + 1) * D, :].rearrange("(r p) c -> p r c", p=P)
        return a["L0_ffn_w_proj"][:, (u - NH) * D:(u - NH + 1) * D].rearrange("(r p) c -> p r c", p=P)

    def load(sp):
        for u in range(NUNIT):
            if u and u % PER == 0:
                sp.wait_ge(t_in, 16 * u)
            sp.dma_start(stage[:, u, :, :], unit(u)).then_inc(t_in, 16)

    def magnitudes(act, i):
        act.wait_ge(t_in, 16 * PER * (i + 1))
        for u in range(PER):
            act.wait_ge(t_abs, PER * i + u + 1)
            nc.scalar.activation(junk[:, :], stage[:, PER * i + u, :, :].rearrange("p r c -> p (r c)"), ACT.Abs,
                                 accum_out=part[:, bass.ds(PER * i + u, 1)]).then_inc(t_abs, 1)

    with nc.Block() as block:
        @block.scalar
        def _(act):
            act.sem_inc(t_abs, 1)
    env["front"]("bit", XTh, XTl, load, magnitudes)
    jst.close()
    below = wb("b_below", [P, 2, 4, D], U8)
    tern = wb("b_tern", [P, 2, 4, D], F16)
    OWN = (0, 2, 4, 6)

    def low(u, eng):
        return eng.tensor_scalar(below[:, u % 2, :, :], stage[:, u, :, :], scale[:, 4 + u // NH:5 + u // NH], None,
                                 ALU.is_lt)

    with nc.Block() as block:
        @block.gpsimd
        def _(pool):
            pool.wait_ge(t_low, 1)
            for u in OWN:
                if u >= 2:
                    pool.wait_ge(t_use, u - 1)
                low(u, nc.gpsimd).then_inc(t_low, 1)

        @block.scalar
        def _(act):
            for u in range(NUNIT):
                for h in range(2):
                    act.wait_ge(t_tr, 2 * u + h + 1)
                    if u < NH:
                        dst = wfc[:, u, 2 * h:2 * h + 2, :]
                    else:
                        dst = wpj[:, KC * (u - NH) + 2 * h:KC * (u - NH) + 2 * h + 2, :]
                    nc.scalar.activation(dst, bank16(h).rearrange("p (k c) -> p k c", k=2),
                                         ACT.Copy).then_inc(t_cp, 1)

        @block.vector
        def _(dve):
            link = Chain(dve, t_ch)
            link(nc.vector.memset(ones[:, :], 1.0))
            nc.vector.reduce_sum(sums[:, :], part[:, :].rearrange("p (m u) -> p m u", m=2), AX_X).then_inc(t_part, 1)
            dve.wait_ge(t_tot, 1)
            link(nc.vector.tensor_scalar(scale[:, 0:2], bank[4][:, 0:2], 1.0 / (F0 * D), None, ALU.mult))
            link(nc.vector.tensor_scalar(scale[:, 2:4], scale[:, 0:2], 1e-6, 0.5, ALU.add, ALU.mult))
            link(nc.vector.tensor_scalar(scale[:, 4:6], scale[:, 2:4], -1.0, None, ALU.mult))
            nc.vector.tensor_tensor(scale[:, 6:7], scale[:, 1:2], tg[:, 2:3], ALU.mult).then_inc(t_low, 1)
            for u in range(NUNIT):
                m = u // NH
                if u in OWN:
                    dve.wait_ge(t_low, 2 + OWN.index(u))
                else:
                    if u >= 2:
                        dve.wait_ge(t_use, u - 1)
                    link(low(u, nc.vector))
                if u >= 2:
                    dve.wait_ge(t_tr, 2 * (u - 1))
                nc.vector.scalar_tensor_tensor(out=tern[:, u % 2, :, :], in0=stage[:, u, :, :],
                                               scalar=scale[:, 2 + m:3 + m], in1=below[:, u % 2, :, :],
                                               op0=ALU.is_gt, op1=ALU.subtract).then_inc(t_use, 1)

        @block.tensor
        def _(pe):
            pe.wait_ge(t_part, 1)
            nc.tensor.matmul(bank[4][:, 0:2], ones[:, :], sums[:, :], start=True, stop=True).then_inc(t_tot, 1)
            for u in range(NUNIT):
                pe.wait_ge(t_use, u + 1)
                for h in range(2):
                    if u:
                        pe.wait_ge(t_cp, 2 * (u - 1) + h + 1)
                    for k in range(2):
                        for r in range(4):
                            last = nc.tensor.transpose(bank16(h)[:, (4 * k + r) * P:(4 * k + r + 1) * P],
                                                       tern[:, u % 2, r, (2 * h + k) * P:(2 * h + k + 1) * P],
                                                       ident16[:, :])
                    last.then_inc(t_tr, 1)
    wst.close()

    h32 = sb("b_h", [P, 2, F0])
    xn = sb("b_xn", [P, 2, F0])
    hTh = sb("b_hTh", [P, 2, HC, P], F16)
    hTl = sb("b_hTl", [P, 2, HC, P], F16)
    stats = sb("b_stats", [P, 2, NH, 6])
    mv = sb("b_mv", [P, 2, 2])
    ve = sb("b_ve", [P, 2, 1])
    rs = sb("b_rs", [P, 2, 2])
    q = sb("b_q", [P, 2, 4])
    mhalf = sb("b_mh", [P, 1])
    hold = sb("b_hold", [P, 1])
    b_up, b_ge, b_ch, b_var, b_rs, b_nm, b_xn, b_q, b_tr, b_hi, b_lo, b_dn, b_out, b_mh = (sem("b_" + n) for n in (
        "up", "gelu", "chain", "var", "rstd", "nmean", "norm", "quant", "tr", "hi", "lo", "down", "out", "mh"))
    UP, TR, ACC = 0, 2, 4

    def rounds(eng, step):
        with eng.Fori(0, TILES // 2 - 1) as t:
            step(2 * t, 0)
            step(2 * t + 1, 1)
        step(TILES - 2, 0, 1)
        step(TILES - 1, 1, 0)

    with nc.Block() as block:
        @block.gpsimd
        def _(pool):
            nc.gpsimd.memset(mhalf[:, :], -0.5).then_inc(b_mh, 1)
            pool.wait_ge(b_mh, 1)
            with pool.Fori(0, TILES // 2) as i:
                for p in range(2):
                    pool.wait_ge(b_var, 2 * i + p + 1)
                    nc.gpsimd.tensor_tensor(rs[:, p, 0:1], ve[:, p, :], mhalf[:, :], ALU.pow).then_inc(b_rs, 1)

        @block.tensor
        def _(pe):
            pe.sem_inc(b_dn, 2)
            pe.sem_inc(b_tr, 2 * KC)
            def up(n, i):
                for h in range(NH):
                    pe.wait_ge(b_ge, NH * n + h + 1)
                    for k in range(KC):
                        x = bass.ds(n * P, P)
                        nc.tensor.matmul(bank[UP + h % 2][:, :], XTh[:, k, x], wfc[:, h, k, :],
                                         start=(k == 0), stop=False)
                        last = nc.tensor.matmul(bank[UP + h % 2][:, :], XTl[:, k, x], wfc[:, h, k, :],
                                                start=False, stop=(k == KC - 1))
                    last.then_inc(b_up, 1)

            def turn(n, i):
                pe.wait_ge(b_q, n + 1)
                for g in range(KC):
                    pe.wait_ge(b_lo, KC * n + g + 1)
                    for r in range(4):
                        c = (4 * g + r) * P
                        last = nc.tensor.transpose(bank[TR + g % 2][:, r * P:(r + 1) * P],
                                                   xn[:, i % 2, c:c + P], ident[:, :])
                    last.then_inc(b_tr, 1)

            def down(n, i):
                pe.wait_ge(b_lo, KC * n + KC + 2)
                pe.wait_ge(b_out, n + 1)
                for c in range(HC):
                    nc.tensor.matmul(bank[ACC + i % 2][:, :], hTh[:, i % 2, c, :], wpj[:, c, :],
                                     start=(c == 0), stop=False)
                    last = nc.tensor.matmul(bank[ACC + i % 2][:, :], hTl[:, i % 2, c, :], wpj[:, c, :],
                                            start=False, stop=(c == HC - 1))
                last.then_inc(b_dn, 1)
            up(0, 0)
            up(1, 1)
            turn(0, 0)

            def step(n, i, ahead=2):
                if ahead > 1:
                    up(n + 2, i)
                down(n, i)
                if ahead:
                    turn(n + 1, 1 - i)
            rounds(pe, step)

        @block.scalar
        def _(act):
            act.sem_inc(b_ge, 2)
            def gelu(n, i, pieces):
                for h in pieces:
                    act.wait_ge(b_up, NH * n + h + 1)
                    nc.scalar.activation(h32[:, i % 2, h * D:(h + 1) * D], bank[UP + h % 2][:, :], ACT.Gelu,
                                         scale=scale[:, 0:1]).then_inc(b_ge, 1)

            def norm(n, i):
                act.wait_ge(b_nm, n + 1)
                act.wait_ge(b_tr, KC * n + KC)
                nc.scalar.activation(xn[:, i % 2, :], h32[:, i % 2, :], ACT.Identity, bias=rs[:, i % 2, 1:2],
                                     scale=rs[:, i % 2, 0:1]).then_inc(b_xn, 1)

            def high(n, i):
                act.wait_ge(b_dn, n + 1)
                for g in range(KC):
                    act.wait_ge(b_tr, KC * n + g + 1 + 2 * KC)
                    nc.scalar.activation(hTh[:, i % 2, 4 * g:4 * g + 4, :],
                                         bank[TR + g % 2][:, :].rearrange("p (r c) -> p r c", r=4),
                                         ACT.Copy).then_inc(b_hi, 1)
            gelu(0, 0, range(NH))
            gelu(1, 1, range(NH // 2))
            norm(0, 0)
            gelu(1, 1, range(NH // 2, NH))
            high(0, 0)

            def step(n, i, ahead=2):
                if ahead > 1:
                    gelu(n + 2, i, range(NH // 2))
                if ahead:
                    norm(n + 1, 1 - i)
                if ahead > 1:
                    gelu(n + 2, i, range(NH // 2, NH))
                if ahead:
                    high(n + 1, 1 - i)
            rounds(act, step)

        @block.vector
        def _(dve):
            dve.sem_inc(b_lo, 2)
            dve.sem_inc(b_out, 2)
            link = Chain(dve, b_ch)
            PER = NH + 1 + 5

            def stat(n, i, pieces):
                for h in pieces:
                    dve.wait_ge(b_ge, NH * n + h + 3)
                    link(nc.vector.bn_stats(stats[:, i % 2, h, :], h32[:, i % 2, h * D:(h + 1) * D]))

            def moments(n, i):
                nc.vector.memset(hold[:, :], 0.0)
                link(nc.vector.bn_aggr(mv[:, i % 2, :], stats[:, i % 2, :, :].rearrange("p h s -> p (h s)")))
                nc.vector.tensor_scalar(ve[:, i % 2, :], mv[:, i % 2, 1:2], 1e-6, None, ALU.add).then_inc(b_var, 1)
                dve.wait_ge(b_rs, n + 1)
                nc.vector.scalar_tensor_tensor(out=rs[:, i % 2, 1:2], in0=mv[:, i % 2, 0:1], scalar=-1.0,
                                               in1=rs[:, i % 2, 0:1], op0=ALU.mult, op1=ALU.mult).then_inc(b_nm, 1)

            def quant(n, i):
                dve.wait_ge(b_xn, n + 1)
                next(env["quantise"](link, [xn[:, i % 2, :]], q[:, i % 2, :])).then_inc(b_q, 1)

            def low(n, i):
                for g in range(KC):
                    dve.wait_ge(b_hi, KC * n + g + 1)
                    nc.vector.tensor_tensor(hTl[:, i % 2, 4 * g:4 * g + 4, :],
                                            bank[TR + g % 2][:, :].rearrange("p (r c) -> p r c", r=4),
                                            hTh[:, i % 2, 4 * g:4 * g + 4, :], ALU.subtract).then_inc(b_lo, 1)

            def result(n, i):
                dve.wait_ge(b_dn, n + 3)
                nc.vector.scalar_tensor_tensor(out=X[:, n, :], in0=bank[ACC + i % 2][:, :], scalar=scale[:, 6:7],
                                               in1=X[:, n, :], op0=ALU.mult, op1=ALU.add).then_inc(b_out, 1)
            stat(0, 0, range(NH))
            moments(0, 0)
            stat(1, 1, range(NH // 2))
            quant(0, 0)
            stat(1, 1, range(NH // 2, NH))
            moments(1, 1)
            low(0, 0)
            before = link.n

            def step(n, i, ahead=2):
                link.start(before + PER * n)
                if ahead > 1:
                    stat(n + 2, i, range(NH // 2))
                if ahead:
                    quant(n + 1, 1 - i)
                if ahead > 1:
                    stat(n + 2, i, range(NH // 2, NH))
                    moments(n + 2, i)
                if ahead:
                    low(n + 1, 1 - i)
                result(n, i)
                assert ahead < 2 or link.n == PER, link.n
            rounds(dve, step)
    st.close()


def phase_c(nc, a, env):
    sem, bank, bank16, X, XTh, XTl, ident, ident16, tg = (env[k] for k in (
        "sem", "bank", "bank16", "X", "XTh", "XTl", "ident", "ident16", "tg"))
    st = ExitStack()

    def sb(name, shape, dt=F32):
        return env["sb"](name, shape, dt, stack=st)

    CTh, CTl = env["CTh"], env["CTl"]
    NW = 5
    WQ, WG, WK, WV, WO = range(NW)
    wh = sb("c_wh", [P, NW, KC, D], F16)
    wl = sb("c_wl", [P, NW, KC, D], F16)
    wkv = a["L1_xattn_Wkv"]
    source = {WQ: a["L1_xattn_Wq"], WG: a["L1_xattn_Wg"], WK: wkv[0:D, :], WV: wkv[D:2 * D, :], WO: a["L1_xattn_Wo"]}
    env["front"]("ln", XTh, XTl, weights=[(source[w], wh[:, w], wl[:, w]) for w in range(NW)])

    bg = sb("c_bg", [P, D])
    blocks = sb("c_blocks", [P, P])
    heads = sb("c_heads", [P, 4])
    GPH = P // HD1
    ek = sb("c_ek", [P, 2, D])
    kk = sb("c_k", [P, 2, D])
    vv = sb("c_v", [P, 2, D])
    eq = sb("c_eq", [P, 2, D])
    qq = sb("c_q", [P, 2, D])
    gt = sb("c_gt", [P, 2, D])
    kv = sb("c_kv", [P, KC, P])
    ks = sb("c_ks", [P, KC, GPH])
    ksr = sb("c_ksr", [P, KC])
    onec = sb("c_one", [P, 1])
    den = sb("c_den", [P, 2, H1])
    og = sb("c_og", [P, 2, D])
    oTh = sb("c_oTh", [P, 2, KC, P], F16)
    oTl = sb("c_oTl", [P, 2, KC, P], F16)
    T = B

    c_in = sem("c_in")
    c_cst = sem("c_const")
    names = ("K0", "K1", "V0", "V1", "Q0", "Q1", "G0", "G1",
             "eK0", "eK1", "eQ0", "eQ1", "tG0", "tG1", "cV0", "cV1", "lG0", "lG1",
             "pK0", "pK1", "pQ0", "pQ1",
             "SUM", "mSUM", "ATT0", "ATT1", "OG0", "OG1", "T0", "T1", "hT0", "hT1", "lT0", "lT1", "O0", "O1",
             "X0", "X1", "ch")
    ev = {n: sem("c_" + n) for n in names}

    with nc.Block() as block:
        @block.sync
        def _(sp):
            sp.dma_start(bg[:, :], env["row"](a["L1_xattn_bg"])).then_inc(c_in, 16)

        @block.gpsimd
        def _(pool):
            nc.gpsimd.memset(onec[:, :], 1.0).then_inc(c_cst, 1)

        @block.vector
        def _(dve):
            link = Chain(dve, ev["ch"])
            link(nc.vector.reduce_sum(heads[:, :], ident[:, :].rearrange("p (h c) -> p h c", h=GPH), AX_X))
            link(nc.vector.tensor_copy(blocks[:, :].rearrange("p (h c) -> p h c", h=GPH),
                                       heads[:, :].unsqueeze(2).broadcast_to([P, GPH, HD1])))

    def rounds(body, tail):
        def go(eng):
            body(0, False)
            with eng.Fori(0, T - 1) as i:
                body(i + 1, True)
            tail(T - 1)
        return go

    with nc.Block() as block:
        @block.tensor
        def _(pe):
            pe.wait_ge(c_cst, 1)

            def wait(n, b):
                pe.wait_ge(ev[n], b + 1)

            def project(dst, xh, xl, w, b, tt, n):
                x = bass.ds((2 * b + tt) * P, P)
                for k in range(KC):
                    last = env["three"](dst, xh[:, k, x], xl[:, k, x], wh[:, w, k, :], wl[:, w, k, :],
                                        k == 0, k == KC - 1)
                last.then_inc(ev[n], 1)

            def turn(b):
                for tt in range(2):
                    wait(f"OG{tt}", b)
                    for k in range(KC):
                        last = nc.tensor.transpose(bank[4 + tt][:, k * P:(k + 1) * P],
                                                   og[:, tt, k * P:(k + 1) * P], ident[:, :])
                    last.then_inc(ev[f"T{tt}"], 1)

            def output(b):
                for tt in range(2):
                    wait(f"lT{tt}", b)
                    for k in range(KC):
                        last = env["three"](bank[4 + tt][:, :], oTh[:, tt, k, :], oTl[:, tt, k, :],
                                            wh[:, WO, k, :], wl[:, WO, k, :], k == 0, k == KC - 1)
                    last.then_inc(ev[f"O{tt}"], 1)

            def body(b, more):
                for tt in range(2):
                    if more:
                        wait("mSUM", b - 1)
                    project(bank[tt][:, :], CTh, CTl, WK, b, tt, f"K{tt}")
                if more:
                    turn(b - 1)
                for tt in range(2):
                    project(bank[2 + tt][:, :], CTh, CTl, WV, b, tt, f"V{tt}")
                if more:
                    output(b - 1)
                for n in ("pK0", "pK1", "cV0", "cV1"):
                    wait(n, b)
                for c in range(KC):
                    for tt in range(2):
                        nc.tensor.matmul(bank[0][:, c * P:(c + 1) * P], kk[:, tt, c * P:(c + 1) * P],
                                         vv[:, tt, c * P:(c + 1) * P], start=(tt == 0), stop=(tt == 1))
                for c in range(KC):
                    for tt in range(2):
                        last = nc.tensor.matmul(bank[1][:, c:c + 1], kk[:, tt, c * P:(c + 1) * P], onec[:, :],
                                                start=(tt == 0), stop=(tt == 1))
                last.then_inc(ev["SUM"], 1)
                for half in range(2):
                    if more:
                        wait(f"X{half}", b - 1)
                    for oc in range(2):
                        o = (2 * half + oc) * P
                        for k in range(KC):
                            x = bass.ds(2 * b * P, 2 * P)
                            last = env["three"](bank[4 + half][:, oc * 2 * P:(oc + 1) * 2 * P],
                                                wh[:, WQ, k, o:o + P], wl[:, WQ, k, o:o + P],
                                                XTh[:, k, x], XTl[:, k, x], k == 0, k == KC - 1)
                    last.then_inc(ev[f"Q{half}"], 1)
                for tt in range(2):
                    project(bank[6 + tt][:, :], XTh, XTl, WG, b, tt, f"G{tt}")
                for n in ("mSUM", "pQ0", "pQ1"):
                    wait(n, b)
                for tt in range(2):
                    wait(f"lG{tt}", b)
                    for c in range(KC):
                        qT = qq[:, c // 2, (c % 2) * 2 * P + tt * P:(c % 2) * 2 * P + (tt + 1) * P]
                        nc.tensor.matmul(bank[2 + tt][:, c * P:(c + 1) * P], qT, kv[:, c, :], start=True, stop=True)
                    for c in range(KC):
                        qT = qq[:, c // 2, (c % 2) * 2 * P + tt * P:(c % 2) * 2 * P + (tt + 1) * P]
                        last = nc.tensor.matmul(bank[6 + tt][:, c * GPH:(c + 1) * GPH], qT, ks[:, c, :],
                                                start=True, stop=True)
                    last.then_inc(ev[f"ATT{tt}"], 1)

            def tail(b):
                turn(b)
                output(b)
            rounds(body, tail)(pe)

        @block.scalar
        def _(act):
            def step(n, b, dst, src, then, func=ACT.Copy, scale=1.0):
                for tt in range(2):
                    act.wait_ge(ev[f"{n}{tt}"], b + 1)
                    nc.scalar.activation(dst(tt), src(tt), func, scale=scale).then_inc(ev[f"{then}{tt}"], 1)

            def high(b):
                step("T", b, lambda tt: oTh[:, tt], lambda tt: bank[4 + tt][:, :].rearrange("p (k c) -> p k c", k=KC),
                     "hT")

            def body(b, more):
                step("K", b, lambda tt: ek[:, tt, :], lambda tt: bank[tt][:, :], "eK", ACT.Exp)
                if more:
                    high(b - 1)
                step("V", b, lambda tt: vv[:, tt, :], lambda tt: bank[2 + tt][:, :], "cV")
                step("Q", b, lambda tt: eq[:, tt, :], lambda tt: bank[4 + tt][:, :], "eQ", ACT.Exp)
                step("lG", b, lambda tt: gt[:, tt, :], lambda tt: gt[:, tt, :], "tG", ACT.Tanh, 0.5)
            rounds(body, high)(act)

        @block.vector
        def _(dve):
            dve.wait_ge(c_in, 16)
            PER = 2 + 2 + 1 + 2 * 4
            link = Chain(dve, ev["ch"])

            def wait(n, b):
                dve.wait_ge(ev[n], b + 1)

            def phi(dst, e, src, n):
                link(nc.vector.tensor_scalar(e, e, 1.0, None, ALU.min))
                nc.vector.scalar_tensor_tensor(out=dst, in0=src, scalar=0.0, in1=e, op0=ALU.max,
                                               op1=ALU.add).then_inc(ev[n], 1)

            def tail(b):
                for tt in range(2):
                    wait(f"hT{tt}", b)
                    nc.vector.tensor_tensor(oTl[:, tt], bank[4 + tt][:, :].rearrange("p (k c) -> p k c", k=KC),
                                            oTh[:, tt], ALU.subtract).then_inc(ev[f"lT{tt}"], 1)
                for tt in range(2):
                    wait(f"O{tt}", b)
                    xt = X[:, 2 * b + tt, :]
                    nc.vector.scalar_tensor_tensor(out=xt, in0=bank[4 + tt][:, :], scalar=tg[:, 1:2], in1=xt,
                                                   op0=ALU.mult, op1=ALU.add).then_inc(ev[f"X{tt}"], 1)

            def body(b, more):
                link.start(b * PER + 2)
                for tt in range(2):
                    wait(f"eK{tt}", b)
                    phi(kk[:, tt, :], ek[:, tt, :], bank[tt][:, :], f"pK{tt}")
                if more:
                    tail(b - 1)
                wait("SUM", b)
                nc.vector.tensor_tensor(kv[:, :, :], bank[0][:, :].rearrange("p (k c) -> p k c", k=KC),
                                        blocks[:, :].unsqueeze(1).broadcast_to([P, KC, P]), ALU.mult)
                link(nc.vector.tensor_copy(ksr[:, :], bank[1][:, 0:KC]))
                nc.vector.tensor_tensor(ks[:, :, :], ksr[:, :].unsqueeze(2).broadcast_to([P, KC, GPH]),
                                        heads[:, :].unsqueeze(1).broadcast_to([P, KC, GPH]), ALU.mult)\
                  .then_inc(ev["mSUM"], 1)
                for tt in range(2):
                    wait(f"eQ{tt}", b)
                    phi(qq[:, tt, :], eq[:, tt, :], bank[4 + tt][:, :], f"pQ{tt}")
                for tt in range(2):
                    wait(f"G{tt}", b)
                    nc.vector.tensor_tensor(gt[:, tt, :], bank[6 + tt][:, :], bg[:, :], ALU.add)\
                      .then_inc(ev[f"lG{tt}"], 1)
                for tt in range(2):
                    wait(f"ATT{tt}", b)
                    link(nc.vector.tensor_scalar(den[:, tt, :], bank[6 + tt][:, 0:H1], 1e-6, None, ALU.add))
                    link(nc.vector.reciprocal(den[:, tt, :], den[:, tt, :]))
                    o3 = og[:, tt, :].rearrange("p (h c) -> p h c", h=H1)
                    link(nc.vector.tensor_tensor(o3, bank[2 + tt][:, :].rearrange("p (h c) -> p h c", h=H1),
                                                 den[:, tt, :].unsqueeze(2).broadcast_to([P, H1, HD1]), ALU.mult))
                    wait(f"tG{tt}", b)
                    link(nc.vector.tensor_scalar(gt[:, tt, :], gt[:, tt, :], 0.5, 0.5, ALU.mult, ALU.add))
                    nc.vector.tensor_tensor(og[:, tt, :], og[:, tt, :], gt[:, tt, :], ALU.mult)\
                      .then_inc(ev[f"OG{tt}"], 1)
                assert link.n == PER, link.n
            rounds(body, tail)(dve)
    st.close()


def phase_d(nc, a, env):
    sem, bank, bank16, X, XTh, XTl, ident, ident16, tg = (env[k] for k in (
        "sem", "bank", "bank16", "X", "XTh", "XTl", "ident", "ident16", "tg"))
    st = ExitStack()

    def sb(name, shape, dt=F32):
        return env["sb"](name, shape, dt, stack=st)

    NU = 3
    wh = sb("d_wh", [P, 2, NU, KC, CH], F16)
    wl = sb("d_wl", [P, 2, NU, KC, CH], F16)
    stage = sb("d_stage", [P, NU, 4, P])
    env["front"]("ln", XTh, XTl, weights=[
        (w, wh[:, 0, k], wl[:, 0, k]) for k, w in enumerate(
            (a["L1_ffn_sw1"][0:CH, :], a["L1_ffn_sw2"][0:CH, :], a["L1_ffn_sw3"][:, 0:CH]))])
    combT = sb("d_combT", [P, TILES * P], F16)
    pick = sb("d_pick", [P, E, P], F16)

    rst = ExitStack()

    def rb(name, shape, dt=F32):
        return env["sb"](name, shape, dt, stack=rst)

    rw = rb("r_w", [E, D])
    rwT = rb("r_wT", [P, KC, 2 * E], F16)
    ebias = rb("r_bias", [P, E])
    sc = rb("r_sc", [P, TILES, E])
    sel = rb("r_sel", [P, TILES, E])
    rank = rb("r_rank", [P, TILES, E])
    cmp_ = rb("r_cmp", [P, TILES, E])
    tot = rb("r_tot", [P, TILES])
    inv = rb("r_inv", [P, TILES])
    both = rb("r_both", [P, TILES, 2 * E], F16)
    ones = rb("r_ones", [2 * E, E])
    r_in, r_wt, r_whi, r_wlo, r_lg, r_add, r_sig, r_ch, r_split, r_tr, r_done = (sem("r_" + n) for n in (
        "in", "wt", "whi", "wlo", "lg", "add", "sig", "ch", "split", "tr", "done"))
    with nc.Block() as block:
        @block.sync
        def _(sp):
            sp.dma_start(rw[:, :], a["L1_ffn_router_w"]).then_inc(r_in, 16)
            sp.dma_start(ebias[:, :], env["row"](a["L1_ffn_expert_bias"])).then_inc(r_in, 16)

        @block.tensor
        def _(pe):
            pe.wait_ge(r_in, 32)
            for k in range(KC):
                last = nc.tensor.transpose(bank[0][:, k * E:(k + 1) * E], rw[:, k * P:(k + 1) * P], ident[0:E, 0:E])
            last.then_inc(r_wt, 1)
            pe.wait_ge(r_wlo, 1)
            with pe.Fori(0, TILES) as i:
                for k in range(KC):
                    cols = bass.ts(i, P)
                    nc.tensor.matmul(bank[1][:, bass.ts(i, 2 * E)], XTh[:, k, cols], rwT[:, k, :],
                                     start=(k == 0), stop=False)
                    nc.tensor.matmul(bank[1][:, bass.ds(i * 2 * E, E)], XTl[:, k, cols], rwT[:, k, 0:E],
                                     start=False, stop=(k == KC - 1)).then_inc(r_lg, 1)
            pe.wait_ge(r_split, 1)
            for i in range(TILES):
                last = nc.tensor.transpose(bank16(2 + i // 8)[0:2 * E, (i % 8) * P:(i % 8 + 1) * P],
                                           both[:, i, :], ident16[:, :])
            last.then_inc(r_tr, 1)

        @block.scalar
        def _(act):
            act.wait_ge(r_wt, 1)
            nc.scalar.activation(rwT[:, :, 0:E], bank[0][:, 0:KC * E].rearrange("p (k e) -> p k e", k=KC),
                                 ACT.Copy).then_inc(r_whi, 1)
            act.wait_ge(r_add, 1)
            nc.scalar.activation(sc[:, :, :], rank[:, :, :], ACT.Sigmoid).then_inc(r_sig, 1)
            act.wait_ge(r_tr, 1)
            for h in range(2):
                nc.scalar.activation(combT[0:2 * E, h * 1024:(h + 1) * 1024], bank16(2 + h)[0:2 * E, :],
                                     ACT.Copy).then_inc(r_done, 1)

        @block.vector
        def _(dve):
            link = Chain(dve, r_ch)
            link(nc.vector.memset(combT[:, :], 0.0))
            link(nc.vector.memset(pick[:, :, :], 0.0))
            link(nc.vector.tensor_tensor(ones[:, :], ident16[0:2 * E, 0:E], ident16[0:2 * E, E:2 * E], ALU.add))
            link(nc.vector.tensor_copy(pick[0:2 * E, :, :], ones[:, :].unsqueeze(2).broadcast_to([2 * E, E, P])))
            dve.wait_ge(r_whi, 1)
            nc.vector.tensor_tensor(rwT[:, :, E:2 * E], bank[0][:, 0:KC * E].rearrange("p (k e) -> p k e", k=KC),
                                    rwT[:, :, 0:E], ALU.subtract).then_inc(r_wlo, 1)
            dve.wait_ge(r_lg, TILES * KC)
            lg = bank[1][:, 0:TILES * 2 * E].rearrange("p (t e) -> p t e", t=TILES)
            link(nc.vector.tensor_copy(cmp_[:, :, :], lg[:, :, E:2 * E]))
            nc.vector.tensor_tensor(rank[:, :, :], lg[:, :, 0:E], cmp_[:, :, :], ALU.add).then_inc(r_add, 1)
            dve.wait_ge(r_sig, 1)
            link(nc.vector.tensor_tensor(sel[:, :, :], sc[:, :, :],
                                         ebias[:, :].unsqueeze(1).broadcast_to([P, TILES, E]), ALU.add))
            link(nc.vector.memset(rank[:, :, :], 0.0))
            for d in range(1, E):
                link(nc.vector.tensor_tensor(cmp_[:, :, 0:E - d], sel[:, :, 0:E - d], sel[:, :, d:E], ALU.is_ge))
                link(nc.vector.tensor_tensor(rank[:, :, d:E], rank[:, :, d:E], cmp_[:, :, 0:E - d], ALU.add))
                link(nc.vector.tensor_tensor(cmp_[:, :, 0:E - d], sel[:, :, d:E], sel[:, :, 0:E - d], ALU.is_gt))
                link(nc.vector.tensor_tensor(rank[:, :, 0:E - d], rank[:, :, 0:E - d], cmp_[:, :, 0:E - d], ALU.add))
            link(nc.vector.scalar_tensor_tensor(out=sel[:, :, :], in0=rank[:, :, :], scalar=1.5, in1=sc[:, :, :],
                                                op0=ALU.is_lt, op1=ALU.mult))
            link(nc.vector.reduce_sum(tot[:, :], sel[:, :, :], AX_X))
            link(nc.vector.tensor_scalar(tot[:, :], tot[:, :], 1e-9, None, ALU.add))
            link(nc.vector.reciprocal(inv[:, :], tot[:, :]))
            link(nc.vector.tensor_tensor(sel[:, :, :], sel[:, :, :],
                                         inv[:, :].unsqueeze(2).broadcast_to([P, TILES, E]), ALU.mult))
            link(nc.vector.tensor_copy(both[:, :, 0:E], sel[:, :, :]))
            nc.vector.tensor_tensor(both[:, :, E:2 * E], sel[:, :, :], both[:, :, 0:E],
                                    ALU.subtract).then_inc(r_split, 1)
    rst.close()

    silu = sb("d_silu", [P, BLK])
    hid = sb("d_hid", [P, 2, BLK])
    hh = sb("d_hh", [P, 2, BLK], F16)
    hl = sb("d_hl", [P, 2, BLK], F16)
    d_g, d_u, d_s, d_hm, d_h, d_hi, d_lo, d_dn, d_accf, d_bc = (sem("d_" + n) for n in (
        "gate", "up", "silu", "mul", "weighted", "hi", "lo", "down", "acc_free", "bc"))
    p_st = [sem(f"p_stage{k}") for k in range(NU)]
    p_tr, p_hi, p_lo = sem("p_tr"), sem("p_hi"), sem("p_lo")
    PRE = NU * KC
    GATE, UP, BC, TR = 4, 5, 6, 7
    NS = FS // CH
    NR = E * FR // CH
    BPC = TILES * P // BLK
    TPB = BLK // P

    def source(c, k, t):
        if k < 2:
            if isinstance(c, tuple):
                return [a["L1_ffn_w12"][2 * c[1] + j, k * FR:(k + 1) * FR, t * P:(t + 1) * P]
                        .rearrange("(r p) c -> p r c", p=P) for j in range(2)]
            w = a[("L1_ffn_sw1", "L1_ffn_sw2")[k]]
            return [w[bass.ts(c, CH), t * P:(t + 1) * P].rearrange("(r p) c -> p r c", p=P)]
        if isinstance(c, tuple):
            return [a["L1_ffn_w3"][2 * c[1] + t // 2, :, (t % 2) * P:(t % 2 + 1) * P]
                    .rearrange("(r p) c -> p r c", p=P)]
        return [a["L1_ffn_sw3"][:, bass.ds(c * CH + t * P, P)].rearrange("(r p) c -> p r c", p=P)]

    def plan(eng, chunk):
        with eng.Fori(0, NS // 2 - 1) as cp:
            chunk(2 * cp, 0, None, 2 * cp + 1)
            chunk(2 * cp + 1, 1, None, 2 * cp + 2)
        chunk(NS - 2, 0, None, NS - 1)
        chunk(NS - 1, 1, None, ("routed", 0))
        for r in range(NR):
            chunk(NS + r, r % 2, r, ("routed", r + 1) if r + 1 < NR else None)

    with nc.Block() as block:
        @block.sync
        def _(sp):
            def load(c, q):
                for t in range(BPC):
                    for k in range(NU):
                        sp.wait_ge(p_tr, q + NU * t + k + 1)
                        parts = source(c, k, t)
                        w = 4 // len(parts)
                        for j, part in enumerate(parts):
                            sp.dma_start(stage[:, k, w * j:w * j + w, :], part)\
                              .then_inc(p_st[k], 16)
            for c in range(1, NS):
                load(c, PRE * c)
            for r in range(NR):
                load(("routed", r), PRE * (NS + r))

        @block.tensor
        def _(pe):
            pe.sem_inc(p_tr, NU + PRE)
            pe.sem_inc(d_dn, 2)

            def transposes(k, q, dma):
                pe.wait_ge(p_st[k], dma)
                pe.wait_ge(p_lo, q + 1)
                for r in range(4):
                    last = nc.tensor.transpose(bank[TR][:, r * P:(r + 1) * P], stage[:, k, r, :], ident[:, :])
                last.then_inc(p_tr, 1)

            def down(j, s, n, par):
                pe.wait_ge(d_lo, s + 1)
                if j == 0:
                    pe.wait_ge(d_accf, n + 1)
                for tt in range(TPB):
                    cols = slice(tt * P, (tt + 1) * P)
                    last = three_(bank[tt][:, :], hh[:, j % 2, cols], hl[:, j % 2, cols],
                                  wh[:, par, 2, j, :], wl[:, par, 2, j, :], j == 0, j == KC - 1)
                last.then_inc(d_dn, 1)

            three_ = env["three"]

            def chunk(c, par, routed, nxt):
                with pe.Fori(0, BPC) as t:
                    n = c * BPC + t
                    tok = bass.ts(t, BLK)
                    for j in range(KC):
                        s = n * KC + j
                        pe.wait_ge(d_s, s + 1)
                        cols = slice(j * P, (j + 1) * P)
                        for k in range(KC):
                            last = three_(bank[GATE][:, :], wh[:, par, 0, k, cols], wl[:, par, 0, k, cols],
                                          XTh[:, k, tok], XTl[:, k, tok], k == 0, k == KC - 1)
                        last.then_inc(d_g, 1)
                        pe.wait_ge(d_hm, s + 1)
                        for k in range(KC):
                            last = three_(bank[UP][:, :], wh[:, par, 1, k, cols], wl[:, par, 1, k, cols],
                                          XTh[:, k, tok], XTl[:, k, tok], k == 0, k == KC - 1)
                        last.then_inc(d_u, 1)
                        if routed is not None and j % 2 == 0:
                            pe.wait_ge(d_h, s - NS * BPC * KC + 1)
                            nc.tensor.matmul(bank[BC][:, :], pick[:, 2 * routed + j // 2, :], combT[:, tok],
                                             start=True, stop=True).then_inc(d_bc, 1)
                        if nxt is not None and j < NU:
                            transposes(j, PRE + n * NU + j, dma_value(nxt, j, t))
                        if j:
                            down(j - 1, s - 1, n, par)
                    down(KC - 1, n * KC + KC - 1, n, par)

            def dma_value(c, k, t):
                if isinstance(c, tuple):
                    per = 2 if k < 2 else 1
                    return 16 * BPC * (NS - 1) + 16 * per * (BPC * c[1] + t + 1)
                return 16 * (BPC * (c - 1) + t + 1)

            plan(pe, chunk)

        @block.scalar
        def _(act):
            act.sem_inc(d_s, 1)
            act.sem_inc(p_hi, PRE)

            def high(par, k, t, q):
                act.wait_ge(p_tr, q + 1 + NU)
                nc.scalar.activation(wh[:, par, k, t, :], bank[TR][:, :], ACT.Copy).then_inc(p_hi, 1)

            def chunk(c, par, routed, nxt):
                with act.Fori(0, BPC) as t:
                    n = c * BPC + t
                    for j in range(KC):
                        s = n * KC + j
                        act.wait_ge(d_g, s + 1)
                        act.wait_ge(d_hm, s + 1)
                        nc.scalar.activation(silu[:, :], bank[GATE][:, :], ACT.Silu).then_inc(d_s, 1)
                        if nxt is not None and j < NU:
                            high(1 - par, j, t, PRE + n * NU + j)
                        if routed is None:
                            act.wait_ge(d_hm, s + 2)
                        else:
                            act.wait_ge(d_h, s - NS * BPC * KC + 2)
                        act.wait_ge(d_dn, s + 1)
                        nc.scalar.activation(hh[:, j % 2, :], hid[:, j % 2, :], ACT.Copy).then_inc(d_hi, 1)

            plan(act, chunk)

        @block.vector
        def _(dve):
            dve.sem_inc(d_hm, 1)
            dve.sem_inc(d_accf, 1)
            dve.sem_inc(p_lo, 1 + PRE)
            dve.sem_inc(d_h, 1)

            def low(par, k, t, q):
                dve.wait_ge(p_hi, q + 1)
                nc.vector.tensor_tensor(wl[:, par, k, t, :], bank[TR][:, :], wh[:, par, k, t, :],
                                        ALU.subtract).then_inc(p_lo, 1)

            def chunk(c, par, routed, nxt):
                with dve.Fori(0, BPC) as t:
                    n = c * BPC + t
                    for j in range(KC):
                        s = n * KC + j
                        dve.wait_ge(d_u, s + 1)
                        dve.wait_ge(d_s, s + 2)
                        nc.vector.tensor_tensor(hid[:, j % 2, :], silu[:, :], bank[UP][:, :],
                                                ALU.mult).then_inc(d_hm, 1)
                        if routed is not None:
                            dve.wait_ge(d_hm, s + 2)
                            if j % 2 == 0:
                                dve.wait_ge(d_bc, (n - NS * BPC) * 2 + j // 2 + 1)
                            nc.vector.tensor_tensor(hid[:, j % 2, :], hid[:, j % 2, :], bank[BC][:, :],
                                                    ALU.mult).then_inc(d_h, 1)
                        if nxt is not None and j < NU:
                            low(1 - par, j, t, PRE + n * NU + j)
                        dve.wait_ge(d_hi, s + 1)
                        nc.vector.tensor_tensor(hl[:, j % 2, :], hid[:, j % 2, :], hh[:, j % 2, :],
                                                ALU.subtract).then_inc(d_lo, 1)
                    dve.wait_ge(d_dn, (n + 1) * KC + 2)
                    for tt in range(TPB):
                        xt = X[:, t * TPB + tt, :]
                        last = nc.vector.scalar_tensor_tensor(out=xt, in0=bank[tt][:, :], scalar=tg[:, 3:4], in1=xt,
                                                              op0=ALU.mult, op1=ALU.add)
                    last.then_inc(d_accf, 1)

            plan(dve, chunk)
    st.close()


_INS = ['x', 'ctx_2048', 'mask_SxS2_bc0', 'mask_BxS2_bk0', 'g_xattn', 'g_ffn', 'L0_xattn_Wq', 'L0_xattn_bq',
        'L0_xattn_Wk', 'L0_xattn_bk', 'L0_xattn_Wv', 'L0_xattn_bv', 'L0_xattn_Wo', 'L0_xattn_bo', 'L0_ffn_w_fc',
        'L0_ffn_w_proj', 'L1_xattn_Wq', 'L1_xattn_Wg', 'L1_xattn_bg', 'L1_xattn_Wkv', 'L1_xattn_Wo', 'L1_ffn_w12',
        'L1_ffn_w3', 'L1_ffn_router_w', 'L1_ffn_expert_bias', 'L1_ffn_sw1', 'L1_ffn_sw2', 'L1_ffn_sw3']
PHASES = "ABCD"


def kernel(**inputs):
    import numpy as _np
    import concourse.bacc as _bacc
    from concourse import mybir as _mybir
    from concourse.bass_utils import run_bass_kernel_spmd as _run

    nc = _bacc.Bacc("TRN2", target_bir_lowering=False, num_devices=1)
    arrays, args = {}, {}
    for name in _INS:
        v = _np.ascontiguousarray(inputs[name])
        arrays[f"in_{name}"] = v
        args[name] = nc.dram_tensor(f"in_{name}", v.shape, _mybir.dt.from_np(v.dtype), kind="ExternalInput").ap()
    out = nc.dram_tensor("out_x", (B, S, D), F32, kind="ExternalOutput").ap()
    flamingo(nc, args, out, PHASES)
    r = _run(nc, [arrays], core_ids=[0])
    return r.results[0]["out_x"]
```

```python
from contextlib import ExitStack

import concourse.bass as bass
from concourse import mybir

F32 = mybir.dt.float32
F16 = mybir.dt.float16
U8 = mybir.dt.uint8
I32 = mybir.dt.int32
ALU = mybir.AluOpType
ACT = mybir.ActivationFunctionType
AX_X = mybir.AxisListType.X

P = 128
B, S, D = 8, 256, 512
TILES = B * S // P
KC = D // P
MASKED = -60000.0

H0, G0, HD0 = 32, 8, 16
STK = 64
H1, HD1 = 16, 32
F0 = 2048
FS, E, FR = 2048, 8, 256
TOP = 2
NT = (B * S * TOP - E) // P + E
CH = 512
BLK = 512


class Chain:

    def __init__(self, eng, sem, base=0):
        self.eng, self.sem = eng, sem
        self.start(base)

    def start(self, base):
        self.base, self.n = base, 0

    def __call__(self, ins):
        self.n += 1
        ins.then_inc(self.sem, 1)
        self.eng.wait_ge(self.sem, self.base + self.n)


def flamingo(nc, a, out, phases="ABCD"):
    with ExitStack() as ctx:
        used = {}

        def sb(name, shape, dt=F32, stack=None):
            used[name] = used.get(name, 0) + 1
            name = name if used[name] == 1 else f"{name}_{used[name]}"
            return (stack or ctx).enter_context(nc.sbuf_tensor(name, shape, dt))

        phase_sems = []

        def sem(name):
            if not phase_sems:
                return ctx.enter_context(nc.semaphore(name))
            stack, held = phase_sems[-1]
            s = stack.enter_context(nc.semaphore(name))
            held.append(s)
            return s

        def phase(write):
            phase_sems.append((ExitStack(), []))
            write(nc, a, env)
            stack, held = phase_sems.pop()
            with nc.Block() as block:
                @block.gpsimd
                def _(pool):
                    for s in held:
                        pool.sem_clear(s)
            stack.close()

        bank = [ctx.enter_context(nc.psum_tensor(f"bank{i}", [P, 512], F32)) for i in range(8)]

        def bank16(i):
            return bank[i][:, :].bitcast(F16)

        X = sb("X", [P, TILES, D])
        XTh = sb("XTh", [P, KC, TILES * P], F16)
        XTl = sb("XTl", [P, KC, TILES * P], F16)
        ident = sb("ident", [P, P])
        ident16 = sb("ident16", [P, P], F16)
        gates = sb("gates", [P, 4])
        tg = sb("tg", [P, 4])

        x_tiles = a["x"].rearrange("b (t p) d -> p (b t) d", p=P)
        out_tiles = out.rearrange("b (t p) d -> p (b t) d", p=P)
        ctx_tiles = a["ctx_2048"].rearrange("b (t p) d -> p (b t) d", p=P)

        def row(ap):
            return ap.rearrange("(a n) -> a n", a=1).partition_broadcast(P) if len(ap.shape) == 1 else ap

        s_load = [sem(f"s_load{i}") for i in range(4)]

        def load_x(sp):
            for i in range(4):
                sp.dma_start(X[:, 4 * i:4 * i + 4, :], x_tiles[:, 4 * i:4 * i + 4, :]).then_inc(s_load[i], 16)
            for i in range(4):
                sp.wait_ge(s_load[i], 16)

        s_g = sem("s_gates")
        s_id = sem("s_ident")
        with nc.Block() as block:
            @block.sync
            def _(sp):
                sp.dma_start(gates[:, 0:2], row(a["g_xattn"])).then_inc(s_g, 16)
                sp.dma_start(gates[:, 2:4], row(a["g_ffn"])).then_inc(s_g, 16)
                if not ("A" in phases or "C" in phases):
                    load_x(sp)

            @block.gpsimd
            def _(pool):
                nc.gpsimd.memset(ident[:, :], 0.0).then_inc(s_id, 1)
                nc.gpsimd.memset(ident16[:, :], 0.0).then_inc(s_id, 1)
                pool.wait_ge(s_id, 2)
                for m in (ident, ident16):
                    nc.gpsimd.affine_select(out=m[:, :], in_=m[:, :], compare_op=ALU.not_equal, fill=1.0,
                                            base=0, pattern=[[-1, P]], channel_multiplier=1).then_inc(s_id, 1)

            @block.scalar
            def _(act):
                act.wait_ge(s_g, 32)
                nc.scalar.activation(tg[:, :], gates[:, :], ACT.Tanh)

        f_chain, f_pchain = sem("f_chain"), sem("f_pchain")
        f_var, f_rstd, f_nm, f_nrm, f_q, f_tr, f_hi, f_lo = (sem("f_" + n) for n in (
            "var", "rstd", "nmean", "normed", "quant", "tr", "hi", "lo"))
        FT = 4
        CT = 2 * FT
        f_in = [sem(f"f_in{p}") for p in range(CT)]
        f_keep = [sem(f"f_keep{p}") for p in range(FT)]
        w_in, w_tr, w_hi, w_lo = (sem("w_" + n) for n in ("in", "tr", "hi", "lo"))
        f_base = {"w": 0, "tile": 0, "norm": 0, "nrm": 0, "chain": 0, "front": 1}

        def front(kind, dsth, dstl, load=None, beside=None, weights=(), keep=None):
            st = ExitStack()
            ft = CT if kind == "ctx" else FT
            NW = len(weights)
            rows = [w.shape[0] // P for w, hi, lo in weights]
            wst = sb("f_w", [P, sum(rows), P], stack=st) if NW else None
            WB = 4
            xn = sb("f_x", [P, ft, D], stack=st)
            stats = sb("f_stats", [P, ft, 6], stack=st)
            mv = sb("f_mv", [P, ft, 2], stack=st)
            ve = sb("f_ve", [P, 2, ft], stack=st)
            rstd = sb("f_r", [P, 2, ft], stack=st)
            nmean = sb("f_nm", [P, 2, ft], stack=st)
            hold = sb("f_hold", [P, 1], stack=st)
            mhalf = sb("f_mh", [P, ft], stack=st)
            q = sb("f_q", [P, 4 * ft], stack=st)
            at = dict(f_base)
            free = 1 + CT - ft
            norms = {"ln": 1, "bit": 2, "ctx": 0}[kind]
            per = {"ln": 2, "bit": 4 + 4 + ft, "ctx": 0}[kind]

            def transposed(g):
                return bank[WB + g % 4][:, 0:rows[g] * P].rearrange("p (o c) -> p o c", o=1)

            with nc.Block() as block:
                @block.sync
                def _(sp):
                    if kind == "ctx":
                        for i in range(TILES):
                            sp.wait_ge(f_tr, at["tile"] + i + free)
                            sp.dma_start(xn[:, i % ft, :], ctx_tiles[:, i, :]).then_inc(f_in[i % ft], 16)
                    if load:
                        load(sp)
                    for k in range(KC if NW else 0):
                        if k:
                            sp.wait_ge(w_tr, at["w"] + NW * k)
                        for g, (w, hi, lo) in enumerate(weights):
                            r0 = sum(rows[:g])
                            sp.dma_start(wst[:, r0:r0 + rows[g], :],
                                         w[:, k * P:(k + 1) * P].rearrange("(r p) c -> p r c", p=P)).then_inc(w_in, 16)
                        for n in range(ft * k, ft * k + ft) if keep is not None else ():
                            sp.wait_ge(f_nrm, at["nrm"] + n + 1)
                            sp.dma_start(keep[n * P:(n + 1) * P, :], xn[:, n % ft, :]).then_inc(f_keep[n % ft], 16)
                    for p in range(ft) if keep is not None else ():
                        sp.wait_ge(f_keep[p], 16 * (TILES // ft) + 16)

                @block.gpsimd
                def _(pool):
                    if norms:
                        nc.gpsimd.memset(mhalf[:, :], -0.5).then_inc(f_pchain, 1)
                        pool.wait_ge(f_pchain, at["front"])
                        with pool.Fori(0, TILES // ft) as i:
                            for v in range(norms):
                                pool.wait_ge(f_var, at["norm"] + norms * i + v + 1)
                                nc.gpsimd.tensor_tensor(rstd[:, v, :], ve[:, v, :], mhalf[:, :],
                                                        ALU.pow).then_inc(f_rstd, 1)

                @block.tensor
                def _(pe):
                    if at["tile"] == 0:
                        pe.sem_inc(f_tr, CT)
                    with pe.Fori(0, TILES // ft) as i:
                        if NW:
                            pe.wait_ge(w_in, 16 * (at["w"] + NW * i + NW))
                        for g in range(NW):
                            pe.wait_ge(w_lo, at["w"] + NW * i + max(0, g - 3) + 1)
                            for r in range(rows[g]):
                                last = nc.tensor.transpose(bank[WB + g % 4][:, r * P:(r + 1) * P],
                                                           wst[:, sum(rows[:g]) + r, :], ident[:, :])
                            last.then_inc(w_tr, 1)
                        for p in range(ft):
                            n = at["tile"] + ft * i + p
                            if kind == "ctx":
                                pe.wait_ge(f_in[p], 16 * i + 16)
                            elif kind == "ln":
                                pe.wait_ge(f_nrm, at["nrm"] + ft * i + p + 1)
                            else:
                                pe.wait_ge(f_q, ft * i + p + 1)
                            pe.wait_ge(f_lo, n + free)
                            for k in range(KC):
                                last = nc.tensor.transpose(bank[p][:, k * P:(k + 1) * P],
                                                           xn[:, p, k * P:(k + 1) * P], ident[:, :])
                            last.then_inc(f_tr, 1)

                @block.scalar
                def _(act):
                    if keep is not None:
                        for p in range(ft):
                            act.sem_inc(f_keep[p], 16)
                    with act.Fori(0, TILES // ft) as i:
                        for v in range(norms):
                            act.wait_ge(f_nm, at["norm"] + norms * i + v + 1)
                            for p in range(ft):
                                if v == 0:
                                    act.wait_ge(f_tr, at["tile"] + ft * i + p + free)
                                    if keep is not None:
                                        act.wait_ge(f_keep[p], 16 * i + 16)
                                nc.scalar.activation(xn[:, p, :], X[:, ft * i + p, :] if v == 0 else xn[:, p, :],
                                                     ACT.Identity, bias=nmean[:, v, p:p + 1],
                                                     scale=rstd[:, v, p:p + 1]).then_inc(f_nrm, 1)
                        if beside:
                            beside(act, i)
                        for g, (w, hi, lo) in enumerate(weights):
                            act.wait_ge(w_tr, at["w"] + NW * i + g + 1)
                            nc.scalar.activation(hi[:, bass.ds(i, 1), :], transposed(g), ACT.Copy).then_inc(w_hi, 1)
                        for p in range(ft):
                            act.wait_ge(f_tr, at["tile"] + ft * i + p + 1 + CT)
                            nc.scalar.activation(dsth[:, :, bass.ts(ft * i + p, P)],
                                                 bank[p][:, :].rearrange("p (k c) -> p k c", k=KC),
                                                 ACT.Copy).then_inc(f_hi, 1)

                @block.vector
                def _(dve):
                    if at["tile"] == 0:
                        dve.sem_inc(f_lo, CT)
                        dve.sem_inc(w_lo, 1)
                    link = Chain(dve, f_chain, at["chain"])

                    def row_stats(i, v):
                        for p in range(ft):
                            if v == 1:
                                dve.wait_ge(f_nrm, at["nrm"] + norms * ft * i + p + 1)
                            last = nc.vector.bn_stats(stats[:, p, :], X[:, ft * i + p, :] if v == 0 else xn[:, p, :])
                        link(last)

                    def round_(i, more):
                        link.start(at["chain"] + per * i + (norms > 0))
                        for v in range(norms):
                            if v == 1:
                                row_stats(i, 1)
                            nc.vector.memset(hold[:, :], 0.0)
                            for p in range(ft):
                                last = nc.vector.bn_aggr(mv[:, p, :], stats[:, p, :])
                            link(last)
                            nc.vector.tensor_scalar(ve[:, v, :], mv[:, :, 1], (1e-5, 1e-6)[v], None,
                                                    ALU.add).then_inc(f_var, 1)
                            dve.wait_ge(f_rstd, at["norm"] + norms * i + v + 1)
                            nc.vector.scalar_tensor_tensor(out=nmean[:, v, :], in0=mv[:, :, 0], scalar=-1.0,
                                                           in1=rstd[:, v, :], op0=ALU.mult,
                                                           op1=ALU.mult).then_inc(f_nm, 1)
                        if norms and more:
                            row_stats(i + 1, 0)
                        for g, (w, hi, lo) in enumerate(weights):
                            dve.wait_ge(w_hi, at["w"] + NW * i + g + 1)
                            nc.vector.tensor_tensor(lo[:, bass.ds(i, 1), :], transposed(g), hi[:, bass.ds(i, 1), :],
                                                    ALU.subtract).then_inc(w_lo, 1)
                        if kind == "bit":
                            for p, ins in enumerate(quantise(
                                    link, [xn[:, p, :] for p in range(ft)], q,
                                    lambda p: dve.wait_ge(f_nrm, at["nrm"] + norms * ft * i + ft + p + 1))):
                                ins.then_inc(f_q, 1)
                        for p in range(ft):
                            dve.wait_ge(f_hi, at["tile"] + ft * i + p + 1)
                            cols = bass.ts(ft * i + p, P)
                            nc.vector.tensor_tensor(dstl[:, :, cols],
                                                    bank[p][:, :].rearrange("p (k c) -> p k c", k=KC),
                                                    dsth[:, :, cols], ALU.subtract).then_inc(f_lo, 1)
                        assert not more or link.n == per, link.n
                    if norms:
                        row_stats(0, 0)
                    with dve.Fori(0, TILES // ft - 1) as i:
                        round_(i, True)
                    round_(TILES // ft - 1, False)
            f_base["w"] += NW * KC
            f_base["tile"] += TILES
            if norms:
                f_base["front"] += 1
            f_base["norm"] += norms * TILES // ft
            f_base["nrm"] += norms * TILES
            f_base["chain"] += per * (TILES // ft)
            st.close()

        def quantise(link, xs, q, ready=lambda p: None):
            n = len(xs)
            g, r, up, down = (q[:, k * n:(k + 1) * n] for k in range(4))
            for p, x in enumerate(xs):
                ready(p)
                last = nc.vector.tensor_reduce(g[:, p:p + 1], x, AX_X, ALU.max, apply_absolute_value=True)
            link(last)
            link(nc.vector.reciprocal(r, g))
            link(nc.vector.tensor_scalar(up, r, 128.0, None, ALU.mult))
            link(nc.vector.tensor_scalar(down, g, 1.0 / 128.0, None, ALU.mult))
            for p, x in enumerate(xs):
                link(nc.vector.tensor_scalar(x, x, up[:, p:p + 1], 128.0 - 1e-6, ALU.mult, ALU.min))
                yield nc.vector.tensor_scalar(x, x, 1e-6 - 128.0, down[:, p:p + 1], ALU.max, ALU.mult)

        def three(out_ap, lhi, llo, rhi, rlo, first, last_one):
            nc.tensor.matmul(out_ap, lhi, rhi, start=first, stop=False)
            nc.tensor.matmul(out_ap, lhi, rlo, start=False, stop=False)
            return nc.tensor.matmul(out_ap, llo, rhi, start=False, stop=last_one)

        cst = ExitStack()
        if "A" in phases or "C" in phases:
            CTh = sb("CTh", [P, KC, TILES * P], F16, stack=cst)
            CTl = sb("CTl", [P, KC, TILES * P], F16, stack=cst)
            front("ctx", CTh, CTl, load=load_x)
        env = dict(locals())
        if "A" in phases:
            phase(phase_a)
        if "B" in phases:
            phase(phase_b)
        if "C" in phases:
            phase(phase_c)
        cst.close()
        if "D" in phases:
            phase(phase_d)

        s_out = sem("s_out")
        with nc.Block() as block:
            @block.sync
            def _(sp):
                sp.dma_start(out_tiles, X[:, :, :]).then_inc(s_out, 16)
                sp.wait_ge(s_out, 16)


def phase_a(nc, a, env):
    sem, bank, bank16, X, XTh, XTl, ident, ident16, tg = (env[k] for k in (
        "sem", "bank", "bank16", "X", "XTh", "XTl", "ident", "ident16", "tg"))
    st = ExitStack()

    def sb(name, shape, dt=F32):
        return env["sb"](name, shape, dt, stack=st)

    CTh, CTl = env["CTh"], env["CTl"]
    KV = G0 * HD0
    NEG, ONE = 3 * HD0, 3 * HD0 + 1
    wqh = sb("a_wqh", [P, KC, D], F16)
    wql = sb("a_wql", [P, KC, D], F16)
    woh = sb("a_woh", [P, KC, D], F16)
    wol = sb("a_wol", [P, KC, D], F16)
    wkvh = sb("a_wkvh", [P, KC, 2 * KV], F16)
    wkvl = sb("a_wkvl", [P, KC, 2 * KV], F16)
    env["front"]("ln", XTh, XTl, weights=[
        (a["L0_xattn_Wq"], wqh, wql), (a["L0_xattn_Wo"], woh, wol),
        (a["L0_xattn_Wk"], wkvh[:, :, 0:KV], wkvl[:, :, 0:KV]),
        (a["L0_xattn_Wv"], wkvh[:, :, KV:2 * KV], wkvl[:, :, KV:2 * KV])])

    bq = sb("a_bq", [P, D])
    bkv = sb("a_bkv", [P, 2 * KV])
    bo = sb("a_bo", [P, D])
    m8 = sb("a_m8", [P, 2, S], U8)
    pad8 = sb("a_pad8", [B, S], U8)
    padf = sb("a_padf", [B, S])
    madd = sb("a_madd", [P, 2, S], F16)
    maddT = sb("a_maddT", [P, 2, S], F16)
    pad = sb("a_pad", [P, 2, B])
    q32 = sb("a_q32", [P, 2, D])
    qs = sb("a_qs", [P, 2, H0, STK], F16)
    qT = sb("a_qT", [P, 2, H0 // 2, S], F16)
    k32 = sb("a_k32", [P, 2, KV])
    ks = sb("a_ks", [P, 2, G0, 4, STK], F16)
    kd = ks[:, :, :, 0:4:3, :]
    kT = sb("a_kT", [P, 2, 2 * G0, S], F16)
    v32 = sb("a_v32", [P, 2, KV])
    VW = 2 * HD0 + 1
    vv = sb("a_v", [P, 2, 2, G0, VW], F16)
    mx = sb("a_mx", [P, 2, H0])
    NP = 4
    prob = sb("a_prob", [P, 2, D])
    ph = sb("a_ph", [P, NP, D], F16)
    pl = sb("a_pl", [P, NP, D], F16)
    rec = sb("a_rec", [P, 2, 8])
    oa = sb("a_oa", [P, 2, 8, HD0])
    ob = sb("a_ob", [P, 2, 8, HD0])
    on = sb("a_on", [P, 2, D])
    oTh = sb("a_oTh", [P, 2, KC, P], F16)
    oTl = sb("a_oTl", [P, 2, KC, P], F16)

    k_in, k_ch, k_pad, k_tr, k_m = (sem("k_" + n) for n in ("in", "chain", "pad", "tr", "mask"))
    with nc.Block() as block:
        @block.sync
        def _(sp):
            sp.dma_start(bq[:, :], env["row"](a["L0_xattn_bq"])).then_inc(k_in, 16)
            sp.dma_start(bkv[:, 0:KV], env["row"](a["L0_xattn_bk"])).then_inc(k_in, 16)
            sp.dma_start(bkv[:, KV:2 * KV], env["row"](a["L0_xattn_bv"])).then_inc(k_in, 16)
            sp.dma_start(bo[:, :], env["row"](a["L0_xattn_bo"])).then_inc(k_in, 16)
            sp.dma_start(m8[:, :, :], a["mask_SxS2_bc0"].rearrange("(t p) k -> p t k", p=P)).then_inc(k_in, 16)
            sp.dma_start(pad8[:, :], a["mask_BxS2_bk0"]).then_inc(k_in, 16)

        @block.vector
        def _(dve):
            link = Chain(dve, k_ch)
            nc.vector.memset(qs[:, :, :, :], 0.0)
            nc.vector.memset(ks[:, :, :, :, :], 0.0)
            link(nc.vector.memset(mx[:, :, :], 0.0))
            nc.vector.memset(qs[:, :, :, ONE:ONE + 1], 1.0)
            nc.vector.memset(kd[:, :, :, :, NEG:NEG + 1], 1.0)
            nc.vector.memset(vv[:, :, :, :, HD0:HD0 + 1], 1.0)
            dve.wait_ge(k_in, 96)
            link(nc.vector.tensor_scalar(bq[:, :], bq[:, :], HD0 ** -0.5, None, ALU.mult))
            nc.vector.tensor_scalar(padf[:, :], pad8[:, :], MASKED, None, ALU.mult).then_inc(k_pad, 1)
            nc.vector.tensor_scalar(madd[:, :, :], m8[:, :, :], MASKED, None, ALU.mult).then_inc(k_m, 1)
            dve.wait_ge(k_tr, 1)
            link(nc.vector.tensor_copy(pad[:, :, :], bank[0][:, 0:2 * B].rearrange("p (t b) -> p t b", t=2)))
            dve.wait_ge(k_tr, 2)
            link(nc.vector.tensor_copy(maddT[:, :, :], bank16(1)[:, 0:2 * S].rearrange("p (t q) -> p t q", t=2)))

        @block.tensor
        def _(pe):
            pe.wait_ge(k_pad, 1)
            for t in range(2):
                last = nc.tensor.transpose(bank[0][:, t * B:(t + 1) * B], padf[:, t * P:(t + 1) * P], ident[0:B, 0:B])
            last.then_inc(k_tr, 1)
            pe.wait_ge(k_m, 1)
            for k in range(2):
                for t in range(2):
                    last = nc.tensor.transpose(bank16(1)[:, k * S + t * P:k * S + (t + 1) * P],
                                               madd[:, t, k * P:(k + 1) * P], ident16[:, :])
            last.then_inc(k_tr, 1)

    names = ("Q0", "Q1", "KV0", "KV1", "dq0", "dq1", "dk0", "dk1", "hq0", "hq1", "lq0", "lq1", "hk0", "hk1",
             "lk0", "lk1", "hv0", "hv1", "lv0", "lv1", "tq", "t2", "tk", "cq", "ck", "c2", "S", "M", "nm0", "nm1",
             "ST", "E", "L", "AV", "ON", "To0", "To1", "hO0", "hO1", "lO0", "lO1", "O0", "O1", "x0", "x1", "ch")
    ev = {n: sem("a_" + n) for n in names}
    NS = 2 * G0 * 2
    LAG = 3
    BST, BAV, BS, BM = 0, 2, 4, 6
    PQ, PK = (1, 5), (3, 7)
    TQ, TK = (9, 12), (11, 14)
    FIRST = 15
    NORM = LAG + 4

    def due(n):
        if not FIRST <= n < NS:
            return range(0)
        return range((n - FIRST) * NS // (NS - FIRST), (n + 1 - FIRST) * NS // (NS - FIRST))
    HALF = next(n for n in range(NS) if due(n).stop >= NS // 2 + 3)

    def rounds(eng, first, body):
        first()
        with eng.Fori(0, B // 2 - 1) as i:
            body(2 * i, 0, True)
            body(2 * i + 1, 1, True)
        body(B - 2, 0, True)
        body(B - 1, 1, False)

    with nc.Block() as block:
        @block.tensor
        def _(pe):
            pe.sem_inc(ev["AV"], 4)

            def wait(n, b, count=1, per=1):
                pe.wait_ge(ev[n], b * per + count)

            def project(dst, xh, xl, w_h, w_l, b, tt, n):
                x = bass.ds((2 * b + tt) * P, P)
                for k in range(KC):
                    last = env["three"](dst, xh[:, k, x], xl[:, k, x], w_h[:, k, :], w_l[:, k, :],
                                        k == 0, k == KC - 1)
                last.then_inc(ev[n], 1)

            def q_of(b, tt):
                if tt:
                    wait("dq0", b)
                project(bank[BM][:, :], XTh, XTl, wqh, wql, b, tt, f"Q{tt}")

            def kv_of(b, tt):
                if tt:
                    wait("dk0", b)
                project(bank[BM + 1][:, 0:2 * KV], CTh, CTl, wkvh, wkvl, b, tt, f"KV{tt}")

            def turn_q(b, tt, n):
                for h in range(2):
                    if n == "tq":
                        if tt:
                            wait("ck", b, h + 1, 4)
                        else:
                            wait(("dq1", "dk1")[h], b)
                    elif tt:
                        wait("c2", b, h + 1, 4)
                    else:
                        wait("ck", b, h + 3, 4)
                    for j in range(8):
                        c = qs[:, tt, 16 * h + 2 * j:16 * h + 2 * j + 2, :].rearrange("p h c -> p (h c)")
                        last = nc.tensor.transpose(bank16(BM + h)[:, j * P:(j + 1) * P], c, ident16[:, :])
                    last.then_inc(ev[n], 1)

            def turn_k(b, tt):
                wait(f"lk{tt}", b)
                for h in range(2):
                    wait("cq", b, 2 * tt + h + 1, 4)
                    for j in range(8):
                        c = ks[:, tt, 4 * h + j // 2, 2 * (j % 2):2 * (j % 2) + 2, :].rearrange("p d c -> p (d c)")
                        last = nc.tensor.transpose(bank16(BM + h)[:, j * P:(j + 1) * P], c, ident16[:, :])
                    last.then_inc(ev["tk"], 1)

            def scores(b, par, m):
                tt, g, half = m // 16, m // 2 % G0, m % 2
                bk = bank[BS + m % 2]
                wait("M", b, m + 1, NS)
                if m < 2:
                    wait(f"x{m}", b)
                if m == 0:
                    wait("ck", b, 4, 4)
                    wait("cq", b, 4, 4)
                nc.tensor.matmul(bk[:, :].rearrange("p (r k) -> p r k", r=2), ident16[:, :],
                                 madd[:, tt, :].unsqueeze(1).broadcast_to([P, 2, S]), start=True, stop=False)
                for r in range(2):
                    last = nc.tensor.matmul(bk[:, r * S:(r + 1) * S], qT[:, par, 2 * g + r, tt * P:(tt + 1) * P],
                                            kT[:, par, 2 * g + half, :], start=False, stop=(r == 1))
                last.then_inc(ev["S"], 1)

            def second(b, tt):
                wait(f"nm{tt}", b)
                turn_q(b, tt, "t2")

            def turned_scores(b, par, n):
                g, half, kc = n // 4, n // 2 % 2, n % 2
                bk = bank[BST + n % 2]
                wait("E", b, n + 1, NS)
                nc.tensor.matmul(bk[:, :].rearrange("p (r k) -> p r k", r=2), ident16[:, :],
                                 maddT[:, kc, :].unsqueeze(1).broadcast_to([P, 2, S]), start=True, stop=False)
                nc.tensor.matmul(bk[:, :], kT[:, par, 2 * g + half, kc * P:(kc + 1) * P],
                                 qT[:, par, 2 * g:2 * g + 2, :].rearrange("p r q -> p (r q)"),
                                 start=False, stop=True).then_inc(ev["ST"], 1)

            def times_v(b, par, n):
                g, half, kc = n // 4, n // 2 % 2, n % 2
                if n % 4 == 0:
                    wait("ON", b, g + 1, G0)
                wait("L", b, n + 3, NS)
                for r in range(2):
                    for qt in range(2):
                        c = ((qt * 2 + r) * 2 + half) * VW
                        q = slice((2 * r + qt) * P, (2 * r + qt + 1) * P)
                        first = n % 4 == 0 and r == 0 and qt == 0
                        nc.tensor.matmul(bank[BAV + g % 2][:, c:c + VW], ph[:, n % NP, q], vv[:, par, kc, g, :],
                                         start=first, stop=False, skip_group_check=True)
                        last = nc.tensor.matmul(bank[BAV + g % 2][:, c:c + HD0 + 1], pl[:, n % NP, q],
                                                vv[:, par, kc, g, 0:HD0 + 1], start=False, stop=(kc == 1),
                                                skip_group_check=True)
                last.then_inc(ev["AV"], 1)

            def output(b):
                wait("ch", b, 2 * G0, 2 * G0)
                for tt in range(2):
                    for k in range(KC):
                        last = nc.tensor.transpose(bank[BS + tt][:, k * P:(k + 1) * P], on[:, tt, k * P:(k + 1) * P],
                                                   ident[:, :])
                    last.then_inc(ev[f"To{tt}"], 1)
                for tt in range(2):
                    wait(f"lO{tt}", b)
                    for k in range(KC):
                        last = env["three"](bank[BS + tt][:, :], oTh[:, tt, k, :], oTl[:, tt, k, :],
                                            woh[:, k, :], wol[:, k, :], k == 0, k == KC - 1)
                    last.then_inc(ev[f"O{tt}"], 1)

            def first():
                for tt in range(2):
                    q_of(0, tt)
                    kv_of(0, tt)
                for tt in range(2):
                    wait(f"lq{tt}", 0)
                    turn_q(0, tt, "tq")
                    turn_k(0, tt)
                for m in range(NS):
                    scores(0, 0, m)
                second(0, 0)
                second(0, 1)

            def body(b, par, more):
                nx = b + 1
                wait("c2", b, 4, 4)
                wait("lv0", b)
                wait("lv1", b)
                for n in range(NS + LAG):
                    if n < NS:
                        turned_scores(b, par, n)
                    if n >= LAG:
                        times_v(b, par, n - LAG)
                    if not more:
                        continue
                    for tt in range(2):
                        if n == PQ[tt]:
                            q_of(nx, tt)
                        if n == PK[tt]:
                            kv_of(nx, tt)
                        if n == TQ[tt]:
                            wait(f"lq{tt}", nx)
                            turn_q(nx, tt, "tq")
                        if n == TK[tt]:
                            turn_k(nx, tt)
                    for m in due(n - 1):
                        scores(nx, 1 - par, m)
                    if n == HALF:
                        second(nx, 0)
                if more:
                    second(nx, 1)
                output(b)
            rounds(pe, first, body)

        @block.scalar
        def _(act):
            act.sem_inc(ev["E"], 2)

            def wait(n, b, count=1, per=1):
                act.wait_ge(ev[n], b * per + count)

            def high_q(b, tt):
                wait(f"dq{tt}", b)
                q3 = q32[:, tt, :].rearrange("p (h c) -> p h c", h=H0)
                nc.scalar.activation(qs[:, tt, :, 0:HD0], q3, ACT.Copy)
                nc.scalar.activation(qs[:, tt, :, HD0:2 * HD0], q3, ACT.Copy).then_inc(ev[f"hq{tt}"], 1)

            def high_kv(b, par, tt):
                wait(f"dk{tt}", b)
                k4 = k32[:, tt, :].rearrange("p (g c) -> p g c", g=G0).unsqueeze(2).broadcast_to([P, G0, 2, HD0])
                nc.scalar.activation(vv[:, par, tt, :, 0:HD0], v32[:, tt, :].rearrange("p (g c) -> p g c", g=G0),
                                     ACT.Copy).then_inc(ev[f"hv{tt}"], 1)
                nc.scalar.activation(kd[:, tt, :, :, 0:HD0], k4, ACT.Copy)
                nc.scalar.activation(kd[:, tt, :, :, 2 * HD0:3 * HD0], k4, ACT.Copy).then_inc(ev[f"hk{tt}"], 1)

            def take_second(b, par, tt):
                for h in range(2):
                    wait("t2", b, 2 * tt + h + 1, 4)
                    nc.scalar.activation(qT[:, par, 8 * h:8 * h + 8, tt * P:(tt + 1) * P],
                                         bank16(BM + h).rearrange("p (j q) -> p j q", j=8), ACT.Copy)\
                      .then_inc(ev["c2"], 1)

            def first():
                for tt in range(2):
                    high_q(0, tt)
                    high_kv(0, 0, tt)
                take_second(0, 0, 0)
                take_second(0, 0, 1)

            def body(b, par, more):
                for n in range(NS):
                    wait("ST", b, n + 1, NS)
                    wait("AV", b, n + 1, NS)
                    wait("L", b, n + 1, NS)
                    nc.scalar.activation(ph[:, n % NP, :], bank[BST + n % 2][:, :], ACT.Exp)
                    nc.scalar.activation(prob[:, n % 2, :], bank[BST + n % 2][:, :], ACT.Exp).then_inc(ev["E"], 1)
                    if not more:
                        continue
                    for tt in range(2):
                        if n == PQ[tt] + 2:
                            high_q(b + 1, tt)
                        if n == PK[tt] + 2:
                            high_kv(b + 1, 1 - par, tt)
                    if n == min(HALF + 1, NS - 1):
                        take_second(b + 1, 1 - par, 0)
                if more:
                    take_second(b + 1, 1 - par, 1)
                for tt in range(2):
                    wait(f"To{tt}", b)
                    nc.scalar.activation(oTh[:, tt], bank[BS + tt][:, :].rearrange("p (k c) -> p k c", k=KC), ACT.Copy)\
                      .then_inc(ev[f"hO{tt}"], 1)
            rounds(act, first, body)

        @block.gpsimd
        def _(pool):
            pool.sem_inc(ev["L"], 2)

            def body(b, par, more):
                for n in range(NS):
                    pool.wait_ge(ev["E"], b * NS + n + 3)
                    nc.gpsimd.tensor_tensor(pl[:, n % NP, :], prob[:, n % 2, :], ph[:, n % NP, :],
                                            ALU.subtract).then_inc(ev["L"], 1)
            rounds(pool, lambda: None, body)

        @block.vector
        def _(dve):
            for n, credit in (("ON", 2), ("x0", 2), ("x1", 2), ("M", 2)):
                dve.sem_inc(ev[n], credit)

            def wait(n, b, count=1, per=1):
                dve.wait_ge(ev[n], b * per + count)

            PER = 2 * G0

            def bias_q(b, tt):
                wait(f"Q{tt}", b)
                nc.vector.memset(qs[:, tt, :, NEG:NEG + 1], 0.0)
                nc.vector.scalar_tensor_tensor(out=q32[:, tt, :], in0=bank[BM][:, :], scalar=HD0 ** -0.5,
                                               in1=bq[:, :], op0=ALU.mult, op1=ALU.add).then_inc(ev[f"dq{tt}"], 1)

            def bias_kv(b, tt):
                wait(f"KV{tt}", b)
                nc.vector.tensor_copy(kd[:, tt, :, :, ONE],
                                      pad[:, tt, bass.ds(b, 1)].unsqueeze(1).broadcast_to([P, G0, 2]))
                nc.vector.tensor_tensor(v32[:, tt, :], bank[BM + 1][:, KV:2 * KV], bkv[:, KV:2 * KV], ALU.add)
                nc.vector.tensor_tensor(k32[:, tt, :], bank[BM + 1][:, 0:KV], bkv[:, 0:KV],
                                        ALU.add).then_inc(ev[f"dk{tt}"], 1)

            def low_q(b, tt):
                wait(f"hq{tt}", b)
                nc.vector.tensor_tensor(qs[:, tt, :, 2 * HD0:3 * HD0],
                                        q32[:, tt, :].rearrange("p (h c) -> p h c", h=H0),
                                        qs[:, tt, :, 0:HD0], ALU.subtract).then_inc(ev[f"lq{tt}"], 1)

            def low_kv(b, par, tt):
                wait(f"hk{tt}", b)
                k4 = k32[:, tt, :].rearrange("p (g c) -> p g c", g=G0).unsqueeze(2).broadcast_to([P, G0, 2, HD0])
                nc.vector.tensor_tensor(kd[:, tt, :, :, HD0:2 * HD0], k4, kd[:, tt, :, :, 0:HD0],
                                        ALU.subtract).then_inc(ev[f"lk{tt}"], 1)
                wait(f"hv{tt}", b)
                nc.vector.tensor_tensor(vv[:, par, tt, :, HD0 + 1:VW], v32[:, tt, :].rearrange("p (g c) -> p g c", g=G0),
                                        vv[:, par, tt, :, 0:HD0], ALU.subtract).then_inc(ev[f"lv{tt}"], 1)

            def take(b, par, tt, what):
                dst, n, c = (qT, "tq", "cq") if what == "q" else (kT, "tk", "ck")
                for h in range(2):
                    wait(n, b, 2 * tt + h + 1, 4)
                    nc.vector.tensor_copy(dst[:, par, 8 * h:8 * h + 8, tt * P:(tt + 1) * P],
                                          bank16(BM + h).rearrange("p (j q) -> p j q", j=8)).then_inc(ev[c], 1)

            def maxima(b, m):
                tt, g, half = m // 16, m // 2 % G0, m % 2
                wait("S", b, m + 1, NS)
                nc.vector.tensor_reduce(mx[:, tt, 4 * g + half:4 * g + half + 3:2],
                                        bank[BS + m % 2][:, :].rearrange("p (r k) -> p r k", r=2), AX_X, ALU.max)\
                  .then_inc(ev["M"], 1)
                if m % 16 == 15:
                    wait("M", b, m + 3, NS)
                    nc.vector.tensor_scalar(qs[:, tt, :, NEG], mx[:, tt, :], -1.0, None, ALU.mult)\
                      .then_inc(ev[f"nm{tt}"], 1)

            def normalise(link, b, g):
                wait("AV", b, 4 * g + 4 + NP, NS)
                o = bank[BAV + g % 2][:, 0:8 * VW].rearrange("p (s c) -> p s c", s=8)
                nc.vector.reciprocal(rec[:, g % 2, :], o[:, :, HD0])
                link(nc.vector.tensor_copy(oa[:, g % 2], o[:, :, HD0 + 1:VW]))
                nc.vector.tensor_tensor(ob[:, g % 2], o[:, :, 0:HD0], oa[:, g % 2], ALU.add).then_inc(ev["ON"], 1)
                wait("ON", b, g + 3, G0)
                link(nc.vector.tensor_tensor(on[:, :, g * 4 * HD0:(g + 1) * 4 * HD0].rearrange(
                    "p t (h c) -> p t h c", h=4), ob[:, g % 2].rearrange("p (t h) c -> p t h c", t=2),
                    rec[:, g % 2, :].rearrange("p (t h) -> p t h", t=2).unsqueeze(3)
                    .broadcast_to([P, 2, 4, HD0]), ALU.mult))

            def first():
                for tt in range(2):
                    bias_q(0, tt)
                    bias_kv(0, tt)
                    low_q(0, tt)
                    low_kv(0, 0, tt)
                for tt in range(2):
                    take(0, 0, tt, "q")
                    take(0, 0, tt, "k")
                for m in range(NS):
                    maxima(0, m)

            def body(b, par, more):
                link = Chain(dve, ev["ch"], b * PER)
                nx = b + 1
                for n in range(NS):
                    if n >= NORM and (n - NORM) % 4 == 0:
                        normalise(link, b, (n - NORM) // 4)
                    if not more:
                        continue
                    for tt in range(2):
                        if n == PQ[tt]:
                            bias_q(nx, tt)
                        if n == PK[tt]:
                            low_q(nx, tt)
                            bias_kv(nx, tt)
                        if n == PK[tt] + 2:
                            low_kv(nx, 1 - par, tt)
                    for tt in range(2):
                        if n == TQ[tt]:
                            take(nx, 1 - par, tt, "q")
                        if n == TK[tt]:
                            take(nx, 1 - par, tt, "k")
                    for m in due(n):
                        maxima(nx, m)
                normalise(link, b, G0 - 1)
                for tt in range(2):
                    wait(f"hO{tt}", b)
                    nc.vector.tensor_tensor(oTl[:, tt], bank[BS + tt][:, :].rearrange("p (k c) -> p k c", k=KC),
                                            oTh[:, tt], ALU.subtract).then_inc(ev[f"lO{tt}"], 1)
                for tt in range(2):
                    wait(f"O{tt}", b)
                    nc.vector.tensor_tensor(on[:, tt, :], bank[BS + tt][:, :], bo[:, :], ALU.add)\
                      .then_inc(ev[f"x{tt}"], 1)
                    wait(f"x{tt}", b, 3)
                    nc.vector.scalar_tensor_tensor(out=X[:, 2 * b + tt, :], in0=on[:, tt, :], scalar=tg[:, 0:1],
                                                   in1=X[:, 2 * b + tt, :], op0=ALU.mult, op1=ALU.add)
                assert link.n == PER, link.n
            rounds(dve, first, body)
    st.close()


def phase_b(nc, a, env):
    sem, bank, bank16, X, XTh, XTl, ident, ident16, tg = (env[k] for k in (
        "sem", "bank", "bank16", "X", "XTh", "XTl", "ident", "ident16", "tg"))
    st = ExitStack()

    def sb(name, shape, dt=F32):
        return env["sb"](name, shape, dt, stack=st)

    NH = F0 // D
    HC = F0 // P
    wfc = sb("b_wfc", [P, NH, KC, D], F16)
    wpj = sb("b_wpj", [P, HC, D], F16)
    scale = sb("b_scale", [P, 8])

    wst = ExitStack()

    def wb(name, shape, dt=F32):
        return env["sb"](name, shape, dt, stack=wst)

    NUNIT = 2 * NH
    stage = wb("b_stage", [P, NUNIT, 4, D])
    part = wb("b_part", [P, NUNIT])
    sums = wb("b_sums", [P, 2])
    ones = wb("b_ones", [P, P])
    t_in, t_abs, t_ch, t_part, t_tot, t_low, t_use, t_tr, t_cp = (sem("t_" + n) for n in (
        "in", "abs", "ch", "part", "tot", "below", "use", "tr", "cp"))
    jst = ExitStack()
    junk = env["sb"]("b_junk", [P, 4 * D], F16, stack=jst)
    PER = NUNIT // (TILES // env["FT"])

    def unit(u):
        if u < NH:
            return a["L0_ffn_w_fc"][u * D:(u + 1) * D, :].rearrange("(r p) c -> p r c", p=P)
        return a["L0_ffn_w_proj"][:, (u - NH) * D:(u - NH + 1) * D].rearrange("(r p) c -> p r c", p=P)

    def load(sp):
        for u in range(NUNIT):
            if u and u % PER == 0:
                sp.wait_ge(t_in, 16 * u)
            sp.dma_start(stage[:, u, :, :], unit(u)).then_inc(t_in, 16)

    def magnitudes(act, i):
        act.wait_ge(t_in, 16 * PER * (i + 1))
        for u in range(PER):
            act.wait_ge(t_abs, PER * i + u + 1)
            nc.scalar.activation(junk[:, :], stage[:, PER * i + u, :, :].rearrange("p r c -> p (r c)"), ACT.Abs,
                                 accum_out=part[:, bass.ds(PER * i + u, 1)]).then_inc(t_abs, 1)

    with nc.Block() as block:
        @block.scalar
        def _(act):
            act.sem_inc(t_abs, 1)
    env["front"]("bit", XTh, XTl, load, magnitudes)
    jst.close()
    below = wb("b_below", [P, 2, 4, D], U8)
    tern = wb("b_tern", [P, 2, 4, D], F16)
    OWN = (0, 2, 4, 6)

    def low(u, eng):
        return eng.tensor_scalar(below[:, u % 2, :, :], stage[:, u, :, :], scale[:, 4 + u // NH:5 + u // NH], None,
                                 ALU.is_lt)

    with nc.Block() as block:
        @block.gpsimd
        def _(pool):
            pool.wait_ge(t_low, 1)
            for u in OWN:
                if u >= 2:
                    pool.wait_ge(t_use, u - 1)
                low(u, nc.gpsimd).then_inc(t_low, 1)

        @block.scalar
        def _(act):
            for u in range(NUNIT):
                for h in range(2):
                    act.wait_ge(t_tr, 2 * u + h + 1)
                    if u < NH:
                        dst = wfc[:, u, 2 * h:2 * h + 2, :]
                    else:
                        dst = wpj[:, KC * (u - NH) + 2 * h:KC * (u - NH) + 2 * h + 2, :]
                    nc.scalar.activation(dst, bank16(h).rearrange("p (k c) -> p k c", k=2),
                                         ACT.Copy).then_inc(t_cp, 1)

        @block.vector
        def _(dve):
            link = Chain(dve, t_ch)
            link(nc.vector.memset(ones[:, :], 1.0))
            nc.vector.reduce_sum(sums[:, :], part[:, :].rearrange("p (m u) -> p m u", m=2), AX_X).then_inc(t_part, 1)
            dve.wait_ge(t_tot, 1)
            link(nc.vector.tensor_scalar(scale[:, 0:2], bank[4][:, 0:2], 1.0 / (F0 * D), None, ALU.mult))
            link(nc.vector.tensor_scalar(scale[:, 2:4], scale[:, 0:2], 1e-6, 0.5, ALU.add, ALU.mult))
            link(nc.vector.tensor_scalar(scale[:, 4:6], scale[:, 2:4], -1.0, None, ALU.mult))
            nc.vector.tensor_tensor(scale[:, 6:7], scale[:, 1:2], tg[:, 2:3], ALU.mult).then_inc(t_low, 1)
            for u in range(NUNIT):
                m = u // NH
                if u in OWN:
                    dve.wait_ge(t_low, 2 + OWN.index(u))
                else:
                    if u >= 2:
                        dve.wait_ge(t_use, u - 1)
                    link(low(u, nc.vector))
                if u >= 2:
                    dve.wait_ge(t_tr, 2 * (u - 1))
                nc.vector.scalar_tensor_tensor(out=tern[:, u % 2, :, :], in0=stage[:, u, :, :],
                                               scalar=scale[:, 2 + m:3 + m], in1=below[:, u % 2, :, :],
                                               op0=ALU.is_gt, op1=ALU.subtract).then_inc(t_use, 1)

        @block.tensor
        def _(pe):
            pe.wait_ge(t_part, 1)
            nc.tensor.matmul(bank[4][:, 0:2], ones[:, :], sums[:, :], start=True, stop=True).then_inc(t_tot, 1)
            for u in range(NUNIT):
                pe.wait_ge(t_use, u + 1)
                for h in range(2):
                    if u:
                        pe.wait_ge(t_cp, 2 * (u - 1) + h + 1)
                    for k in range(2):
                        for r in range(4):
                            last = nc.tensor.transpose(bank16(h)[:, (4 * k + r) * P:(4 * k + r + 1) * P],
                                                       tern[:, u % 2, r, (2 * h + k) * P:(2 * h + k + 1) * P],
                                                       ident16[:, :])
                    last.then_inc(t_tr, 1)
    wst.close()

    h32 = sb("b_h", [P, 2, F0])
    xn = sb("b_xn", [P, 2, F0])
    hTh = sb("b_hTh", [P, 2, HC, P], F16)
    hTl = sb("b_hTl", [P, 2, HC, P], F16)
    stats = sb("b_stats", [P, 2, NH, 6])
    mv = sb("b_mv", [P, 2, 2])
    ve = sb("b_ve", [P, 2, 1])
    rs = sb("b_rs", [P, 2, 2])
    q = sb("b_q", [P, 2, 4])
    mhalf = sb("b_mh", [P, 1])
    hold = sb("b_hold", [P, 1])
    b_up, b_ge, b_ch, b_var, b_rs, b_nm, b_xn, b_q, b_tr, b_hi, b_lo, b_dn, b_out, b_mh = (sem("b_" + n) for n in (
        "up", "gelu", "chain", "var", "rstd", "nmean", "norm", "quant", "tr", "hi", "lo", "down", "out", "mh"))
    UP, TR, ACC = 0, 2, 4

    def rounds(eng, step):
        with eng.Fori(0, TILES // 2 - 1) as t:
            step(2 * t, 0)
            step(2 * t + 1, 1)
        step(TILES - 2, 0, 1)
        step(TILES - 1, 1, 0)

    with nc.Block() as block:
        @block.gpsimd
        def _(pool):
            nc.gpsimd.memset(mhalf[:, :], -0.5).then_inc(b_mh, 1)
            pool.wait_ge(b_mh, 1)
            with pool.Fori(0, TILES // 2) as i:
                for p in range(2):
                    pool.wait_ge(b_var, 2 * i + p + 1)
                    nc.gpsimd.tensor_tensor(rs[:, p, 0:1], ve[:, p, :], mhalf[:, :], ALU.pow).then_inc(b_rs, 1)

        @block.tensor
        def _(pe):
            pe.sem_inc(b_dn, 2)
            pe.sem_inc(b_tr, 2 * KC)
            def up(n, i):
                for h in range(NH):
                    pe.wait_ge(b_ge, NH * n + h + 1)
                    for k in range(KC):
                        x = bass.ds(n * P, P)
                        nc.tensor.matmul(bank[UP + h % 2][:, :], XTh[:, k, x], wfc[:, h, k, :],
                                         start=(k == 0), stop=False)
                        last = nc.tensor.matmul(bank[UP + h % 2][:, :], XTl[:, k, x], wfc[:, h, k, :],
                                                start=False, stop=(k == KC - 1))
                    last.then_inc(b_up, 1)

            def turn(n, i):
                pe.wait_ge(b_q, n + 1)
                for g in range(KC):
                    pe.wait_ge(b_lo, KC * n + g + 1)
                    for r in range(4):
                        c = (4 * g + r) * P
                        last = nc.tensor.transpose(bank[TR + g % 2][:, r * P:(r + 1) * P],
                                                   xn[:, i % 2, c:c + P], ident[:, :])
                    last.then_inc(b_tr, 1)

            def down(n, i):
                pe.wait_ge(b_lo, KC * n + KC + 2)
                pe.wait_ge(b_out, n + 1)
                for c in range(HC):
                    nc.tensor.matmul(bank[ACC + i % 2][:, :], hTh[:, i % 2, c, :], wpj[:, c, :],
                                     start=(c == 0), stop=False)
                    last = nc.tensor.matmul(bank[ACC + i % 2][:, :], hTl[:, i % 2, c, :], wpj[:, c, :],
                                            start=False, stop=(c == HC - 1))
                last.then_inc(b_dn, 1)
            up(0, 0)
            up(1, 1)
            turn(0, 0)

            def step(n, i, ahead=2):
                if ahead > 1:
                    up(n + 2, i)
                down(n, i)
                if ahead:
                    turn(n + 1, 1 - i)
            rounds(pe, step)

        @block.scalar
        def _(act):
            act.sem_inc(b_ge, 2)
            def gelu(n, i, pieces):
                for h in pieces:
                    act.wait_ge(b_up, NH * n + h + 1)
                    nc.scalar.activation(h32[:, i % 2, h * D:(h + 1) * D], bank[UP + h % 2][:, :], ACT.Gelu,
                                         scale=scale[:, 0:1]).then_inc(b_ge, 1)

            def norm(n, i):
                act.wait_ge(b_nm, n + 1)
                act.wait_ge(b_tr, KC * n + KC)
                nc.scalar.activation(xn[:, i % 2, :], h32[:, i % 2, :], ACT.Identity, bias=rs[:, i % 2, 1:2],
                                     scale=rs[:, i % 2, 0:1]).then_inc(b_xn, 1)

            def high(n, i):
                act.wait_ge(b_dn, n + 1)
                for g in range(KC):
                    act.wait_ge(b_tr, KC * n + g + 1 + 2 * KC)
                    nc.scalar.activation(hTh[:, i % 2, 4 * g:4 * g + 4, :],
                                         bank[TR + g % 2][:, :].rearrange("p (r c) -> p r c", r=4),
                                         ACT.Copy).then_inc(b_hi, 1)
            gelu(0, 0, range(NH))
            gelu(1, 1, range(NH // 2))
            norm(0, 0)
            gelu(1, 1, range(NH // 2, NH))
            high(0, 0)

            def step(n, i, ahead=2):
                if ahead > 1:
                    gelu(n + 2, i, range(NH // 2))
                if ahead:
                    norm(n + 1, 1 - i)
                if ahead > 1:
                    gelu(n + 2, i, range(NH // 2, NH))
                if ahead:
                    high(n + 1, 1 - i)
            rounds(act, step)

        @block.vector
        def _(dve):
            dve.sem_inc(b_lo, 2)
            dve.sem_inc(b_out, 2)
            link = Chain(dve, b_ch)
            PER = NH + 1 + 5

            def stat(n, i, pieces):
                for h in pieces:
                    dve.wait_ge(b_ge, NH * n + h + 3)
                    link(nc.vector.bn_stats(stats[:, i % 2, h, :], h32[:, i % 2, h * D:(h + 1) * D]))

            def moments(n, i):
                nc.vector.memset(hold[:, :], 0.0)
                link(nc.vector.bn_aggr(mv[:, i % 2, :], stats[:, i % 2, :, :].rearrange("p h s -> p (h s)")))
                nc.vector.tensor_scalar(ve[:, i % 2, :], mv[:, i % 2, 1:2], 1e-6, None, ALU.add).then_inc(b_var, 1)
                dve.wait_ge(b_rs, n + 1)
                nc.vector.scalar_tensor_tensor(out=rs[:, i % 2, 1:2], in0=mv[:, i % 2, 0:1], scalar=-1.0,
                                               in1=rs[:, i % 2, 0:1], op0=ALU.mult, op1=ALU.mult).then_inc(b_nm, 1)

            def quant(n, i):
                dve.wait_ge(b_xn, n + 1)
                next(env["quantise"](link, [xn[:, i % 2, :]], q[:, i % 2, :])).then_inc(b_q, 1)

            def low(n, i):
                for g in range(KC):
                    dve.wait_ge(b_hi, KC * n + g + 1)
                    nc.vector.tensor_tensor(hTl[:, i % 2, 4 * g:4 * g + 4, :],
                                            bank[TR + g % 2][:, :].rearrange("p (r c) -> p r c", r=4),
                                            hTh[:, i % 2, 4 * g:4 * g + 4, :], ALU.subtract).then_inc(b_lo, 1)

            def result(n, i):
                dve.wait_ge(b_dn, n + 3)
                nc.vector.scalar_tensor_tensor(out=X[:, n, :], in0=bank[ACC + i % 2][:, :], scalar=scale[:, 6:7],
                                               in1=X[:, n, :], op0=ALU.mult, op1=ALU.add).then_inc(b_out, 1)
            stat(0, 0, range(NH))
            moments(0, 0)
            stat(1, 1, range(NH // 2))
            quant(0, 0)
            stat(1, 1, range(NH // 2, NH))
            moments(1, 1)
            low(0, 0)
            before = link.n

            def step(n, i, ahead=2):
                link.start(before + PER * n)
                if ahead > 1:
                    stat(n + 2, i, range(NH // 2))
                if ahead:
                    quant(n + 1, 1 - i)
                if ahead > 1:
                    stat(n + 2, i, range(NH // 2, NH))
                    moments(n + 2, i)
                if ahead:
                    low(n + 1, 1 - i)
                result(n, i)
                assert ahead < 2 or link.n == PER, link.n
            rounds(dve, step)
    st.close()


def phase_c(nc, a, env):
    sem, bank, bank16, X, XTh, XTl, ident, ident16, tg = (env[k] for k in (
        "sem", "bank", "bank16", "X", "XTh", "XTl", "ident", "ident16", "tg"))
    st = ExitStack()

    def sb(name, shape, dt=F32):
        return env["sb"](name, shape, dt, stack=st)

    CTh, CTl = env["CTh"], env["CTl"]
    NW = 5
    WQ, WG, WK, WV, WO = range(NW)
    wh = sb("c_wh", [P, NW, KC, D], F16)
    wl = sb("c_wl", [P, NW, KC, D], F16)
    wkv = a["L1_xattn_Wkv"]
    source = {WQ: a["L1_xattn_Wq"], WG: a["L1_xattn_Wg"], WK: wkv[0:D, :], WV: wkv[D:2 * D, :], WO: a["L1_xattn_Wo"]}
    env["front"]("ln", XTh, XTl, weights=[(source[w], wh[:, w], wl[:, w]) for w in range(NW)])

    bg = sb("c_bg", [P, D])
    blocks = sb("c_blocks", [P, P])
    heads = sb("c_heads", [P, 4])
    GPH = P // HD1
    ek = sb("c_ek", [P, 2, D])
    kk = sb("c_k", [P, 2, D])
    vv = sb("c_v", [P, 2, D])
    eq = sb("c_eq", [P, 2, D])
    qq = sb("c_q", [P, 2, D])
    gt = sb("c_gt", [P, 2, D])
    kv = sb("c_kv", [P, KC, P])
    ks = sb("c_ks", [P, KC, GPH])
    ksr = sb("c_ksr", [P, KC])
    onec = sb("c_one", [P, 1])
    den = sb("c_den", [P, 2, H1])
    og = sb("c_og", [P, 2, D])
    oTh = sb("c_oTh", [P, 2, KC, P], F16)
    oTl = sb("c_oTl", [P, 2, KC, P], F16)
    T = B

    c_in = sem("c_in")
    c_cst = sem("c_const")
    names = ("K0", "K1", "V0", "V1", "Q0", "Q1", "G0", "G1",
             "eK0", "eK1", "eQ0", "eQ1", "tG0", "tG1", "cV0", "cV1", "lG0", "lG1",
             "pK0", "pK1", "pQ0", "pQ1",
             "SUM", "mSUM", "ATT0", "ATT1", "OG0", "OG1", "T0", "T1", "hT0", "hT1", "lT0", "lT1", "O0", "O1",
             "X0", "X1", "ch")
    ev = {n: sem("c_" + n) for n in names}

    with nc.Block() as block:
        @block.sync
        def _(sp):
            sp.dma_start(bg[:, :], env["row"](a["L1_xattn_bg"])).then_inc(c_in, 16)

        @block.gpsimd
        def _(pool):
            nc.gpsimd.memset(onec[:, :], 1.0).then_inc(c_cst, 1)

        @block.vector
        def _(dve):
            link = Chain(dve, ev["ch"])
            link(nc.vector.reduce_sum(heads[:, :], ident[:, :].rearrange("p (h c) -> p h c", h=GPH), AX_X))
            link(nc.vector.tensor_copy(blocks[:, :].rearrange("p (h c) -> p h c", h=GPH),
                                       heads[:, :].unsqueeze(2).broadcast_to([P, GPH, HD1])))

    def rounds(body, tail):
        def go(eng):
            body(0, False)
            with eng.Fori(0, T - 1) as i:
                body(i + 1, True)
            tail(T - 1)
        return go

    with nc.Block() as block:
        @block.tensor
        def _(pe):
            pe.wait_ge(c_cst, 1)

            def wait(n, b):
                pe.wait_ge(ev[n], b + 1)

            def project(dst, xh, xl, w, b, tt, n):
                x = bass.ds((2 * b + tt) * P, P)
                for k in range(KC):
                    last = env["three"](dst, xh[:, k, x], xl[:, k, x], wh[:, w, k, :], wl[:, w, k, :],
                                        k == 0, k == KC - 1)
                last.then_inc(ev[n], 1)

            def turn(b):
                for tt in range(2):
                    wait(f"OG{tt}", b)
                    for k in range(KC):
                        last = nc.tensor.transpose(bank[4 + tt][:, k * P:(k + 1) * P],
                                                   og[:, tt, k * P:(k + 1) * P], ident[:, :])
                    last.then_inc(ev[f"T{tt}"], 1)

            def output(b):
                for tt in range(2):
                    wait(f"lT{tt}", b)
                    for k in range(KC):
                        last = env["three"](bank[4 + tt][:, :], oTh[:, tt, k, :], oTl[:, tt, k, :],
                                            wh[:, WO, k, :], wl[:, WO, k, :], k == 0, k == KC - 1)
                    last.then_inc(ev[f"O{tt}"], 1)

            def body(b, more):
                for tt in range(2):
                    if more:
                        wait("mSUM", b - 1)
                    project(bank[tt][:, :], CTh, CTl, WK, b, tt, f"K{tt}")
                if more:
                    turn(b - 1)
                for tt in range(2):
                    project(bank[2 + tt][:, :], CTh, CTl, WV, b, tt, f"V{tt}")
                if more:
                    output(b - 1)
                for n in ("pK0", "pK1", "cV0", "cV1"):
                    wait(n, b)
                for c in range(KC):
                    for tt in range(2):
                        nc.tensor.matmul(bank[0][:, c * P:(c + 1) * P], kk[:, tt, c * P:(c + 1) * P],
                                         vv[:, tt, c * P:(c + 1) * P], start=(tt == 0), stop=(tt == 1))
                for c in range(KC):
                    for tt in range(2):
                        last = nc.tensor.matmul(bank[1][:, c:c + 1], kk[:, tt, c * P:(c + 1) * P], onec[:, :],
                                                start=(tt == 0), stop=(tt == 1))
                last.then_inc(ev["SUM"], 1)
                for half in range(2):
                    if more:
                        wait(f"X{half}", b - 1)
                    for oc in range(2):
                        o = (2 * half + oc) * P
                        for k in range(KC):
                            x = bass.ds(2 * b * P, 2 * P)
                            last = env["three"](bank[4 + half][:, oc * 2 * P:(oc + 1) * 2 * P],
                                                wh[:, WQ, k, o:o + P], wl[:, WQ, k, o:o + P],
                                                XTh[:, k, x], XTl[:, k, x], k == 0, k == KC - 1)
                    last.then_inc(ev[f"Q{half}"], 1)
                for tt in range(2):
                    project(bank[6 + tt][:, :], XTh, XTl, WG, b, tt, f"G{tt}")
                for n in ("mSUM", "pQ0", "pQ1"):
                    wait(n, b)
                for tt in range(2):
                    wait(f"lG{tt}", b)
                    for c in range(KC):
                        qT = qq[:, c // 2, (c % 2) * 2 * P + tt * P:(c % 2) * 2 * P + (tt + 1) * P]
                        nc.tensor.matmul(bank[2 + tt][:, c * P:(c + 1) * P], qT, kv[:, c, :], start=True, stop=True)
                    for c in range(KC):
                        qT = qq[:, c // 2, (c % 2) * 2 * P + tt * P:(c % 2) * 2 * P + (tt + 1) * P]
                        last = nc.tensor.matmul(bank[6 + tt][:, c * GPH:(c + 1) * GPH], qT, ks[:, c, :],
                                                start=True, stop=True)
                    last.then_inc(ev[f"ATT{tt}"], 1)

            def tail(b):
                turn(b)
                output(b)
            rounds(body, tail)(pe)

        @block.scalar
        def _(act):
            def step(n, b, dst, src, then, func=ACT.Copy, scale=1.0):
                for tt in range(2):
                    act.wait_ge(ev[f"{n}{tt}"], b + 1)
                    nc.scalar.activation(dst(tt), src(tt), func, scale=scale).then_inc(ev[f"{then}{tt}"], 1)

            def high(b):
                step("T", b, lambda tt: oTh[:, tt], lambda tt: bank[4 + tt][:, :].rearrange("p (k c) -> p k c", k=KC),
                     "hT")

            def body(b, more):
                step("K", b, lambda tt: ek[:, tt, :], lambda tt: bank[tt][:, :], "eK", ACT.Exp)
                if more:
                    high(b - 1)
                step("V", b, lambda tt: vv[:, tt, :], lambda tt: bank[2 + tt][:, :], "cV")
                step("Q", b, lambda tt: eq[:, tt, :], lambda tt: bank[4 + tt][:, :], "eQ", ACT.Exp)
                step("lG", b, lambda tt: gt[:, tt, :], lambda tt: gt[:, tt, :], "tG", ACT.Tanh, 0.5)
            rounds(body, high)(act)

        @block.vector
        def _(dve):
            dve.wait_ge(c_in, 16)
            PER = 2 + 2 + 1 + 2 * 4
            link = Chain(dve, ev["ch"])

            def wait(n, b):
                dve.wait_ge(ev[n], b + 1)

            def phi(dst, e, src, n):
                link(nc.vector.tensor_scalar(e, e, 1.0, None, ALU.min))
                nc.vector.scalar_tensor_tensor(out=dst, in0=src, scalar=0.0, in1=e, op0=ALU.max,
                                               op1=ALU.add).then_inc(ev[n], 1)

            def tail(b):
                for tt in range(2):
                    wait(f"hT{tt}", b)
                    nc.vector.tensor_tensor(oTl[:, tt], bank[4 + tt][:, :].rearrange("p (k c) -> p k c", k=KC),
                                            oTh[:, tt], ALU.subtract).then_inc(ev[f"lT{tt}"], 1)
                for tt in range(2):
                    wait(f"O{tt}", b)
                    xt = X[:, 2 * b + tt, :]
                    nc.vector.scalar_tensor_tensor(out=xt, in0=bank[4 + tt][:, :], scalar=tg[:, 1:2], in1=xt,
                                                   op0=ALU.mult, op1=ALU.add).then_inc(ev[f"X{tt}"], 1)

            def body(b, more):
                link.start(b * PER + 2)
                for tt in range(2):
                    wait(f"eK{tt}", b)
                    phi(kk[:, tt, :], ek[:, tt, :], bank[tt][:, :], f"pK{tt}")
                if more:
                    tail(b - 1)
                wait("SUM", b)
                nc.vector.tensor_tensor(kv[:, :, :], bank[0][:, :].rearrange("p (k c) -> p k c", k=KC),
                                        blocks[:, :].unsqueeze(1).broadcast_to([P, KC, P]), ALU.mult)
                link(nc.vector.tensor_copy(ksr[:, :], bank[1][:, 0:KC]))
                nc.vector.tensor_tensor(ks[:, :, :], ksr[:, :].unsqueeze(2).broadcast_to([P, KC, GPH]),
                                        heads[:, :].unsqueeze(1).broadcast_to([P, KC, GPH]), ALU.mult)\
                  .then_inc(ev["mSUM"], 1)
                for tt in range(2):
                    wait(f"eQ{tt}", b)
                    phi(qq[:, tt, :], eq[:, tt, :], bank[4 + tt][:, :], f"pQ{tt}")
                for tt in range(2):
                    wait(f"G{tt}", b)
                    nc.vector.tensor_tensor(gt[:, tt, :], bank[6 + tt][:, :], bg[:, :], ALU.add)\
                      .then_inc(ev[f"lG{tt}"], 1)
                for tt in range(2):
                    wait(f"ATT{tt}", b)
                    link(nc.vector.tensor_scalar(den[:, tt, :], bank[6 + tt][:, 0:H1], 1e-6, None, ALU.add))
                    link(nc.vector.reciprocal(den[:, tt, :], den[:, tt, :]))
                    o3 = og[:, tt, :].rearrange("p (h c) -> p h c", h=H1)
                    link(nc.vector.tensor_tensor(o3, bank[2 + tt][:, :].rearrange("p (h c) -> p h c", h=H1),
                                                 den[:, tt, :].unsqueeze(2).broadcast_to([P, H1, HD1]), ALU.mult))
                    wait(f"tG{tt}", b)
                    link(nc.vector.tensor_scalar(gt[:, tt, :], gt[:, tt, :], 0.5, 0.5, ALU.mult, ALU.add))
                    nc.vector.tensor_tensor(og[:, tt, :], og[:, tt, :], gt[:, tt, :], ALU.mult)\
                      .then_inc(ev[f"OG{tt}"], 1)
                assert link.n == PER, link.n
            rounds(body, tail)(dve)
    st.close()


def phase_d(nc, a, env):
    sem, bank, bank16, X, XTh, XTl, ident, ident16, tg = (env[k] for k in (
        "sem", "bank", "bank16", "X", "XTh", "XTl", "ident", "ident16", "tg"))
    st = ExitStack()

    def sb(name, shape, dt=F32):
        return env["sb"](name, shape, dt, stack=st)

    NU = 3
    rows = nc.dram_tensor("rows", (TILES * P, D), F32, kind="Internal").ap()
    table = nc.dram_tensor("table", (NT * P, 1), I32, kind="Internal").ap()
    made = nc.dram_tensor("made", (NT * P, D), F32, kind="Internal").ap()
    slot = sb("d_slot", [P, TOP, TILES], I32)
    share = sb("d_share", [P, TOP, TILES])
    owner = sb("d_owner", [1, NT], I32)
    token = sb("d_token", [P, TILES], I32)
    who = sb("d_who", [P, NT], I32)
    sst = ExitStack()

    def sb(name, shape, dt=F32):
        return env["sb"](name, shape, dt, stack=sst)

    wh = sb("d_wh", [P, 2, NU, KC, CH], F16)
    wl = sb("d_wl", [P, 2, NU, KC, CH], F16)
    stage = sb("d_stage", [P, NU, 4, P])
    env["front"]("ln", XTh, XTl, weights=[
        (w, wh[:, 0, k], wl[:, 0, k]) for k, w in enumerate(
            (a["L1_ffn_sw1"][0:CH, :], a["L1_ffn_sw2"][0:CH, :], a["L1_ffn_sw3"][:, 0:CH]))], keep=rows)

    rst = ExitStack()

    def rb(name, shape, dt=F32):
        return env["sb"](name, shape, dt, stack=rst)

    rw = rb("r_w", [E, D])
    rwT = rb("r_wT", [P, KC, 2 * E], F16)
    ebias = rb("r_bias", [P, E])
    sc = rb("r_sc", [P, TILES, E])
    sel = rb("r_sel", [P, TILES, E])
    rank = rb("r_rank", [P, TILES, E])
    cmp_ = rb("r_cmp", [P, TILES, E])
    tot = rb("r_tot", [P, TILES])
    inv = rb("r_inv", [P, TILES])
    chosen = rb("r_chosen", [P, TILES, E], F16)
    ones = rb("r_ones", [P, P], F16)
    below = rb("r_below", [P, P], F16)
    mask = rb("r_mask", [P, TILES, E])
    before = rb("r_before", [P, TILES, E])
    count = rb("r_count", [P, E])
    steps = rb("r_steps", [P, max(TILES, NT)], I32)
    stepf = rb("r_stepf", [P, max(TILES, NT)])
    over = rb("r_over", [P, E, TILES])
    tiles = rb("r_tiles", [P, E])
    start = rb("r_start", [P, E + 1])
    place = rb("r_place", [P, TILES, E])
    slotf = rb("r_slotf", [P, TOP, TILES])
    past = rb("r_past", [1, NT, E])
    ownerf = rb("r_ownerf", [1, NT])
    none = rb("r_none", [P, NT], I32)
    r_in, r_wt, r_whi, r_wlo, r_lg, r_add, r_sig, r_ch, r_cst, r_pch, r_msk, r_cnt, r_zero = (
        sem("r_" + n) for n in ("in", "wt", "whi", "wlo", "lg", "add", "sig", "ch", "const", "pchain", "chosen",
                                "counts", "zero"))
    with nc.Block() as block:
        @block.sync
        def _(sp):
            sp.dma_start(rw[:, :], a["L1_ffn_router_w"]).then_inc(r_in, 16)
            sp.dma_start(ebias[:, :], env["row"](a["L1_ffn_expert_bias"])).then_inc(r_in, 16)
            sp.wait_ge(r_pch, 1)
            sp.dma_start(table.rearrange("(p j) o -> p (j o)", p=P), none[:, :]).then_inc(r_zero, 16)
            sp.wait_ge(r_zero, 16)

        @block.gpsimd
        def _(pool):
            nc.gpsimd.memset(none[:, :], 0).then_inc(r_pch, 1)
            nc.gpsimd.iota(token[:, :], pattern=[[P, TILES]], base=0, channel_multiplier=1)
            nc.gpsimd.iota(steps[:, :], pattern=[[1, max(TILES, NT)]], base=0, channel_multiplier=0).then_inc(r_cst, 1)
            nc.gpsimd.memset(ones[:, :], 1.0).then_inc(r_pch, 1)
            pool.wait_ge(r_pch, 2)
            nc.gpsimd.affine_select(out=below[:, :], in_=ones[:, :], compare_op=ALU.is_ge, fill=0.0, base=-1,
                                    pattern=[[1, P]], channel_multiplier=-1).then_inc(r_cst, 1)

        @block.tensor
        def _(pe):
            pe.wait_ge(r_in, 32)
            for k in range(KC):
                last = nc.tensor.transpose(bank[0][:, k * E:(k + 1) * E], rw[:, k * P:(k + 1) * P], ident[0:E, 0:E])
            last.then_inc(r_wt, 1)
            pe.wait_ge(r_wlo, 1)
            with pe.Fori(0, TILES) as i:
                for k in range(KC):
                    cols = bass.ts(i, P)
                    nc.tensor.matmul(bank[1][:, bass.ts(i, 2 * E)], XTh[:, k, cols], rwT[:, k, :],
                                     start=(k == 0), stop=False)
                    nc.tensor.matmul(bank[1][:, bass.ds(i * 2 * E, E)], XTl[:, k, cols], rwT[:, k, 0:E],
                                     start=False, stop=(k == KC - 1)).then_inc(r_lg, 1)
            pe.wait_ge(r_msk, 1)
            pe.wait_ge(r_cst, 2)
            taken = chosen[:, :, :].rearrange("p t e -> p (t e)")
            nc.tensor.matmul(bank[2][:, 0:TILES * E], below[:, :], taken, start=True, stop=True)
            nc.tensor.matmul(bank[3][:, 0:TILES * E], ones[:, :], taken, start=True, stop=True).then_inc(r_cnt, 1)

        @block.scalar
        def _(act):
            act.wait_ge(r_wt, 1)
            nc.scalar.activation(rwT[:, :, 0:E], bank[0][:, 0:KC * E].rearrange("p (k e) -> p k e", k=KC),
                                 ACT.Copy).then_inc(r_whi, 1)
            act.wait_ge(r_add, 1)
            nc.scalar.activation(sc[:, :, :], rank[:, :, :], ACT.Sigmoid).then_inc(r_sig, 1)

        @block.vector
        def _(dve):
            link = Chain(dve, r_ch)
            dve.wait_ge(r_whi, 1)
            nc.vector.tensor_tensor(rwT[:, :, E:2 * E], bank[0][:, 0:KC * E].rearrange("p (k e) -> p k e", k=KC),
                                    rwT[:, :, 0:E], ALU.subtract).then_inc(r_wlo, 1)
            dve.wait_ge(r_lg, TILES * KC)
            lg = bank[1][:, 0:TILES * 2 * E].rearrange("p (t e) -> p t e", t=TILES)
            link(nc.vector.tensor_copy(cmp_[:, :, :], lg[:, :, E:2 * E]))
            nc.vector.tensor_tensor(rank[:, :, :], lg[:, :, 0:E], cmp_[:, :, :], ALU.add).then_inc(r_add, 1)
            dve.wait_ge(r_sig, 1)
            link(nc.vector.tensor_tensor(sel[:, :, :], sc[:, :, :],
                                         ebias[:, :].unsqueeze(1).broadcast_to([P, TILES, E]), ALU.add))
            link(nc.vector.memset(rank[:, :, :], 0.0))
            for d in range(1, E):
                link(nc.vector.tensor_tensor(cmp_[:, :, 0:E - d], sel[:, :, 0:E - d], sel[:, :, d:E], ALU.is_ge))
                link(nc.vector.tensor_tensor(rank[:, :, d:E], rank[:, :, d:E], cmp_[:, :, 0:E - d], ALU.add))
                link(nc.vector.tensor_tensor(cmp_[:, :, 0:E - d], sel[:, :, d:E], sel[:, :, 0:E - d], ALU.is_gt))
                link(nc.vector.tensor_tensor(rank[:, :, 0:E - d], rank[:, :, 0:E - d], cmp_[:, :, 0:E - d], ALU.add))
            nc.vector.tensor_scalar(chosen[:, :, :], rank[:, :, :], TOP - 0.5, None, ALU.is_lt).then_inc(r_msk, 1)
            link(nc.vector.scalar_tensor_tensor(out=sel[:, :, :], in0=rank[:, :, :], scalar=TOP - 0.5,
                                                in1=sc[:, :, :], op0=ALU.is_lt, op1=ALU.mult))
            link(nc.vector.reduce_sum(tot[:, :], sel[:, :, :], AX_X))
            link(nc.vector.tensor_scalar(tot[:, :], tot[:, :], 1e-9, None, ALU.add))
            link(nc.vector.reciprocal(inv[:, :], tot[:, :]))
            link(nc.vector.tensor_tensor(sel[:, :, :], sel[:, :, :],
                                         inv[:, :].unsqueeze(2).broadcast_to([P, TILES, E]), ALU.mult))
            link(nc.vector.tensor_scalar(sel[:, :, :], sel[:, :, :], tg[:, 3:4], None, ALU.mult))
            link(nc.vector.memset(before[:, 0, :], 0.0))
            dve.wait_ge(r_cnt, 1)
            here = bank[3][:, 0:TILES * E].rearrange("p (t e) -> p t e", t=TILES)
            for t in range(1, TILES):
                link(nc.vector.tensor_tensor(before[:, t, :], before[:, t - 1, :], here[:, t - 1, :], ALU.add))
            link(nc.vector.tensor_tensor(count[:, :], before[:, TILES - 1, :], here[:, TILES - 1, :], ALU.add))
            dve.wait_ge(r_cst, 1)
            link(nc.vector.tensor_copy(stepf[:, :], steps[:, :]))
            link(nc.vector.tensor_scalar(count[:, :], count[:, :], 1.0 / P, None, ALU.mult))
            link(nc.vector.tensor_tensor(over[:, :, :], count[:, :].unsqueeze(2).broadcast_to([P, E, TILES]),
                                         stepf[:, 0:TILES].unsqueeze(1).broadcast_to([P, E, TILES]), ALU.is_gt))
            link(nc.vector.reduce_sum(tiles[:, :], over[:, :, :], AX_X))
            link(nc.vector.memset(start[:, 0:1], 0.0))
            for e in range(E):
                link(nc.vector.tensor_tensor(start[:, e + 1:e + 2], start[:, e:e + 1], tiles[:, e:e + 1], ALU.add))
            link(nc.vector.tensor_scalar(count[:, :], start[:, 0:E], float(P), None, ALU.mult))
            link(nc.vector.tensor_tensor(place[:, :, :], before[:, :, :],
                                         bank[2][:, 0:TILES * E].rearrange("p (t e) -> p t e", t=TILES), ALU.add))
            link(nc.vector.tensor_tensor(place[:, :, :], place[:, :, :],
                                         count[:, :].unsqueeze(1).broadcast_to([P, TILES, E]), ALU.add))
            for c in range(TOP):
                link(nc.vector.tensor_scalar(mask[:, :, :], rank[:, :, :], float(c), None, ALU.is_equal))
                link(nc.vector.tensor_tensor(cmp_[:, :, :], mask[:, :, :], place[:, :, :], ALU.mult))
                link(nc.vector.reduce_sum(slotf[:, c, :], cmp_[:, :, :], AX_X))
                link(nc.vector.tensor_tensor(cmp_[:, :, :], mask[:, :, :], sel[:, :, :], ALU.mult))
                link(nc.vector.reduce_sum(share[:, c, :], cmp_[:, :, :], AX_X))
            link(nc.vector.tensor_copy(slot[:, :, :], slotf[:, :, :]))
            link(nc.vector.tensor_tensor(past[:, :, :], stepf[0:1, 0:NT].unsqueeze(2).broadcast_to([1, NT, E]),
                                         start[0:1, 1:E + 1].unsqueeze(1).broadcast_to([1, NT, E]), ALU.is_ge))
            link(nc.vector.reduce_sum(ownerf[:, :], past[:, :, :], AX_X))
            link(nc.vector.tensor_scalar(ownerf[:, :], ownerf[:, :], E - 1.0, None, ALU.min))
            link(nc.vector.tensor_copy(owner[:, :], ownerf[:, :]))
    rst.close()

    silu = sb("d_silu", [P, BLK])
    hid = sb("d_hid", [P, 2, BLK])
    hh = sb("d_hh", [P, 2, BLK], F16)
    hl = sb("d_hl", [P, 2, BLK], F16)
    d_g, d_u, d_s, d_hm, d_hi, d_lo, d_dn, d_accf, d_sc, d_who = (sem("d_" + n) for n in (
        "gate", "up", "silu", "mul", "hi", "lo", "down", "acc_free", "scattered", "who"))
    p_st = [sem(f"p_stage{k}") for k in range(NU)]
    p_tr, p_hi, p_lo = sem("p_tr"), sem("p_hi"), sem("p_lo")
    PRE = NU * KC
    GATE, UP, TR = 4, 5, 7
    NS = FS // CH
    BPC = TILES * P // BLK
    TPB = BLK // P

    def source(c, k, t):
        if k < 2:
            w = a[("L1_ffn_sw1", "L1_ffn_sw2")[k]]
            return w[bass.ts(c, CH), t * P:(t + 1) * P].rearrange("(r p) c -> p r c", p=P)
        return a["L1_ffn_sw3"][:, bass.ds(c * CH + t * P, P)].rearrange("(r p) c -> p r c", p=P)

    def plan(eng, chunk):
        with eng.Fori(0, NS // 2 - 1) as cp:
            chunk(2 * cp, 0, 2 * cp + 1)
            chunk(2 * cp + 1, 1, 2 * cp + 2)
        chunk(NS - 2, 0, NS - 1)
        chunk(NS - 1, 1, None)

    with nc.Block() as block:
        @block.sync
        def _(sp):
            def load(c, q):
                for t in range(BPC):
                    for k in range(NU):
                        sp.wait_ge(p_tr, q + NU * t + k + 1)
                        sp.dma_start(stage[:, k, :, :], source(c, k, t)).then_inc(p_st[k], 16)
            for c in range(1, NS):
                load(c, PRE * c)

        @block.gpsimd
        def _(pool):
            for t in range(TILES):
                for c in range(TOP):
                    pool.indirect_dma_start(table, bass.IndirectOffsetOnAxis(ap=slot[:, c, t:t + 1], axis=0),
                                            token[:, t:t + 1], None).then_inc(d_sc, 16)
            pool.wait_ge(d_sc, 16 * TOP * TILES)
            pool.dma_start(who[:, :], table.rearrange("(j p) o -> p (j o)", p=P),
                           allow_slow_non_contiguous=True).then_inc(d_who, 16)
            pool.wait_ge(d_who, 16)

        @block.tensor
        def _(pe):
            pe.sem_inc(p_tr, NU + PRE)
            pe.sem_inc(d_dn, 2)

            def transposes(k, q, dma):
                pe.wait_ge(p_st[k], dma)
                pe.wait_ge(p_lo, q + 1)
                for r in range(4):
                    last = nc.tensor.transpose(bank[TR][:, r * P:(r + 1) * P], stage[:, k, r, :], ident[:, :])
                last.then_inc(p_tr, 1)

            def down(j, s, n, par):
                pe.wait_ge(d_lo, s + 1)
                if j == 0:
                    pe.wait_ge(d_accf, n + 1)
                for tt in range(TPB):
                    cols = slice(tt * P, (tt + 1) * P)
                    last = three_(bank[tt][:, :], hh[:, j % 2, cols], hl[:, j % 2, cols],
                                  wh[:, par, 2, j, :], wl[:, par, 2, j, :], j == 0, j == KC - 1)
                last.then_inc(d_dn, 1)

            three_ = env["three"]

            def chunk(c, par, nxt):
                with pe.Fori(0, BPC) as t:
                    n = c * BPC + t
                    tok = bass.ts(t, BLK)
                    for j in range(KC):
                        s = n * KC + j
                        pe.wait_ge(d_s, s + 1)
                        cols = slice(j * P, (j + 1) * P)
                        for k in range(KC):
                            last = three_(bank[GATE][:, :], wh[:, par, 0, k, cols], wl[:, par, 0, k, cols],
                                          XTh[:, k, tok], XTl[:, k, tok], k == 0, k == KC - 1)
                        last.then_inc(d_g, 1)
                        pe.wait_ge(d_hm, s + 1)
                        for k in range(KC):
                            last = three_(bank[UP][:, :], wh[:, par, 1, k, cols], wl[:, par, 1, k, cols],
                                          XTh[:, k, tok], XTl[:, k, tok], k == 0, k == KC - 1)
                        last.then_inc(d_u, 1)
                        if nxt is not None and j < NU:
                            transposes(j, PRE + n * NU + j, dma_value(nxt, j, t))
                        if j:
                            down(j - 1, s - 1, n, par)
                    down(KC - 1, n * KC + KC - 1, n, par)

            def dma_value(c, k, t):
                return 16 * (BPC * (c - 1) + t + 1)

            plan(pe, chunk)

        @block.scalar
        def _(act):
            act.sem_inc(d_s, 1)
            act.sem_inc(p_hi, PRE)

            def high(par, k, t, q):
                act.wait_ge(p_tr, q + 1 + NU)
                nc.scalar.activation(wh[:, par, k, t, :], bank[TR][:, :], ACT.Copy).then_inc(p_hi, 1)

            def chunk(c, par, nxt):
                with act.Fori(0, BPC) as t:
                    n = c * BPC + t
                    for j in range(KC):
                        s = n * KC + j
                        act.wait_ge(d_g, s + 1)
                        act.wait_ge(d_hm, s + 1)
                        nc.scalar.activation(silu[:, :], bank[GATE][:, :], ACT.Silu).then_inc(d_s, 1)
                        if nxt is not None and j < NU:
                            high(1 - par, j, t, PRE + n * NU + j)
                        act.wait_ge(d_hm, s + 2)
                        act.wait_ge(d_dn, s + 1)
                        nc.scalar.activation(hh[:, j % 2, :], hid[:, j % 2, :], ACT.Copy).then_inc(d_hi, 1)

            plan(act, chunk)

        @block.vector
        def _(dve):
            dve.sem_inc(d_hm, 1)
            dve.sem_inc(d_accf, 1)
            dve.sem_inc(p_lo, 1 + PRE)

            def low(par, k, t, q):
                dve.wait_ge(p_hi, q + 1)
                nc.vector.tensor_tensor(wl[:, par, k, t, :], bank[TR][:, :], wh[:, par, k, t, :],
                                        ALU.subtract).then_inc(p_lo, 1)

            def chunk(c, par, nxt):
                with dve.Fori(0, BPC) as t:
                    n = c * BPC + t
                    for j in range(KC):
                        s = n * KC + j
                        dve.wait_ge(d_u, s + 1)
                        dve.wait_ge(d_s, s + 2)
                        nc.vector.tensor_tensor(hid[:, j % 2, :], silu[:, :], bank[UP][:, :],
                                                ALU.mult).then_inc(d_hm, 1)
                        if nxt is not None and j < NU:
                            low(1 - par, j, t, PRE + n * NU + j)
                        dve.wait_ge(d_hi, s + 1)
                        nc.vector.tensor_tensor(hl[:, j % 2, :], hid[:, j % 2, :], hh[:, j % 2, :],
                                                ALU.subtract).then_inc(d_lo, 1)
                    dve.wait_ge(d_dn, (n + 1) * KC + 2)
                    for tt in range(TPB):
                        xt = X[:, t * TPB + tt, :]
                        last = nc.vector.scalar_tensor_tensor(out=xt, in0=bank[tt][:, :], scalar=tg[:, 3:4], in1=xt,
                                                              op0=ALU.mult, op1=ALU.add)
                    last.then_inc(d_accf, 1)

            plan(dve, chunk)
    sst.close()
    routed(nc, a, env, st, rows, made, slot, share, owner, who)
    st.close()


def routed(nc, a, env, st, rows, made, slot, share, owner, who):
    sem, bank, X, ident = (env[k] for k in ("sem", "bank", "X", "ident"))

    def sb(name, shape, dt=F32):
        return env["sb"](name, shape, dt, stack=st)

    HC = FR // P
    w12h = sb("e_w12h", [P, E, KC, 2 * FR], F16)
    w12l = sb("e_w12l", [P, E, KC, 2 * FR], F16)
    w3h = sb("e_w3h", [P, E, HC, D], F16)
    w3l = sb("e_w3l", [P, E, HC, D], F16)

    wst = ExitStack()
    st12 = env["sb"]("e_st12", [P, 2, 4, D], stack=wst)
    st3 = env["sb"]("e_st3", [P, 2, 4, FR], stack=wst)
    v_in = [sem("v_in0"), sem("v_in1")]
    v_tr, v_hi, v_lo = (sem("v_" + n) for n in ("tr", "hi", "lo"))
    NG = KC + HC

    def target(w12, w3, e, g):
        w, k = (w12, g) if g < KC else (w3, g - KC)
        return w[:, bass.ds(e, 1), k, :]

    def group(g):
        return bank[g][:, :].rearrange("p (o c) -> p o c", o=1)

    with nc.Block() as block:
        @block.sync
        def _(sp):
            for e in range(E):
                if e >= 2:
                    sp.wait_ge(v_tr, NG * (e - 1))
                sp.dma_start(st12[:, e % 2], a["L1_ffn_w12"][e].rearrange("(r p) c -> p r c", p=P))\
                  .then_inc(v_in[e % 2], 16)
                sp.dma_start(st3[:, e % 2], a["L1_ffn_w3"][e].rearrange("(r p) c -> p r c", p=P))\
                  .then_inc(v_in[e % 2], 16)

        @block.tensor
        def _(pe):
            with pe.Fori(0, E // 2) as i:
                for p in range(2):
                    pe.wait_ge(v_in[p], 32 * i + 32)
                    for g in range(NG):
                        pe.wait_ge(v_lo, NG * (2 * i + p) + g + 1)
                        for r in range(4):
                            src = st12[:, p, r, g * P:(g + 1) * P] if g < KC else \
                                st3[:, p, r, (g - KC) * P:(g - KC + 1) * P]
                            last = nc.tensor.transpose(bank[g][:, r * P:(r + 1) * P], src, ident[:, :])
                        last.then_inc(v_tr, 1)

        @block.scalar
        def _(act):
            with act.Fori(0, E) as e:
                for g in range(NG):
                    act.wait_ge(v_tr, NG * e + g + 1)
                    nc.scalar.activation(target(w12h, w3h, e, g), group(g), ACT.Copy).then_inc(v_hi, 1)

        @block.vector
        def _(dve):
            dve.sem_inc(v_lo, NG)
            with dve.Fori(0, E) as e:
                for g in range(NG):
                    dve.wait_ge(v_hi, NG * e + g + 1)
                    nc.vector.tensor_tensor(target(w12l, w3l, e, g), group(g), target(w12h, w3h, e, g),
                                            ALU.subtract).then_inc(v_lo, 1)
    wst.close()

    xg = sb("e_x", [P, 2, D])
    xh = sb("e_xh", [P, 2, KC, P], F16)
    xl = sb("e_xl", [P, 2, KC, P], F16)
    gate = sb("e_gate", [P, 2, FR])
    hid = sb("e_hid", [P, 2, FR])
    hh = sb("e_hh", [P, 2, HC, P], F16)
    hl = sb("e_hl", [P, 2, HC, P], F16)
    y = sb("e_y", [P, 2, D])
    g_in, g_out = [sem("g_in0"), sem("g_in1")], [sem("g_out0"), sem("g_out1")]
    names = ("x", "xh", "xl", "u", "s", "m", "v", "hh", "hl", "w", "y")
    ev = {n: sem("g_" + n) for n in names}
    TX, UP, TH, DN = 0, 2, 4, 6

    def rounds(eng, step):
        step(0, 0, False, True)
        with eng.Fori(0, (NT - 3) // 2) as i:
            step(2 * i + 1, 1, True, True)
            step(2 * i + 2, 0, True, True)
        step(NT - 2, 1, True, True)
        step(NT - 1, 0, True, False)
    assert NT % 2 == 1

    with nc.Block() as block:
        @block.gpsimd
        def _(pool):
            for j in range(NT):
                if j >= 2:
                    pool.wait_ge(ev["x"], j + 1)
                pool.indirect_dma_start(xg[:, j % 2, :], None, rows,
                                        bass.IndirectOffsetOnAxis(ap=who[:, j:j + 1], axis=0)).then_inc(g_in[j % 2], 16)

        @block.sync
        def _(sp):
            for j in range(NT):
                sp.wait_ge(ev["y"], j + 3)
                sp.dma_start(made[j * P:(j + 1) * P, :], y[:, j % 2, :]).then_inc(g_out[j % 2], 16)
            for p in range(2):
                sp.wait_ge(g_out[p], 16 * len(range(p, NT, 2)) + 16)

        @block.tensor
        def _(pe):
            for n in ("x", "u", "v", "w"):
                pe.sem_inc(ev[n], 2)

            def made_by(n, j):
                pe.wait_ge(ev[n], j + 3)

            def read_by(n, j):
                pe.wait_ge(ev[n], j + 1)

            def expert(j):
                return pe.value_load(owner[0:1, bass.ds(j, 1)], min_val=0, max_val=E - 1)

            def weights(w, e, k):
                return w[:, bass.ds(e, 1), k, :].rearrange("p o c -> p (o c)")

            def turn(j, p):
                pe.wait_ge(g_in[p], 8 * (j - p) + 16)
                read_by("xl", j)
                for k in range(KC):
                    last = nc.tensor.transpose(bank[TX + p][:, k * P:(k + 1) * P], xg[:, p, k * P:(k + 1) * P], ident[:, :])
                last.then_inc(ev["x"], 1)

            def up(j, p):
                e = expert(j)
                made_by("xl", j)
                read_by("m", j)
                for k in range(KC):
                    last = env["three"](bank[UP + p][:, :], xh[:, p, k, :], xl[:, p, k, :], weights(w12h, e, k),
                                        weights(w12l, e, k), k == 0, k == KC - 1)
                last.then_inc(ev["u"], 1)

            def turn_hidden(j, p):
                made_by("m", j)
                read_by("hl", j)
                for k in range(HC):
                    last = nc.tensor.transpose(bank[TH + p][:, k * P:(k + 1) * P], hid[:, p, k * P:(k + 1) * P], ident[:, :])
                last.then_inc(ev["v"], 1)

            def down(j, p):
                e = expert(j)
                made_by("hl", j)
                read_by("y", j)
                for k in range(HC):
                    last = env["three"](bank[DN + p][:, :], hh[:, p, k, :], hl[:, p, k, :], weights(w3h, e, k),
                                        weights(w3l, e, k), k == 0, k == HC - 1)
                last.then_inc(ev["w"], 1)

            def step(j, p, prior, more):
                up(j, p)
                if more:
                    turn(j + 1, 1 - p)
                if prior:
                    down(j - 1, 1 - p)
                turn_hidden(j, p)
            turn(0, 0)
            rounds(pe, step)
            down(NT - 1, (NT - 1) % 2)

        @block.scalar
        def _(act):
            for p in range(2):
                act.sem_inc(g_out[p], 16)
            act.sem_inc(ev["y"], 2)

            def take(n, j, dst, src, then, free=None, func=ACT.Copy):
                act.wait_ge(ev[n], j + 3)
                if free:
                    act.wait_ge(ev[free], j + 1)
                nc.scalar.activation(dst, src, func).then_inc(ev[then], 1)

            def split_x(j, p):
                take("x", j, xh[:, p], bank[TX + p][:, :].rearrange("p (k c) -> p k c", k=KC), "xh", "u")

            def result(j, p):
                act.wait_ge(g_out[p], 8 * (j - p) + 16)
                take("w", j, y[:, p, :], bank[DN + p][:, :], "y")

            def step(j, p, prior, more):
                take("u", j, gate[:, p, :], bank[UP + p][:, 0:FR], "s", "m", ACT.Silu)
                if more:
                    split_x(j + 1, 1 - p)
                if prior:
                    result(j - 1, 1 - p)
                take("v", j, hh[:, p], bank[TH + p][:, 0:FR].rearrange("p (k c) -> p k c", k=HC), "hh", "w")
            split_x(0, 0)
            rounds(act, step)
            result(NT - 1, (NT - 1) % 2)

        @block.vector
        def _(dve):
            for n in ("xl", "m", "hl"):
                dve.sem_inc(ev[n], 2)

            def low(n, j, dst, src, hi, then, free=None):
                dve.wait_ge(ev[n], j + 1)
                nc.vector.tensor_tensor(dst, src, hi, ALU.subtract).then_inc(ev[then], 1)

            def split_x(j, p):
                low("xh", j, xl[:, p], bank[TX + p][:, :].rearrange("p (k c) -> p k c", k=KC), xh[:, p], "xl")

            def step(j, p, prior, more):
                dve.wait_ge(ev["s"], j + 1)
                dve.wait_ge(ev["v"], j + 1)
                nc.vector.tensor_tensor(hid[:, p, :], gate[:, p, :], bank[UP + p][:, FR:2 * FR],
                                        ALU.mult).then_inc(ev["m"], 1)
                if more:
                    split_x(j + 1, 1 - p)
                low("hh", j, hl[:, p], bank[TH + p][:, 0:FR].rearrange("p (k c) -> p k c", k=HC), hh[:, p], "hl")
            split_x(0, 0)
            rounds(dve, step)

    NB = 8
    back = sb("e_back", [P, NB, D])
    c_in = [sem(f"c_in{n}") for n in range(NB)]
    c_x = sem("c_x")
    with nc.Block() as block:
        @block.gpsimd
        def _(pool):
            for n in range(TOP * TILES):
                if n >= NB:
                    pool.wait_ge(c_x, n - NB + 1)
                pool.indirect_dma_start(back[:, n % NB, :], None, made,
                                        bass.IndirectOffsetOnAxis(ap=slot[:, n % TOP, n // TOP:n // TOP + 1], axis=0))\
                    .then_inc(c_in[n % NB], 16)

        @block.vector
        def _(dve):
            with dve.Fori(0, TOP * TILES // NB) as i:
                for n in range(NB):
                    t = (NB // TOP) * i + n // TOP
                    dve.wait_ge(c_in[n], 16 * i + 16)
                    nc.vector.scalar_tensor_tensor(out=X[:, t, :], in0=back[:, n, :],
                                                   scalar=share[:, n % TOP, bass.ds(t, 1)],
                                                   in1=X[:, t, :], op0=ALU.mult, op1=ALU.add).then_inc(c_x, 1)
                    dve.wait_ge(c_x, NB * i + n + 1)


_INS = ['x', 'ctx_2048', 'mask_SxS2_bc0', 'mask_BxS2_bk0', 'g_xattn', 'g_ffn', 'L0_xattn_Wq', 'L0_xattn_bq',
        'L0_xattn_Wk', 'L0_xattn_bk', 'L0_xattn_Wv', 'L0_xattn_bv', 'L0_xattn_Wo', 'L0_xattn_bo', 'L0_ffn_w_fc',
        'L0_ffn_w_proj', 'L1_xattn_Wq', 'L1_xattn_Wg', 'L1_xattn_bg', 'L1_xattn_Wkv', 'L1_xattn_Wo', 'L1_ffn_w12',
        'L1_ffn_w3', 'L1_ffn_router_w', 'L1_ffn_expert_bias', 'L1_ffn_sw1', 'L1_ffn_sw2', 'L1_ffn_sw3']
PHASES = "ABCD"


def kernel(**inputs):
    import numpy as _np
    import concourse.bacc as _bacc
    from concourse import mybir as _mybir
    from concourse.bass_utils import run_bass_kernel_spmd as _run

    nc = _bacc.Bacc("TRN2", target_bir_lowering=False, num_devices=1)
    arrays, args = {}, {}
    for name in _INS:
        v = _np.ascontiguousarray(inputs[name])
        arrays[f"in_{name}"] = v
        args[name] = nc.dram_tensor(f"in_{name}", v.shape, _mybir.dt.from_np(v.dtype), kind="ExternalInput").ap()
    out = nc.dram_tensor("out_x", (B, S, D), F32, kind="ExternalOutput").ap()
    flamingo(nc, args, out, PHASES)
    r = _run(nc, [arrays], core_ids=[0])
    return r.results[0]["out_x"]
```
